# Optimizing a Trainium2 kernel written in Bass

```python
import numpy as np
import jax
import jax.numpy as jnp

def _softmax(x, axis=-1):
    return jax.nn.softmax(x, axis=axis)

def _gelu(x):
    return jax.nn.gelu(x, approximate=True)

def _silu(x):
    return jax.nn.silu(x)

def _sigmoid(x):
    return jax.nn.sigmoid(x)

def _layernorm(x, axis=-1, eps=1e-05):
    m = jnp.mean(x, axis=axis, keepdims=True)
    v = jnp.var(x, axis=axis, keepdims=True)
    return (x - m) / jnp.sqrt(v + eps)

def _scatter_add(tgt, idx, src, axis=0):
    return tgt.at[idx].add(src)

def _segment_sum(src, seg, n):
    return jax.ops.segment_sum(src, seg, n)
kernel_name = 'mk_gnn_preln_d4_gnn_r64_a1707c'

def setup_inputs(seed: int=0):
    np.random.seed(seed)
    _w = jnp.asarray

    def _rec_inputs():
        import jax
        import jax.numpy as jnp
        _gk = jax.random.key(seed)
        x = -0.0005121 + 1.001 * jax.random.normal(jax.random.fold_in(_gk, 1), (50000, 64), jnp.float32)
        src = jax.random.randint(jax.random.fold_in(_gk, 2), (25000,), 0, 50000, jnp.int32)
        dst = jnp.minimum((50000 * jax.random.uniform(jax.random.fold_in(_gk, 3), (25000,)) ** 2.0).astype(jnp.int32), 49999)
        _o = jnp.argsort(dst, stable=True)
        src = src[_o]
        dst = dst[_o]
        edge_attr_4 = jax.random.uniform(jax.random.fold_in(_gk, 12), (25000, 4), jnp.float32, 0.0, 1)
        edge_type_32 = jax.random.randint(jax.random.fold_in(_gk, 14), (25000,), 0, 32, jnp.int32)
        node_vec = jax.random.uniform(jax.random.fold_in(_gk, 15), (50000,), jnp.float32, 0.0, 31.9963)
        return (x, src, dst, edge_attr_4, edge_type_32, node_vec)
    x, src, dst, edge_attr_4, edge_type_32, node_vec = _rec_inputs()

    def _L0_gnn_setup():
        import jax, jax.numpy as jnp
        import numpy as np
        N_NODES = 50000
        N_EDGES = 12500
        N_RELS = 32
        D_IN = 64
        D_OUT = 64
        key = jax.random.key(seed)
        k_feat, k_w, k_src, k_dst, k_et = jax.random.split(key, 5)
        feat = jax.random.normal(k_feat, (N_NODES, D_IN), dtype=jnp.float32)
        weight = jax.random.normal(k_w, (N_RELS, D_IN, D_OUT), dtype=jnp.float32) * 0.05
        src = jax.random.randint(k_src, (N_EDGES,), 0, N_NODES, dtype=jnp.int32)
        dst = jax.random.randint(k_dst, (N_EDGES,), 0, N_NODES, dtype=jnp.int32)
        etypes = jax.random.randint(k_et, (N_EDGES,), 0, N_RELS, dtype=jnp.int32)
        E_per_rel = jnp.bincount(etypes, length=N_RELS)
        return {'feat': feat, 'weight': weight, 'src': src, 'dst': dst, 'etypes': etypes, 'E_per_rel': E_per_rel}
    _L0_gnn_all = _L0_gnn_setup()
    _L0_gnn_in = {k: v for k, v in _L0_gnn_all.items() if k in ('weight', 'E_per_rel')}
    del _L0_gnn_all

    def _L1_gnn_setup():
        import jax, jax.numpy as jnp
        import numpy as np
        N_NODES = 100000
        N_EDGES = 18750
        D_IN = 64
        D_OUT = 64
        BN_EPS = 1e-05
        key = jax.random.key(seed)
        k1, k2, k3, k4 = jax.random.split(key, 4)
        x = jax.random.normal(k1, (N_NODES, D_IN), dtype=jnp.float32)
        edge_index = jax.random.randint(k2, (2, N_EDGES), 0, N_NODES, dtype=jnp.int64)
        W = jax.random.normal(k3, (D_IN, D_OUT), dtype=jnp.float32) / np.sqrt(D_IN)
        gamma = jnp.ones((D_OUT,), dtype=jnp.float32)
        beta = jnp.zeros((D_OUT,), dtype=jnp.float32)
        return {'x': x, 'edge_index': edge_index, 'W': W, 'gamma': gamma, 'beta': beta}
    _L1_gnn_all = _L1_gnn_setup()
    _L1_gnn_in = {k: v for k, v in _L1_gnn_all.items() if k in ('W', 'gamma', 'beta')}
    del _L1_gnn_all

    def _L2_gnn_setup():
        import jax, jax.numpy as jnp
        import numpy as np
        N_NODES = 50000
        N_EDGES = 18750
        D_FEAT = 64
        EMBED = 64
        H = 1
        HEAD_DIM = EMBED // H

        def mish(x):
            return x * jnp.tanh(jax.nn.softplus(x))
        key = jax.random.key(seed)
        ks = jax.random.split(key, 12)
        nodes = jax.random.normal(ks[0], (N_NODES, D_FEAT), dtype=jnp.float32)
        senders = jax.random.randint(ks[1], (N_EDGES,), 0, N_NODES, dtype=jnp.int32)
        receivers = jax.random.randint(ks[2], (N_EDGES,), 0, N_NODES, dtype=jnp.int32)
        s = 0.05
        We_k = jax.random.normal(ks[3], (D_FEAT, H, HEAD_DIM), dtype=jnp.float32) * s
        We_b = jnp.zeros((H, HEAD_DIM), dtype=jnp.float32)
        Ws_k = jax.random.normal(ks[4], (HEAD_DIM, EMBED), dtype=jnp.float32) * s
        Ws_b = jnp.zeros((EMBED,), dtype=jnp.float32)
        Wr_k = jax.random.normal(ks[5], (D_FEAT, H, HEAD_DIM), dtype=jnp.float32) * s
        Wr_b = jnp.zeros((H, HEAD_DIM), dtype=jnp.float32)
        Wa_k = jax.random.normal(ks[6], (EMBED, 1), dtype=jnp.float32) * s
        Wa_b = jnp.zeros((1,), dtype=jnp.float32)
        return {'nodes': nodes, 'senders': senders, 'receivers': receivers, 'We_k': We_k, 'We_b': We_b, 'Ws_k': Ws_k, 'Ws_b': Ws_b, 'Wr_k': Wr_k, 'Wr_b': Wr_b, 'Wa_k': Wa_k, 'Wa_b': Wa_b}
    _L2_gnn_all = _L2_gnn_setup()
    _L2_gnn_in = {k: v for k, v in _L2_gnn_all.items() if k in ('We_k', 'We_b', 'Ws_k', 'Ws_b', 'Wr_k', 'Wr_b', 'Wa_k', 'Wa_b')}
    del _L2_gnn_all

    def _L3_gnn_setup():
        import jax, jax.numpy as jnp
        import numpy as np
        N = 50000
        E = 12500
        C = 64
        key = jax.random.key(seed)
        ks = jax.random.split(key, 16)
        s = 0.05
        x = jax.random.normal(ks[0], (N, C), jnp.float32)
        edge_attr = jax.random.uniform(ks[1], (E, 4), dtype=jnp.float32)
        edge_index = jax.random.randint(ks[2], (2, E), 0, N)
        deg_hist = jax.random.uniform(ks[3], (N,), dtype=jnp.float32) * 32.0
        W = jax.random.normal(ks[4], (C, C), jnp.float32) * s
        We = jax.random.normal(ks[5], (3, C), jnp.float32) * s
        be = jnp.zeros((C,), jnp.float32)
        Wpre = jax.random.normal(ks[6], (3 * C, C), jnp.float32) * s
        bpre = jnp.zeros((C,), jnp.float32)
        A_S = 4 * 3
        Wpost = jax.random.normal(ks[7], ((A_S + 1) * C, C), jnp.float32) * s
        bpost = jnp.zeros((C,), jnp.float32)
        Wih = jax.random.normal(ks[8], (C, 3 * C), jnp.float32) * s
        bih = jnp.zeros((3 * C,), jnp.float32)
        Whh = jax.random.normal(ks[9], (C, 3 * C), jnp.float32) * s
        bhh = jnp.zeros((3 * C,), jnp.float32)
        return dict(x=x, edge_attr=edge_attr, deg_hist=deg_hist, W=W, We=We, be=be, Wpre=Wpre, bpre=bpre, Wpost=Wpost, bpost=bpost, Wih=Wih, bih=bih, Whh=Whh, bhh=bhh, edge_index=edge_index)
    _L3_gnn_all = _L3_gnn_setup()
    _L3_gnn_in = {k: v for k, v in _L3_gnn_all.items() if k in ('W', 'We', 'be', 'Wpre', 'bpre', 'Wpost', 'bpost', 'Wih', 'bih', 'Whh', 'bhh')}
    del _L3_gnn_all
    return {'x': x, 'src': src, 'dst': dst, 'edge_attr_4': edge_attr_4, 'edge_type_32': edge_type_32, 'node_vec': node_vec, 'L0_gnn_weight': _L0_gnn_in['weight'], 'L0_gnn_E_per_rel': _L0_gnn_in['E_per_rel'], 'L1_gnn_W': _L1_gnn_in['W'], 'L1_gnn_gamma': _L1_gnn_in['gamma'], 'L1_gnn_beta': _L1_gnn_in['beta'], 'L2_gnn_We_k': _L2_gnn_in['We_k'], 'L2_gnn_We_b': _L2_gnn_in['We_b'], 'L2_gnn_Ws_k': _L2_gnn_in['Ws_k'], 'L2_gnn_Ws_b': _L2_gnn_in['Ws_b'], 'L2_gnn_Wr_k': _L2_gnn_in['Wr_k'], 'L2_gnn_Wr_b': _L2_gnn_in['Wr_b'], 'L2_gnn_Wa_k': _L2_gnn_in['Wa_k'], 'L2_gnn_Wa_b': _L2_gnn_in['Wa_b'], 'L3_gnn_W': _L3_gnn_in['W'], 'L3_gnn_We': _L3_gnn_in['We'], 'L3_gnn_be': _L3_gnn_in['be'], 'L3_gnn_Wpre': _L3_gnn_in['Wpre'], 'L3_gnn_bpre': _L3_gnn_in['bpre'], 'L3_gnn_Wpost': _L3_gnn_in['Wpost'], 'L3_gnn_bpost': _L3_gnn_in['bpost'], 'L3_gnn_Wih': _L3_gnn_in['Wih'], 'L3_gnn_bih': _L3_gnn_in['bih'], 'L3_gnn_Whh': _L3_gnn_in['Whh'], 'L3_gnn_bhh': _L3_gnn_in['bhh']}

def reference(x, src, dst, edge_attr_4, edge_type_32, node_vec, L0_gnn_weight, L0_gnn_E_per_rel, L1_gnn_W, L1_gnn_gamma, L1_gnn_beta, L2_gnn_We_k, L2_gnn_We_b, L2_gnn_Ws_k, L2_gnn_Ws_b, L2_gnn_Wr_k, L2_gnn_Wr_b, L2_gnn_Wa_k, L2_gnn_Wa_b, L3_gnn_W, L3_gnn_We, L3_gnn_be, L3_gnn_Wpre, L3_gnn_bpre, L3_gnn_Wpost, L3_gnn_bpost, L3_gnn_Wih, L3_gnn_bih, L3_gnn_Whh, L3_gnn_bhh):
    import jax
    import jax.numpy as jnp

    def _L0_gnn_ref(feat, weight, src, dst, etypes, E_per_rel):
        import jax, jax.numpy as jnp
        import numpy as np
        N_NODES = 50000
        N_EDGES = 12500
        N_RELS = 32
        D_IN = 64
        D_OUT = 64
        N = feat.shape[0]
        R, D_in, D_out = weight.shape
        gathered = feat[src]
        seg = dst.astype(jnp.int32) * R + etypes.astype(jnp.int32)
        per_node_rel = jax.ops.segment_sum(gathered, seg, num_segments=N * R)
        per_node_rel = per_node_rel.reshape(N, R, D_in)
        out = jnp.einsum('nri,rio->no', per_node_rel, weight)
        return out

    def _L1_gnn_ref(x, edge_index, W, gamma, beta):
        import jax, jax.numpy as jnp
        import numpy as np
        N_NODES = 100000
        N_EDGES = 18750
        D_IN = 64
        D_OUT = 64
        BN_EPS = 1e-05
        src, dst = (edge_index[0], edge_index[1])
        n = x.shape[0]
        agg = jax.ops.segment_sum(x[src], dst, num_segments=n)
        cnt = jax.ops.segment_sum(jnp.ones((src.shape[0],), x.dtype), dst, num_segments=n)
        mean_agg = agg / jnp.maximum(cnt, 1.0)[:, None]
        h = jax.nn.elu(mean_agg @ W)
        mu = jnp.mean(h, axis=0)
        var = jnp.var(h, axis=0)
        out = (h - mu) * jax.lax.rsqrt(var + BN_EPS) * gamma + beta
        return out

    def _L2_gnn_ref(nodes, senders, receivers, We_k, We_b, Ws_k, Ws_b, Wr_k, Wr_b, Wa_k, Wa_b):
        import jax, jax.numpy as jnp
        import numpy as np
        N_NODES = 50000
        N_EDGES = 18750
        D_FEAT = 64
        EMBED = 64
        H = 1
        HEAD_DIM = EMBED // H

        def mish(x):
            return x * jnp.tanh(jax.nn.softplus(x))
        n = nodes.shape[0]
        sent = nodes[senders]
        edges = jnp.einsum('ef,fhd->ehd', sent, We_k) + We_b
        recv = nodes[receivers]
        s_att = jnp.einsum('ehd,dm->ehm', edges, Ws_k) + Ws_b
        r_att = jnp.einsum('ef,fhd->ehd', recv, Wr_k) + Wr_b
        x = mish(s_att + r_att)
        logits = jnp.einsum('ehm,mo->eho', x, Wa_k) + Wa_b
        seg_max = jax.ops.segment_max(logits, receivers, num_segments=n)
        seg_max = jnp.where(jnp.isfinite(seg_max), seg_max, 0.0)
        unnorm = jnp.exp(logits - seg_max[receivers])
        denom = jax.ops.segment_sum(unnorm, receivers, num_segments=n)
        weights = unnorm / denom[receivers]
        msg = (weights * edges).reshape(edges.shape[0], H * HEAD_DIM)
        out_nodes = jax.ops.segment_sum(msg, receivers, num_segments=n)
        return out_nodes

    def _L3_gnn_ref(x, edge_attr, deg_hist, W, We, be, Wpre, bpre, Wpost, bpost, Wih, bih, Whh, bhh, edge_index):
        import jax, jax.numpy as jnp
        import numpy as np
        N = 50000
        E = 12500
        C = 64
        n_nodes = x.shape[0]
        m = x @ W
        src, dst = (edge_index[0], edge_index[1])
        ew = edge_attr[:, 3:4]
        ea = edge_attr[:, :3] @ We + be
        xi = ew * m[dst]
        xj = ew * m[src]
        ea = ew * ea
        h = jnp.concatenate([xi, xj, ea], axis=-1) @ Wpre + bpre
        ones = jnp.ones((h.shape[0],), h.dtype)
        cnt = jax.ops.segment_sum(ones, dst, num_segments=n_nodes)
        safe = jnp.maximum(cnt, 1.0)[:, None]
        s1 = jax.ops.segment_sum(h, dst, num_segments=n_nodes)
        s2 = jax.ops.segment_sum(h * h, dst, num_segments=n_nodes)
        mean = s1 / safe
        mean_sq = s2 / safe
        std = jnp.sqrt(jax.nn.relu(mean_sq - mean * mean) + 1e-05)
        has = (cnt > 0)[:, None]
        mn = jnp.where(has, jax.ops.segment_min(h, dst, num_segments=n_nodes), 0.0)
        mx = jnp.where(has, jax.ops.segment_max(h, dst, num_segments=n_nodes), 0.0)
        agg = jnp.concatenate([mean, mn, mx, std], axis=-1)
        deg = jnp.maximum(cnt, 1.0)[:, None]
        avg_log = jnp.mean(jnp.log(deg_hist + 1.0))
        logd = jnp.log(deg + 1.0)
        o1 = agg
        o2 = o1 * (logd / avg_log)
        o3 = o2 * (avg_log / logd)
        out = jnp.concatenate([o1, o2, o3], axis=-1)
        out = jnp.concatenate([m, out], axis=-1) @ Wpost + bpost
        gi = out @ Wih + bih
        gh = x @ Whh + bhh
        ir, iz, i_n = jnp.split(gi, 3, axis=-1)
        hr, hz, h_n = jnp.split(gh, 3, axis=-1)
        r = jax.nn.sigmoid(ir + hr)
        z = jax.nn.sigmoid(iz + hz)
        n = jnp.tanh(i_n + r * h_n)
        return (1.0 - z) * n + z * x
    edge_index = jnp.stack([src, dst])
    h = jnp.maximum(_layernorm(x, axis=-1), 0.0)
    x = x + _L0_gnn_ref(h, L0_gnn_weight, src, dst, edge_type_32, L0_gnn_E_per_rel)
    h = jnp.maximum(_layernorm(x, axis=-1), 0.0)
    x = x + _L1_gnn_ref(h, edge_index, L1_gnn_W, L1_gnn_gamma, L1_gnn_beta)
    h = jnp.maximum(_layernorm(x, axis=-1), 0.0)
    x = x + _L2_gnn_ref(h, src, dst, L2_gnn_We_k, L2_gnn_We_b, L2_gnn_Ws_k, L2_gnn_Ws_b, L2_gnn_Wr_k, L2_gnn_Wr_b, L2_gnn_Wa_k, L2_gnn_Wa_b)
    h = jnp.maximum(_layernorm(x, axis=-1), 0.0)
    x = x + _L3_gnn_ref(h, edge_attr_4, node_vec, L3_gnn_W, L3_gnn_We, L3_gnn_be, L3_gnn_Wpre, L3_gnn_bpre, L3_gnn_Wpost, L3_gnn_bpost, L3_gnn_Wih, L3_gnn_bih, L3_gnn_Whh, L3_gnn_bhh, edge_index)
    return x

_drawn_inputs = setup_inputs


def setup_inputs(seed=0):
    import zlib

    import numpy as np

    out = dict(_drawn_inputs(seed))
    spreads = {'L1_gnn_gamma': (1.0, 0.2),
     'L1_gnn_beta': (0.0, 0.1),
     'L2_gnn_We_b': (0.0, 0.1),
     'L2_gnn_Ws_b': (0.0, 2.0),
     'L2_gnn_Wr_b': (0.0, 2.0),
     'L3_gnn_be': (0.0, 0.8),
     'L3_gnn_bpre': (0.0, 0.8),
     'L3_gnn_bpost': (0.0, 0.609),
     'L3_gnn_bih': (0.0, 0.518),
     'L3_gnn_bhh': (0.0, 0.478)}
    factors = {'edge_attr_4': 8.0,
     'node_vec': 8.0,
     'L2_gnn_Ws_k': 8.0,
     'L2_gnn_Wr_k': 22.213,
     'L2_gnn_Wa_k': 8.0,
     'L3_gnn_W': 3.797,
     'L3_gnn_We': 8.0,
     'L3_gnn_Wpre': 8.0,
     'L3_gnn_Wpost': 3.448,
     'L3_gnn_Wih': 2.77}
    for name, (base, spread) in spreads.items():
        noise = np.random.default_rng([zlib.crc32(name.encode()), seed]).standard_normal(out[name].shape)
        drawn = base * np.exp(spread * noise) if base else spread * noise
        out[name] = jnp.asarray(drawn.astype(out[name].dtype))
    for name, factor in factors.items():
        out[name] = (out[name] * factor).astype(out[name].dtype)
    return out
```

```python
from contextlib import ExitStack

import concourse.bass as bass
from concourse import mybir

F32 = mybir.dt.float32
BF16 = mybir.dt.bfloat16
I32 = mybir.dt.int32
ALU = mybir.AluOpType
ACT = mybir.ActivationFunctionType
AX = mybir.AxisListType

P = 128
D = 64
EPS = 1e-5
LIMIT = 1e38
FAR = float(1 << 20)


def gnn_kernel(nc, x, src, dst, attr, etype, node_vec, w0, w1, gamma, beta,
               we_k, we_b, ws_k, ws_b, wr_k, wr_b, wa_k, wa_b,
               w3, w3e, b3e, wpre, bpre, wpost, bpost, wih, bih, whh, bhh, out, debug=None):
    N = x.shape[0]
    E = src.shape[0]
    PAIR = 8 * P
    HALF = PAIR // 2
    NPAIR = -(-E // PAIR)
    EP = NPAIR * PAIR
    RQ = EP // 256
    NREL = w0.shape[0]
    assert NPAIR % 2 == 1 and NREL == 32 and N % 1000 == 0 and RQ <= P
    UNITS = N // 1000
    ROUNDS = (NPAIR - 3) // 2

    with ExitStack() as ctx:
        def sb(name, shape, dt=F32):
            return ctx.enter_context(nc.sbuf_tensor(name, shape, dt))

        def dram(name, shape, dt=F32):
            return nc.dram_tensor(name, shape, dt).ap()

        sems = {}

        def sem(name):
            if name not in sems:
                sems[name] = nc.alloc_semaphore(name=name.replace(" ", "_"))
            return sems[name]

        def stage_over():
            nc.clear_and_free_semaphores(list(sems.values()))
            sems.clear()
            nc.all_engine_barrier()

        def rounds(eng, body):
            with eng.Fori(0, ROUNDS) as r:
                body(2 * r, r, 0)
                body(2 * r + 1, r, 1)
            for i in range(2 * ROUNDS, NPAIR):
                body(i, i // 2, i % 2)

        def exists(i):
            return not isinstance(i, int) or i < NPAIR

        src_d = dram("src_d", (EP,), I32)
        dst_d = dram("dst_d", (EP + 2,), I32)
        typ_d = dram("typ_d", (EP,), I32)
        att_d = dram("att_d", (EP, 4))
        same_prev_d = dram("same_prev_d", (EP,), BF16)
        same_next_d = dram("same_next_d", (EP,), BF16)
        thi_d = dram("thi_d", (EP,), BF16)
        tlo_d = dram("tlo_d", (EP,), BF16)
        rcnt_d = dram("rcnt_d", (EP,))
        amp_d = dram("amp_d", (EP,))
        att_amp_d = dram("att_amp_d", (EP,))
        ew_d = dram("ew_d", (EP,))
        comp_d = dram("comp_d", (4, EP))
        where_d = dram("where_d", (N, 1), I32)
        ta = dram("ta", (N + EP, D))
        tb = dram("tb", (N + EP, D))

        def flat(t, p):
            return t.rearrange("(p c) -> p c", p=p)

        def edge_rows(t, i):
            return t[N:N + EP, :].rearrange("(a p c) d -> p a (c d)", p=P, c=8)[:, bass.ds(i, 1), :] \
                .rearrange("p a c -> p (a c)")

        ident = sb("ident", [P, P])
        ones = sb("ones", [P, P])
        XD = sb("XD", [P, NPAIR * 512])
        HH = sb("HH", [P, NPAIR * 512])
        LI = sb("LI", [P, NPAIR, 4, 8], I32)
        IX = sb("IX", [P, NPAIR * 8], I32)
        LASTF = sb("LASTF", [P, NPAIR * 8])
        RCL = sb("RCL", [P, NPAIR * 8])
        CB = sb("CB", [P, D])
        AB = sb("AB", [P, D])
        cols = sb("cols", [P, 32])
        (C_EPS, C_NLIM, C_ATT, C_WEB, C_WAB, C_SGN, C_PRE, C_SPRE, C_POST, C_Z, C_R, C_IN, C_HN,
         C_DZ, C_DR, C_DIN, C_AVG, C_RAVG, C_ONE, C_G0, C_G1, C_G2, C_G3, C_L0, C_L1,
         C_EMPTY, C_TWO) = range(27)

        def col(n, a=0, b=P):
            return cols[a:b, n:n + 1]

        PS = [ctx.enter_context(nc.psum_tensor(f"ps{n}", [P, 512], F32)) for n in range(8)]

        W0S = sb("W0S", [P, 4, 4, D])
        bd = {n: sb("bd_" + n, [P, P]) for n in (
            "sumA", "sumB", "w1", "wews", "wr", "we", "wa",
            "hsA", "hsB", "hdA", "hdB", "mmA", "mmB", "xxA", "xxB", "mq", "xq", "u0",
            "z", "r", "in", "hz", "hr", "hn", "dz", "dr", "din")}
        attw = sb("attw", [4, P])
        sel = sb("sel", [P, 2])

        G = [sb(f"G{k}", [P, 8, D]) for k in range(2)]
        XG = [sb(f"XG{k}", [P, 8, D]) for k in range(2)]
        MST = sb("MST", [P, 2, 8], I32)
        MG = [sb(f"MG{k}", [P, 8], I32) for k in range(2)]
        ST = [sb(f"ST{k}", [P, 4, 8], I32) for k in range(2)]
        Y = [sb(f"Y{k}", [P, 8, D]) for k in range(2)]
        XC = [sb(f"XC{k}", [P, 8, D]) for k in range(2)]
        SQ = [sb(f"SQ{k}", [P, 8, D]) for k in range(2)]
        H = [sb(f"H{k}", [P, 8, 2, D]) for k in range(2)]
        SM = [sb(f"SM{k}", [P, 4, 8]) for k in range(2)]
        big = [sb(f"big{k}", [P, 1024]) for k in range(8)]

        def bc8(t):
            return t.rearrange("p (c o) -> p c o", o=1).broadcast_to([t.shape[0], 8, D])

        def bcd(t, p=P):
            return t.rearrange("p (o d) -> p o d", o=1).broadcast_to([p, 8, D])

        def rows(t):
            return t.rearrange("p (c d) -> p c d", d=D)

        stage_over()

        zeros_i = HH[0:1, 0:4 * (EP - E)].bitcast(I32)
        node_n = HH[0:1, 2400:2400 + EP - E + 1].bitcast(I32)
        minus1 = HH[0:1, 3008:3010].bitcast(I32)
        iota_w = HH[0:125, 3072:3072 + N // 125].bitcast(I32)
        with nc.Block() as block:
            @block.gpsimd
            def _(pool):
                nc.gpsimd.memset(zeros_i[:], 0).then_inc(sem("pads made"), 1)
                nc.gpsimd.memset(node_n[:], N).then_inc(sem("pads made"), 1)
                nc.gpsimd.memset(minus1[:], -1).then_inc(sem("pads made"), 1)
                nc.gpsimd.iota(iota_w[:], [[1, N // 125]], base=0, channel_multiplier=N // 125).then_inc(sem("pads made"), 1)
                nc.gpsimd.memset(ident[:], 0.0).then_inc(sem("ident zero"), 1)
                nc.gpsimd.memset(ones[:], 1.0)
                pool.wait_ge(sem("ident zero"), 1)
                nc.gpsimd.affine_select(out=ident[:], in_=ident[:], compare_op=ALU.not_equal, fill=1.0,
                                        base=0, pattern=[[-1, P]], channel_multiplier=1)
                nc.gpsimd.iota(LI[:, :, 3, :], [[PAIR, NPAIR], [1, 8]], base=N, channel_multiplier=8)

            @block.sync
            def _(sp):
                s = sem("lists copied")
                sp.dma_start(flat(src_d[0:E], 125), flat(src, 125)).then_inc(s, 16)
                sp.dma_start(flat(dst_d[1:E + 1], 125), flat(dst, 125)).then_inc(s, 16)
                sp.dma_start(flat(typ_d[0:E], 125), flat(etype, 125)).then_inc(s, 16)
                sp.dma_start(att_d[0:E, :].rearrange("(p c) d -> p (c d)", p=125),
                             attr.rearrange("(p c) d -> p (c d)", p=125)).then_inc(s, 16)
                sp.wait_ge(sem("pads made"), 4)

                def line(t):
                    return t.rearrange("(o c) -> o c", o=1)
                sp.dma_start(line(src_d[E:EP]), zeros_i[:, 0:EP - E]).then_inc(s, 16)
                sp.dma_start(line(typ_d[E:EP]), zeros_i[:, 0:EP - E]).then_inc(s, 16)
                sp.dma_start(line(att_d[E:EP, :].rearrange("e d -> (e d)")), zeros_i[:].bitcast(F32)).then_inc(s, 16)
                sp.dma_start(line(dst_d[E + 1:EP + 2]), node_n[:]).then_inc(s, 16)
                sp.dma_start(line(dst_d[0:1]), minus1[:, 0:1]).then_inc(s, 16)
                sp.dma_start(where_d.rearrange("(p c) o -> p (c o)", p=125), iota_w[:]).then_inc(s, 16)
                sp.wait_ge(s, 160)

        stage_over()

        taken = [0]

        def rl(name, dt=F32, w=256):
            words = w * (2 if dt == BF16 else 4) // 4
            t = XD[0:RQ, taken[0]:taken[0] + words]
            taken[0] += words
            return t if dt == F32 else t.bitcast(dt)
        r_src, r_typ, r_dst, r_prev, r_next = (rl(n, I32) for n in ("r_src", "r_typ", "r_dst", "r_prev", "r_next"))
        r_att = rl("r_att", F32, 1024)
        r_e = rl("r_e", I32)
        r_sp, r_sn, r_hi, r_lo = (rl(n, BF16) for n in ("r_sp", "r_sn", "r_hi", "r_lo"))
        f_src, f_dst, f_sc, f_cnt, f_last = (big[n][0:RQ, 0:256] for n in range(5))
        r_ef, r_st, r_loc = (big[n][0:RQ, 256:512] for n in range(3))
        r_hii, r_loi = (rl(n, I32) for n in ("r_hii", "r_loi"))
        r_rc, r_lg, r_s, r_q, r_rl = (big[n][0:RQ, 512:768] for n in range(5))
        r_ew, r_c0, r_c1, r_c2, r_one = (big[n][0:RQ, 768:1024] for n in range(5))
        carry_row = sb("carry_row", [1, RQ + 1])
        carry_col = sb("carry_col", [RQ, 1])
        nv = big[6][0:125, 0:400]
        nvl = big[7][0:125, 0:400]
        nvs = sb("nvs", [125, 1])
        with nc.Block() as block:
            @block.sync
            def _(sp):
                s = sem("rows loaded")
                for t, d in ((r_src, src_d), (r_typ, typ_d), (r_dst, dst_d[1:EP + 1]), (r_prev, dst_d[0:EP]),
                             (r_next, dst_d[2:EP + 2])):
                    sp.dma_start(t[:], flat(d, RQ)).then_inc(s, 16)
                sp.dma_start(r_att[:], att_d.rearrange("(p c) d -> p (c d)", p=RQ)).then_inc(s, 16)
                sp.dma_start(nv, flat(node_vec, 125)).then_inc(sem("node_vec loaded"), 16)
                w = sem("edge values written")
                sp.wait_ge(sem("flags"), 9)
                sp.dma_start(flat(same_prev_d, RQ), r_sp[:]).then_inc(w, 16)
                sp.dma_start(flat(same_next_d, RQ), r_sn[:]).then_inc(w, 16)
                sp.dma_start(flat(thi_d, RQ), r_hi[:]).then_inc(w, 16)
                sp.dma_start(flat(tlo_d, RQ), r_lo[:]).then_inc(w, 16)
                sp.wait_ge(sem("components"), 5)
                sp.dma_start(flat(ew_d, RQ), r_ew).then_inc(w, 16)
                for n, t in enumerate((r_c0, r_c1, r_c2, r_one)):
                    sp.dma_start(flat(comp_d[n, :], RQ), t).then_inc(w, 16)
                sp.wait_ge(sem("scalers"), 4)
                sp.dma_start(flat(rcnt_d, RQ), r_rc).then_inc(w, 16)
                sp.dma_start(flat(amp_d, RQ), r_s).then_inc(w, 16)
                sp.dma_start(flat(att_amp_d, RQ), r_q).then_inc(w, 16)
                sp.wait_ge(w, 16 * 12)

            @block.gpsimd
            def _(pool):
                nc.gpsimd.iota(r_e[:], [[1, 256]], base=0, channel_multiplier=256).then_inc(sem("edge numbers"), 1)

            @block.vector
            def _(dve):
                dve.wait_ge(sem("rows loaded"), 96)
                f = sem("flags")
                nc.vector.tensor_tensor(r_sp[:], r_dst[:], r_prev[:], ALU.is_equal).then_inc(f, 1)
                nc.vector.tensor_tensor(r_sn[:], r_dst[:], r_next[:], ALU.is_equal).then_inc(f, 1)
                nc.vector.tensor_scalar(r_hii[:], r_typ[:], 2, None, ALU.logical_shift_right).then_inc(f, 1)
                nc.vector.tensor_scalar(r_loi[:], r_typ[:], 3, None, ALU.bitwise_and).then_inc(f, 1)
                dve.wait_ge(f, 4)
                nc.vector.tensor_copy(r_hi[:], r_hii[:]).then_inc(f, 1)
                nc.vector.tensor_copy(r_lo[:], r_loi[:]).then_inc(f, 1)
                nc.vector.tensor_copy(f_src, r_src[:]).then_inc(f, 1)
                nc.vector.tensor_scalar(f_dst, r_dst[:], float(N - 1), None, ALU.min).then_inc(f, 1)
                nc.vector.tensor_scalar(f_last, r_sn[:], -1.0, 1.0, ALU.mult, ALU.add).then_inc(f, 1)
                nc.vector.scalar_tensor_tensor(out=f_sc, in0=r_sn[:], scalar=FAR, in1=r_dst[:],
                                               op0=ALU.mult, op1=ALU.add).then_inc(sem("far"), 1)
                c = sem("components")
                av = r_att[:].rearrange("p (e c) -> p e c", c=4)
                nc.vector.tensor_copy(r_ew, av[:, :, 3]).then_inc(c, 1)
                for n, t in enumerate((r_c0, r_c1, r_c2)):
                    nc.vector.tensor_copy(t, av[:, :, n]).then_inc(c, 1)
                nc.vector.memset(r_one, 1.0).then_inc(c, 1)
                q = sem("count steps")
                dve.wait_ge(sem("edge numbers"), 1)
                nc.vector.tensor_copy(r_ef, r_e[:]).then_inc(q, 1)
                nc.vector.tensor_scalar(r_st, r_sp[:], -1.0, 1.0, ALU.mult, ALU.add).then_inc(q, 1)
                dve.wait_ge(q, 2)
                nc.vector.tensor_tensor(r_st, r_st, r_ef, ALU.mult).then_inc(q, 1)
                dve.wait_ge(q, 3)
                nc.vector.tensor_tensor_scan(r_loc, r_st, r_st, 0.0, ALU.max, ALU.max).then_inc(q, 1)
                nc.vector.memset(carry_row[:, 0:1], 0.0).then_inc(q, 1)
                dve.wait_ge(sem("carry turned"), 1)
                dve.wait_ge(q, 5)
                nc.vector.tensor_copy(carry_row[:, 1:RQ + 1], PS[0][0:1, 0:RQ]).then_inc(q, 1)
                dve.wait_ge(q, 6)
                nc.vector.tensor_tensor_scan(carry_row[:, 1:RQ + 1], carry_row[:, 1:RQ + 1], carry_row[:, 1:RQ + 1],
                                             0.0, ALU.max, ALU.max).then_inc(q, 1)
                dve.wait_ge(sem("carry turned"), 2)
                nc.vector.tensor_copy(carry_col[:], PS[1][0:RQ, 0:1]).then_inc(q, 1)
                dve.wait_ge(q, 8)
                nc.vector.tensor_scalar(r_loc, r_loc, carry_col[:, 0:1], None, ALU.max).then_inc(q, 1)
                dve.wait_ge(q, 9)
                nc.vector.tensor_tensor(f_cnt, r_ef, r_loc, ALU.subtract).then_inc(q, 1)
                dve.wait_ge(q, 10)
                nc.vector.tensor_scalar(f_cnt, f_cnt, 1.0, None, ALU.add).then_inc(sem("counts"), 1)
                dve.wait_ge(sem("log sum"), 1)
                nc.vector.tensor_scalar(col(C_AVG), PS[2][:, 0:1], 1.0 / N, None, ALU.mult).then_inc(q, 1)
                dve.wait_ge(q, 11)
                nc.vector.reciprocal(col(C_RAVG), col(C_AVG)).then_inc(q, 1)
                dve.wait_ge(sem("counts"), 1)
                nc.vector.reciprocal(r_rc, f_cnt).then_inc(sem("scalers"), 1)
                dve.wait_ge(sem("log counts"), 1)
                nc.vector.reciprocal(r_rl, r_lg).then_inc(sem("scalers"), 1)
                dve.wait_ge(q, 12)
                nc.vector.tensor_scalar(r_s, r_lg, col(C_RAVG, 0, RQ), None, ALU.mult).then_inc(sem("scalers"), 1)
                dve.wait_ge(sem("scalers"), 3)
                nc.vector.scalar_tensor_tensor(out=r_q, in0=r_rl, scalar=col(C_AVG, 0, RQ), in1=r_s,
                                               op0=ALU.mult, op1=ALU.mult).then_inc(sem("scalers"), 1)
                dve.wait_ge(sem("lists turned"), 10)

                def turned(n, half):
                    return PS[3 + n // 2][:, (n % 2) * 256 + half * 100:(n % 2) * 256 + half * 100 + RQ] \
                        .rearrange("p (a h j) -> p a j h", h=2, j=2)

                def placed(t, half):
                    return t.rearrange("p a (j k h) -> p a j k h", j=2, k=2)[:, :, :, half, :]
                for half in range(2):
                    for n in range(3):
                        nc.vector.tensor_copy(placed(LI[:, :, n, :], half), turned(n, half)).then_inc(sem("lists"), 1)
                    nc.vector.tensor_copy(placed(RCL[:].rearrange("p (a c) -> p a c", c=8), half), turned(3, half)).then_inc(sem("lists"), 1)
                    nc.vector.tensor_copy(placed(LASTF[:].rearrange("p (a c) -> p a c", c=8), half), turned(4, half)).then_inc(sem("lists"), 1)
                dve.wait_ge(sem("lists"), 10)
                nc.vector.reciprocal(RCL[:], RCL[:]).then_inc(sem("lists"), 1)
                dve.wait_ge(sem("lists"), 11)
                nc.vector.tensor_tensor(RCL[:], RCL[:], LASTF[:], ALU.mult)

            @block.scalar
            def _(act):
                act.wait_ge(sem("node_vec loaded"), 16)
                nc.scalar.activation(nvl, nv, ACT.Ln, bias=1.0, accum_out=nvs[:]).then_inc(sem("logs"), 1)
                act.wait_ge(sem("counts"), 1)
                nc.scalar.activation(r_lg, f_cnt, ACT.Ln, bias=1.0).then_inc(sem("log counts"), 1)

            @block.tensor
            def _(pe):
                pe.wait_ge(sem("logs"), 1)
                nc.tensor.matmul(PS[2][:, 0:1], ones[0:125, :], nvs[:], start=True, stop=True).then_inc(sem("log sum"), 1)
                pe.wait_ge(sem("count steps"), 4)
                nc.tensor.transpose(PS[0][0:1, 0:RQ], r_loc[:, 255:256], ident[0:RQ, 0:RQ]).then_inc(sem("carry turned"), 1)
                pe.wait_ge(sem("count steps"), 7)
                nc.tensor.transpose(PS[1][0:RQ, 0:1], carry_row[:, 0:RQ], ident[0:1, 0:1]).then_inc(sem("carry turned"), 1)
                pe.wait_ge(sem("flags"), 9)
                pe.wait_ge(sem("far"), 1)
                pe.wait_ge(sem("counts"), 1)
                for n, t in enumerate((f_src, f_dst, f_sc, f_cnt, f_last)):
                    for half in range(2):
                        o = (n % 2) * 256 + half * 100
                        nc.tensor.transpose(PS[3 + n // 2][:, o:o + RQ], t[:, half * P:(half + 1) * P],
                                            ident[0:RQ, 0:RQ]).then_inc(sem("lists turned"), 1)

        stage_over()

        used = [4096]

        def wt(name, a, b):
            t = HH[0:a, used[0]:used[0] + b]
            used[0] += b
            return t
        t_we, t_ws2, t_w3, t_p3, t_wih, t_whh = (wt(n, D, w) for n, w in (
            ("we", 64), ("ws2", 128), ("w3", 64), ("p3", 128), ("wih", 192), ("whh", 192)))
        t_pre = wt("pre", D, 192)
        t_e3 = wt("e3", 4, D)
        t_web, t_post_col = wt("web", D, 1), wt("bpost", D, 1)
        t_std = wt("std", D, 192)
        t_big = [big[n][:, :] for n in range(8)]
        o_mm, o_xx, q_mm, q_xx = t_big[0][:, 0:64], t_big[1][:, 0:64], t_big[2][:, 0:128], t_big[3][:, 0:128]
        t_wet, t_w3t, t_ut = t_big[4][0:D, 0:64], t_big[4][0:D, 64:128], t_big[4][0:D, 128:192]
        t_e3t = t_big[4][0:D, 192:196]
        t_w3p = t_big[5][0:D, 0:192]
        t_gin = t_big[6][0:D, 0:192]
        t_bias = t_big[7][:, 0:16]
        t_co, t_sc = wt("co", D, 1), wt("sc", D, 3)
        NAT = D

        def wpost_rows(scaling, aggregate):
            o = NAT * (1 + 4 * scaling + aggregate)
            return wpost[o:o + NAT, :]
        MEAN, MIN, MAX, STD = range(4)

        def column(v):
            return v.rearrange("(p o) -> p o", o=1)
        loads = []
        for g2 in range(2):
            for k in range(4):
                r0 = 8 * k + 4 * g2
                loads.append((W0S[g2 * D:(g2 + 1) * D, k, :, :], w0[r0:r0 + 4].rearrange("x i o -> i x o")))
        for h in range(2):
            q = slice(h * D, (h + 1) * D)
            loads += [(bd["w1"][q, q], w1), (bd["wr"][q, q], wr_k.rearrange("f h d -> f (h d)")),
                      (bd["we"][q, q], we_k.rearrange("f h d -> f (h d)")),
                      (bd["z"][q, q], wih[:, 64:128]), (bd["r"][q, q], wih[:, 0:64]), (bd["in"][q, q], wih[:, 128:192]),
                      (bd["hz"][q, q], whh[:, 64:128]), (bd["hr"][q, q], whh[:, 0:64]), (bd["hn"][q, q], whh[:, 128:192]),
                      (t_ws2[:, q], ws_k), (t_p3[:, q], wpre[128:192, :])]
            for n, v in enumerate((ws_b, wr_b.rearrange("h d -> (h d)"), we_b.rearrange("h d -> (h d)"), bpre, bpost,
                                   bih[64:128], bhh[64:128], bih[0:64], bhh[0:64], bih[128:192], bhh[128:192])):
                loads.append((t_bias[q, n:n + 1], column(v)))
            loads += [(o_mm[q, :], wpost_rows(0, (MEAN, STD)[h])), (o_xx[q, :], wpost_rows(0, (MAX, MIN)[h]))]
            for n in range(2):
                loads += [(q_mm[q, n * D:(n + 1) * D], wpost_rows(1 + n, (MEAN, STD)[h])),
                          (q_xx[q, n * D:(n + 1) * D], wpost_rows(1 + n, (MAX, MIN)[h]))]
        loads += [(t_we[:], we_k.rearrange("f h d -> f (h d)")), (t_w3[:], w3), (t_wih[:], wih), (t_whh[:], whh),
                  (t_pre[:, 0:64], wpre[0:64, :]), (t_pre[:, 64:128], wpre[64:128, :]), (t_pre[:, 128:192], wpost[0:64, :]),
                  (t_e3[0:3, :], w3e), (t_e3[3:4, :], b3e.rearrange("(o d) -> o d", o=1)),
                  (t_web[:], column(we_b.rearrange("h d -> (h d)"))), (t_post_col[:], column(bpost)),
                  (col(C_WAB), wa_b.rearrange("(o d) -> o d", o=1).broadcast_to([P, 1]))]
        for n in range(3):
            loads.append((t_std[:, n * D:(n + 1) * D], wpost_rows(n, STD)))
        t_wa = wt("wa", P, 1)
        loads += [(t_wa[h * D:(h + 1) * D, :], wa_k) for h in range(2)]
        BLOCKS = ("w1", "wr", "we", "z", "r", "in", "hz", "hr", "hn")
        with nc.Block() as block:
            @block.gpsimd
            def _(pool):
                for t in BLOCKS:
                    nc.gpsimd.memset(bd[t][:], 0.0).then_inc(sem("blocks cleared"), 1)
                for t in ("sumA", "sumB", "wews", "wa", "hsA", "hsB", "hdA", "hdB", "mmA", "mmB", "xxA", "xxB", "u0",
                          "dz", "dr", "din"):
                    nc.gpsimd.memset(bd[t][:], 0.0).then_inc(sem("products cleared"), 1)
                nc.gpsimd.memset(sel[:], 0.0).then_inc(sem("products cleared"), 1)

            @block.sync
            def _(sp):
                sp.wait_ge(sem("blocks cleared"), len(BLOCKS))
                for t, v in loads[::2]:
                    sp.dma_start(t, v).then_inc(sem("weights loaded"), 16)

            @block.scalar
            def _(act):
                act.wait_ge(sem("blocks cleared"), len(BLOCKS))
                for t, v in loads[1::2]:
                    act.dma_start(t, v).then_inc(sem("weights loaded"), 16)

            @block.tensor
            def _(pe):
                pe.wait_ge(sem("weights loaded"), 16 * len(loads))
                i64 = ident[0:D, 0:D]
                nc.tensor.transpose(PS[0][0:D, 0:64], t_we[:], i64)
                nc.tensor.transpose(PS[0][0:D, 64:128], t_w3[:], i64)
                nc.tensor.transpose(PS[0][0:D, 192:196], t_e3[:], ident[0:4, 0:4]).then_inc(sem("products"), 1)
                pe.wait_ge(sem("factors"), 1)
                nc.tensor.matmul(PS[1][0:D, 0:64], t_wet, t_ws2[:, 0:64], start=True, stop=True)
                nc.tensor.matmul(PS[1][0:D, 64:256], t_w3t, t_pre[:], start=True, stop=True)
                nc.tensor.matmul(PS[1][0:4, 256:384], t_e3t, t_p3[:], start=True, stop=True)
                nc.tensor.matmul(PS[1][:, 384:385], t_ws2[:], t_web[:], start=True, stop=True).then_inc(sem("products"), 1)
                pe.wait_ge(sem("factors"), 2)
                nc.tensor.transpose(PS[2][0:D, 0:64], t_w3p[:, 128:192], i64).then_inc(sem("products"), 1)
                pe.wait_ge(sem("factors"), 3)
                nc.tensor.matmul(PS[3][0:D, 0:192], t_ut, t_wih[:], start=True, stop=True).then_inc(sem("products"), 1)
                for n in range(3):
                    nc.tensor.matmul(PS[4][0:D, 0:1], t_std[:, n * D:(n + 1) * D], t_sc[:, n:n + 1],
                                     start=(n == 0), stop=(n == 2))
                nc.tensor.matmul(PS[5][:, 0:1], ident[:], t_bias[:, 0:1], start=True, stop=True).then_inc(sem("products"), 1)
                pe.wait_ge(sem("factors"), 4)
                for n, g in enumerate((1, 0, 2)):
                    for h in range(2):
                        nc.tensor.matmul(PS[6][h * D:(h + 1) * D, n:n + 1], t_wih[:, g * D:(g + 1) * D], t_co[:],
                                         start=True, stop=True).then_inc(sem("empty gates"), 1)

            @block.vector
            def _(dve):
                f = sem("factors")
                b = sem("stationaries")
                nc.vector.memset(col(C_EPS), EPS).then_inc(sem("constants"), 1)
                nc.vector.memset(col(C_NLIM), -LIMIT).then_inc(sem("constants"), 1)
                nc.vector.memset(col(C_ONE), 1.0).then_inc(sem("constants"), 1)
                nc.vector.memset(col(C_TWO), 2.0).then_inc(sem("constants"), 1)
                nc.vector.memset(col(C_EMPTY), EPS ** 0.5).then_inc(sem("constants"), 1)
                nc.vector.memset(col(C_SGN, 0, D), 1.0).then_inc(sem("constants"), 1)
                nc.vector.memset(col(C_SGN, D, P), -1.0).then_inc(sem("constants"), 1)
                for h in range(2):
                    for k in range(4):
                        nc.vector.memset(col(C_G0 + k, h * D, (h + 1) * D), float(2 * k + h)).then_inc(sem("constants"), 1)
                    for m in range(2):
                        nc.vector.memset(col(C_L0 + m, h * D, (h + 1) * D), float(2 * m + h)).then_inc(sem("constants"), 1)
                dve.wait_ge(sem("constants"), 19)
                dve.wait_ge(sem("products"), 1)
                nc.vector.tensor_copy(t_big[4][0:D, 0:128], PS[0][0:D, 0:128]).then_inc(b, 1)
                nc.vector.tensor_copy(t_e3t, PS[0][0:D, 192:196]).then_inc(f, 1)
                nc.vector.tensor_copy(t_sc[:, 0:1], col(C_EMPTY, 0, D)).then_inc(b, 1)
                dve.wait_ge(b, 2)
                import math
                ln2 = math.log(2.0)
                nc.vector.scalar_tensor_tensor(out=t_sc[:, 1:2], in0=col(C_RAVG, 0, D), scalar=ln2, in1=t_sc[:, 0:1],
                                               op0=ALU.mult, op1=ALU.mult).then_inc(b, 1)
                dve.wait_ge(b, 3)
                nc.vector.scalar_tensor_tensor(out=t_sc[:, 2:3], in0=col(C_AVG, 0, D), scalar=1.0 / ln2, in1=t_sc[:, 1:2],
                                               op0=ALU.mult, op1=ALU.mult).then_inc(b, 1)
                dve.wait_ge(sem("products"), 2)
                nc.vector.tensor_copy(t_w3p, PS[1][0:D, 64:256]).then_inc(f, 1)
                dve.wait_ge(sem("products cleared"), 17)
                for h in range(2):
                    q = slice(h * D, (h + 1) * D)
                    i64 = ident[q, q]
                    nc.vector.tensor_copy(bd["wews"][q, q], PS[1][0:D, 0:64]).then_inc(b, 1)
                    for n in range(2):
                        c = slice(n * D, (n + 1) * D)
                        t = bd[("hdA", "hdB")[h]]
                        nc.vector.tensor_copy(t[q, c], PS[1][0:D, 64:128]).then_inc(b, 1)
                        t = bd[("hsA", "hsB")[h]]
                        nc.vector.tensor_copy(t[q, c], PS[1][0:D, 128:192]).then_inc(b, 1)
                    nc.vector.tensor_copy(bd["u0"][q, q], PS[1][0:D, 192:256]).then_inc(b, 1)
                    nc.vector.tensor_copy(bd["sumA"][q, 0:D], i64).then_inc(b, 1)
                    nc.vector.tensor_copy(bd["sumB"][q, D:P], i64).then_inc(b, 1)
                    nc.vector.tensor_copy(sel[h * D:h * D + 1, h:h + 1], ones[h * D:h * D + 1, 0:1]).then_inc(b, 1)
                    nc.vector.tensor_copy(bd["wa"][q, q], t_wa[q, 0:1].broadcast_to([D, D])).then_inc(b, 1)
                nc.vector.tensor_copy(attw[:], PS[1][0:4, 256:384]).then_inc(b, 1)
                nc.vector.tensor_copy(bd["mmA"][:, 0:D], o_mm).then_inc(b, 1)
                nc.vector.tensor_copy(bd["mmB"][:, D:P], o_mm).then_inc(b, 1)
                nc.vector.tensor_copy(bd["mq"][:], q_mm).then_inc(b, 1)
                nc.vector.tensor_scalar(bd["xxA"][:, 0:D], o_xx, col(C_SGN), None, ALU.mult).then_inc(b, 1)
                nc.vector.tensor_scalar(bd["xxB"][:, D:P], o_xx, col(C_SGN), None, ALU.mult).then_inc(b, 1)
                nc.vector.tensor_scalar(bd["xq"][:], q_xx, col(C_SGN), None, ALU.mult).then_inc(b, 1)
                nc.vector.tensor_tensor(col(C_ATT), PS[1][:, 384:385], t_bias[:, 0:1], ALU.add).then_inc(b, 1)
                dve.wait_ge(b, 4 + 20 + 8)
                nc.vector.tensor_tensor(col(C_ATT), col(C_ATT), t_bias[:, 1:2], ALU.add).then_inc(b, 1)
                nc.vector.tensor_copy(col(C_WEB), t_bias[:, 2:3]).then_inc(b, 1)
                nc.vector.tensor_copy(col(C_PRE), t_bias[:, 3:4]).then_inc(b, 1)
                nc.vector.tensor_scalar(col(C_SPRE), t_bias[:, 3:4], col(C_SGN), None, ALU.mult).then_inc(b, 1)
                nc.vector.tensor_copy(col(C_POST), t_bias[:, 4:5]).then_inc(b, 1)
                nc.vector.tensor_tensor(col(C_Z), t_bias[:, 5:6], t_bias[:, 6:7], ALU.add).then_inc(b, 1)
                nc.vector.tensor_tensor(col(C_R), t_bias[:, 7:8], t_bias[:, 8:9], ALU.add).then_inc(b, 1)
                nc.vector.tensor_copy(col(C_IN), t_bias[:, 9:10]).then_inc(b, 1)
                nc.vector.tensor_copy(col(C_HN), t_bias[:, 10:11]).then_inc(b, 1)
                dve.wait_ge(sem("products"), 3)
                nc.vector.tensor_copy(t_ut, PS[2][0:D, 0:64]).then_inc(f, 1)
                dve.wait_ge(sem("products"), 4)
                nc.vector.tensor_copy(t_gin, PS[3][0:D, 0:192]).then_inc(b, 1)
                dve.wait_ge(sem("products"), 5)
                nc.vector.tensor_tensor(t_co[:], PS[4][0:D, 0:1], t_post_col[:], ALU.add).then_inc(f, 1)
                dve.wait_ge(b, 4 + 20 + 8 + 10)
                for h in range(2):
                    q = slice(h * D, (h + 1) * D)
                    nc.vector.tensor_tensor(t_big[7][0:D, 64 + 192 * h:128 + 192 * h], t_gin[:, 64:128], t_whh[:, 64:128], ALU.add).then_inc(b, 1)
                    nc.vector.tensor_tensor(t_big[7][0:D, 128 + 192 * h:192 + 192 * h], t_gin[:, 0:64], t_whh[:, 0:64], ALU.add).then_inc(b, 1)
                    dve.wait_ge(b, 42 + 5 * h + 2)
                    nc.vector.tensor_copy(bd["dz"][q, q], t_big[7][0:D, 64 + 192 * h:128 + 192 * h]).then_inc(b, 1)
                    nc.vector.tensor_copy(bd["dr"][q, q], t_big[7][0:D, 128 + 192 * h:192 + 192 * h]).then_inc(b, 1)
                    nc.vector.tensor_copy(bd["din"][q, q], t_gin[:, 128:192]).then_inc(b, 1)
                dve.wait_ge(sem("empty gates"), 6)
                for n, (o, i) in enumerate(((C_DZ, C_Z), (C_DR, C_R), (C_DIN, C_IN))):
                    nc.vector.tensor_tensor(col(o), PS[6][:, n:n + 1], col(i), ALU.add)

        stage_over()

        TY = [sb(f"TY{k}", [P, 2, 1024], BF16) for k in range(2)]
        FL = [sb(f"FL{k}", [P, 512], BF16) for k in range(2)]
        S = sb("S", [P, 512])
        CR = sb("CR", [P, 2])
        MASKED = [[big[2 * h + k // 2][:, (k % 2) * 512:(k % 2 + 1) * 512] for k in range(4)] for h in range(2)]
        CHOSEN = [[big[4 + h][:, m * 512:(m + 1) * 512] for m in range(2)] for h in range(2)]

        def load_flags(sp, t, flags, i, name):
            for h in range(2):
                sp.dma_start(t[h * D:(h + 1) * D, :],
                             flags[bass.ds(i * PAIR + h * HALF, HALF)].rearrange("(o c) -> o c", o=1)
                             .broadcast_to([D, HALF])).then_inc(sem(name), 16)

        def ln_sum(dve, t, k, name, i, bias=False):
            v = t
            if bias:
                nc.vector.tensor_tensor(Y[k][:], t, bcd(CB[:]), ALU.add).then_inc(sem(name + " y"), 1)
                dve.wait_ge(sem(name + " y"), i + 1)
                v = Y[k][:]
            nc.vector.tensor_reduce(SM[k][:, 0, :], v, AX.X, ALU.add).then_inc(sem(name + " sum"), 1)
            dve.wait_ge(sem(name + " sum"), i + 1)
            nc.vector.scalar_tensor_tensor(out=XC[k][:], in0=bc8(SM[k][:, 0, :]), scalar=-1.0 / D, in1=v,
                                           op0=ALU.mult, op1=ALU.add).then_inc(sem(name + " centred"), 1)

        def ln_square(act, k, name, i):
            act.wait_ge(sem(name + " centred"), i + 1)
            nc.scalar.activation(SQ[k][:], XC[k][:], ACT.Square).then_inc(sem(name + " squares"), 1)

        def ln_var(dve, k, name, i):
            dve.wait_ge(sem(name + " squares"), i + 1)
            nc.vector.tensor_reduce(SM[k][:, 1, :], SQ[k][:], AX.X, ALU.add).then_inc(sem(name + " var"), 1)

        def ln_rstd(act, k, name, i):
            act.wait_ge(sem(name + " var"), i + 1)
            nc.scalar.activation(SM[k][:, 2, :], SM[k][:, 1, :], ACT.Ln, scale=1.0 / D, bias=col(C_EPS)).then_inc(sem(name + " log"), 1)
            act.wait_ge(sem(name + " log"), i + 1)
            nc.scalar.activation(SM[k][:, 3, :], SM[k][:, 2, :], ACT.Exp, scale=-0.5).then_inc(sem(name + " rstd"), 1)

        def ln_out(dve, k, name, i, twice=False):
            dve.wait_ge(sem(name + " rstd"), i + 1)
            for c in range(2 if twice else 1):
                nc.vector.scalar_tensor_tensor(out=H[k][:, :, c, :] if twice else H[k][:].rearrange("p a b d -> p (a b d)")[:, 0:512].rearrange("p (c d) -> p c d", d=D),
                                               in0=XC[k][:], scalar=0.0, in1=bc8(SM[k][:, 3, :]),
                                               op0=ALU.max, op1=ALU.mult).then_inc(sem(name + " h"), 1)

        def hrow(k, j):
            return H[k][:].rearrange("p a b d -> p (a b d)")[:, j * P:(j + 1) * P]

        def scan_pair(dve, out, flags, data, carry, name, n):
            for h in range(2):
                q = slice(h * D, (h + 1) * D)
                o = slice((1 - h) * D, (2 - h) * D)
                nc.vector.tensor_tensor_scan(out[q, :], flags[q, :], data[q, :], carry[q, 0:1], ALU.mult, ALU.add).then_inc(sem(name), 1)
                dve.wait_ge(sem(name), n + 2 * h + 1)
                nc.vector.tensor_copy(carry[o, 0:1], out[q, 511:512]).then_inc(sem(name), 1)
                dve.wait_ge(sem(name), n + 2 * h + 2)

        with nc.Block() as block:
            @block.scalar
            def _(act):
                for t in (ta, tb):
                    act.dma_start(t[0:N, :].rearrange("n d -> (n d)").rearrange("(p c) -> p c", p=1280),
                                  x.rearrange("n d -> (n d)").rearrange("(p c) -> p c", p=1280)).then_inc(sem("tables filled"), 16)

                def stage(i, k):
                    nc.scalar.activation(ST[k][:], LI[:, bass.ds(i, 1), :, :].rearrange("p a b c -> p (a b) c"), ACT.Copy).then_inc(sem("l0 staged"), 1)
                stage(0, 0)
                stage(1, 1)
                ln_square(act, 0, "l0", 0)
                ln_rstd(act, 0, "l0", 0)

                def body(i, r, k):
                    if exists(i + 1):
                        ln_square(act, 1 - k, "l0", i + 1)
                        ln_rstd(act, 1 - k, "l0", i + 1)
                    act.wait_ge(sem(f"l0 where landed {k}"), 128 * r + 128)
                    nc.scalar.activation(IX[:, bass.ds(i * 8, 8)], MG[k][:], ACT.Copy).then_inc(sem("l0 where kept"), 1)
                    if exists(i + 2):
                        act.wait_ge(sem("l0 x1"), i + 1)
                        stage(i + 2, k)
                rounds(act, body)

            @block.gpsimd
            def _(pool):
                with pool.Fori(0, NPAIR) as i:
                    nc.gpsimd.tensor_copy(MST[:], LI[:, bass.ds(i, 1), 2:4, :].rearrange("p a b c -> p (a b) c")).then_inc(sem("where staged"), 1)
                    pool.wait_ge(sem("where staged"), i + 1)
                    pool.sem_inc(sem("where turn"), 1)
                    for c in range(8):
                        nc.gpsimd.indirect_dma_start(where_d, bass.IndirectOffsetOnAxis(ap=MST[:, 0, c:c + 1], axis=0),
                                                     MST[:, 1, c:c + 1], None, bounds_check=N - 1, oob_is_err=False).then_inc(sem("where written"), 16)
                    pool.wait_ge(sem("where written"), 128 * i + 128)

                def body(i, r, k):
                    pool.wait_ge(sem("l0 staged"), i + 1)
                    pool.sem_inc(sem("l0 turn"), 1)
                    for c in range(8):
                        nc.gpsimd.indirect_dma_start(G[k][:, c, :], None, x, bass.IndirectOffsetOnAxis(ap=ST[k][:, 0, c:c + 1], axis=0)).then_inc(sem(f"l0 src landed {k}"), 16)
                    for c in range(8):
                        nc.gpsimd.indirect_dma_start(XG[k][:, c, :], None, x, bass.IndirectOffsetOnAxis(ap=ST[k][:, 1, c:c + 1], axis=0)).then_inc(sem(f"l0 dst landed {k}"), 16)
                    for c in range(8):
                        nc.gpsimd.indirect_dma_start(MG[k][:, c:c + 1], None, where_d, bass.IndirectOffsetOnAxis(ap=ST[k][:, 0, c:c + 1], axis=0)).then_inc(sem(f"l0 where landed {k}"), 16)
                rounds(pool, body)

            @block.sync
            def _(sp):
                def load(i, k):
                    for n, t in enumerate((thi_d, tlo_d)):
                        sp.dma_start(TY[k][:, n, :], t[bass.ds(i * PAIR, PAIR)].rearrange("(o c) -> o c", o=1).broadcast_to([P, PAIR])).then_inc(sem(f"l0 types landed {k}"), 16)
                    load_flags(sp, FL[k], same_prev_d, i, f"l0 flags landed {k}")
                load(0, 0)
                load(1, 1)

                def body(i, r, k):
                    sp.wait_ge(sem("l0 x1"), i + 1)
                    sp.dma_start(edge_rows(ta, i), XD[:, bass.ds(i * 512, 512)]).then_inc(sem("l0 rows written"), 16)
                    if exists(i + 2):
                        load(i + 2, k)
                rounds(sp, body)
                sp.wait_ge(sem("l0 rows written"), 16 * NPAIR)
                sp.wait_ge(sem("tables filled"), 32)

            @block.tensor
            def _(pe):
                def body(i, r, k):
                    pe.wait_ge(sem("l0 h"), 2 * i + 2)
                    for h in range(2):
                        for j in range(4):
                            ins = nc.tensor.transpose(PS[h][:, j * P:(j + 1) * P],
                                                      H[k][:, 2 * j + h, :, :].rearrange("p b d -> p (b d)"), ident[:])
                        ins.then_inc(sem("l0 turned"), 1)
                    for h in range(2):
                        pe.wait_ge(sem("l0 masked"), 8 * i + 4 * h + 4)
                        for m in range(2):
                            for g in range(4):
                                ins = nc.tensor.matmul(PS[2 + 2 * h + m][:], W0S[:, g, 2 * m:2 * m + 2, :].rearrange("p l o -> p (l o)"),
                                                       MASKED[h][g], start=(g == 0), stop=(g == 3))
                        ins.then_inc(sem("l0 products"), 1)
                    for h in range(2):
                        pe.wait_ge(sem("l0 chosen"), 4 * i + 2 * h + 2)
                        for m in range(2):
                            ins = nc.tensor.matmul(PS[6][:], bd[("sumA", "sumB")[h]][:], CHOSEN[h][m],
                                                   start=(h + m == 0), stop=(h + m == 2))
                    ins.then_inc(sem("l0 messages"), 1)
                    pe.wait_ge(sem("l0 scanned"), 4 * i + 4)
                    for j in range(4):
                        ins = nc.tensor.transpose(PS[7][:, j * P:(j + 1) * P], S[:, j * P:(j + 1) * P], ident[:])
                    ins.then_inc(sem("l0 sums back"), 1)
                rounds(pe, body)

            @block.vector
            def _(dve):
                nc.vector.memset(CR[:], 0.0).then_inc(sem("l0 carry clear"), 1)
                dve.wait_ge(sem("l0 src landed 0"), 128)
                ln_sum(dve, G[0][:], 0, "l0", 0)
                ln_var(dve, 0, "l0", 0)
                ln_out(dve, 0, "l0", 0, twice=True)

                def body(i, r, k):
                    nk, nr = 1 - k, r + k
                    dve.wait_ge(sem(f"l0 types landed {k}"), 32 * r + 32)
                    for h in range(2):
                        dve.wait_ge(sem("l0 turned"), 2 * i + h + 1)
                        for g in range(4):
                            nc.vector.scalar_tensor_tensor(out=MASKED[h][g], in0=TY[k][:, 0, h * 512:(h + 1) * 512],
                                                           scalar=col(C_G0 + g), in1=PS[h][:],
                                                           op0=ALU.is_equal, op1=ALU.mult).then_inc(sem("l0 masked"), 1)
                    if exists(i + 1):
                        dve.wait_ge(sem(f"l0 src landed {nk}"), 128 * nr + 128)
                        ln_sum(dve, G[nk][:], nk, "l0", i + 1)
                    for h in range(2):
                        dve.wait_ge(sem("l0 products"), 2 * i + h + 1)
                        for m in range(2):
                            nc.vector.scalar_tensor_tensor(out=CHOSEN[h][m], in0=TY[k][:, 1, h * 512:(h + 1) * 512],
                                                           scalar=col(C_L0 + m), in1=PS[2 + 2 * h + m][:],
                                                           op0=ALU.is_equal, op1=ALU.mult).then_inc(sem("l0 chosen"), 1)
                        if h == 0 and exists(i + 1):
                            ln_var(dve, nk, "l0", i + 1)
                    if exists(i + 1):
                        ln_out(dve, nk, "l0", i + 1, twice=True)
                    dve.wait_ge(sem("l0 messages"), i + 1)
                    dve.wait_ge(sem(f"l0 flags landed {k}"), 32 * r + 32)
                    scan_pair(dve, S, FL[k], PS[6], CR, "l0 scanned", 4 * i)
                    dve.wait_ge(sem("l0 sums back"), i + 1)
                    dve.wait_ge(sem(f"l0 dst landed {k}"), 128 * r + 128)
                    nc.vector.tensor_tensor(rows(XD[:, bass.ds(i * 512, 512)]), rows(PS[7][:]), XG[k][:], ALU.add).then_inc(sem("l0 x1"), 1)
                rounds(dve, body)

        stage_over()

        U = [XG[k][:] for k in range(2)]
        EX = [big[k][:, 0:512] for k in range(2)]
        RU = [big[k][:, 512:1024] for k in range(2)]
        H2 = [big[2 + k][:, 0:512] for k in range(2)]

        def gather_stage(act, i, k, name):
            nc.scalar.activation(ST[k][:, 0, :], IX[:, bass.ds(i * 8, 8)], ACT.Copy).then_inc(sem(name + " staged"), 1)

        def gather(pool, i, k, name, table):
            pool.wait_ge(sem(name + " staged"), i + 1)
            pool.sem_inc(sem(name + " turn"), 1)
            for c in range(8):
                nc.gpsimd.indirect_dma_start(G[k][:, c, :], None, table, bass.IndirectOffsetOnAxis(ap=ST[k][:, 0, c:c + 1], axis=0)).then_inc(sem(f"{name} landed {k}"), 16)

        def turn_rows(pe, k, i, name, out):
            for j in range(4):
                ins = nc.tensor.transpose(out[:, j * P:(j + 1) * P], hrow(k, j), ident[:])
            ins.then_inc(sem(name + " turned"), 1)

        with nc.Block() as block:
            @block.gpsimd
            def _(pool):
                rounds(pool, lambda i, r, k: gather(pool, i, k, "l1", ta))

            @block.sync
            def _(sp):
                load_flags(sp, FL[0], same_prev_d, 0, "l1 flags landed 0")
                load_flags(sp, FL[1], same_prev_d, 1, "l1 flags landed 1")

                def body(i, r, k):
                    if exists(i + 2):
                        sp.wait_ge(sem("l1 scanned"), 4 * i + 4)
                        load_flags(sp, FL[k], same_prev_d, i + 2, f"l1 flags landed {k}")
                rounds(sp, body)

            @block.scalar
            def _(act):
                gather_stage(act, 0, 0, "l1")
                gather_stage(act, 1, 1, "l1")
                ln_square(act, 0, "l1", 0)
                ln_rstd(act, 0, "l1", 0)

                def body(i, r, k):
                    if exists(i + 1):
                        ln_square(act, 1 - k, "l1", i + 1)
                        if exists(i + 2):
                            gather_stage(act, i + 2, k, "l1")
                        ln_rstd(act, 1 - k, "l1", i + 1)
                    act.wait_ge(sem("l1 u"), i + 1)
                    nc.scalar.activation(rows(EX[k]), U[k], ACT.Exp).then_inc(sem("l1 exp"), 1)
                    act.wait_ge(sem("l1 elu"), i + 1)
                    nc.scalar.activation(H2[k], HH[:, bass.ds(i * 512, 512)], ACT.Square).then_inc(sem("l1 squared"), 1)
                rounds(act, body)

            @block.tensor
            def _(pe):
                def total(ps, rhs, first, last):
                    return nc.tensor.matmul(ps[:], ones[:], rhs, start=first, stop=last, skip_group_check=True)
                pe.wait_ge(sem("l1 zeros"), 1)
                total(PS[4], H2[0], True, False)
                total(PS[5], H2[0], True, False).then_inc(sem("l1 sums open"), 1)

                def body(i, r, k):
                    pe.wait_ge(sem("l1 h"), i + 1)
                    turn_rows(pe, k, i, "l1", PS[0])
                    pe.wait_ge(sem("l1 scanned"), 4 * i + 4)
                    for j in range(4):
                        ins = nc.tensor.matmul(PS[1][:, j * P:(j + 1) * P], S[:, j * P:(j + 1) * P], bd["w1"][:], start=True, stop=True)
                    ins.then_inc(sem("l1 products"), 1)
                    last = isinstance(i, int) and i == NPAIR - 1
                    pe.wait_ge(sem("l1 elu"), i + 1)
                    total(PS[4], HH[:, bass.ds(i * 512, 512)], False, last)
                    pe.wait_ge(sem("l1 squared"), i + 1)
                    total(PS[5], H2[k], False, last).then_inc(sem("l1 summed"), 1)
                rounds(pe, body)

            @block.vector
            def _(dve):
                nc.vector.memset(CR[:], 0.0).then_inc(sem("l1 carry clear"), 1)
                nc.vector.memset(H2[0], 0.0).then_inc(sem("l1 zeros"), 1)
                dve.wait_ge(sem("l1 landed 0"), 128)
                ln_sum(dve, G[0][:], 0, "l1", 0)
                ln_var(dve, 0, "l1", 0)
                ln_out(dve, 0, "l1", 0)
                dve.wait_ge(sem("l1 sums open"), 1)

                def body(i, r, k):
                    nk, nr = 1 - k, r + k
                    more = exists(i + 1)
                    if more:
                        dve.wait_ge(sem(f"l1 landed {nk}"), 128 * nr + 128)
                        ln_sum(dve, G[nk][:], nk, "l1", i + 1)
                    dve.wait_ge(sem("l1 turned"), i + 1)
                    dve.wait_ge(sem(f"l1 flags landed {k}"), 32 * r + 32)
                    scan_pair(dve, S, FL[k], PS[0], CR, "l1 scanned", 4 * i)
                    if more:
                        ln_var(dve, nk, "l1", i + 1)
                    dve.wait_ge(sem("l1 products"), i + 1)
                    nc.vector.tensor_tensor(U[k], rows(PS[1][:]), bc8(RCL[:, bass.ds(i * 8, 8)]), ALU.mult).then_inc(sem("l1 u"), 1)
                    if more:
                        ln_out(dve, nk, "l1", i + 1)
                    dve.wait_ge(sem("l1 u"), i + 1)
                    nc.vector.tensor_scalar(rows(RU[k]), U[k], 0.0, -1.0, ALU.max, ALU.add).then_inc(sem("l1 relu"), 1)
                    dve.wait_ge(sem("l1 exp"), i + 1)
                    dve.wait_ge(sem("l1 relu"), i + 1)
                    nc.vector.scalar_tensor_tensor(out=HH[:, bass.ds(i * 512, 512)], in0=EX[k], scalar=1.0, in1=RU[k],
                                                   op0=ALU.min, op1=ALU.add).then_inc(sem("l1 elu"), 1)
                rounds(dve, body)

        gb = big[0][:, 0:128]
        bn = big[1][:, 0:64 * 8]
        with nc.Block() as block:
            @block.sync
            def _(sp):
                sp.dma_start(gb[:, 0:D], gamma.rearrange("(o d) -> o d", o=1).broadcast_to([P, D])).then_inc(sem("bn loaded"), 16)
                sp.dma_start(gb[:, D:2 * D], beta.rearrange("(o d) -> o d", o=1).broadcast_to([P, D])).then_inc(sem("bn loaded"), 16)

                def body(i, r, k):
                    sp.wait_ge(sem("z made"), i + 1)
                    sp.dma_start(edge_rows(ta, i), XD[:, bass.ds(i * 512, 512)]).then_inc(sem("z written"), 16)
                rounds(sp, body)
                sp.wait_ge(sem("z written"), 16 * NPAIR)

            @block.scalar
            def _(act):
                act.wait_ge(sem("bn steps"), 6)
                nc.scalar.activation(bn[:, 320:384], bn[:, 256:320], ACT.Ln, bias=col(C_EPS)).then_inc(sem("bn rstd"), 1)
                act.wait_ge(sem("bn rstd"), 1)
                nc.scalar.activation(bn[:, 384:448], bn[:, 320:384], ACT.Exp, scale=-0.5).then_inc(sem("bn rstd"), 1)

            @block.vector
            def _(dve):
                q = sem("bn steps")
                m, m2, sq, v = (bn[:, n * D:(n + 1) * D] for n in range(4))
                nc.vector.tensor_reduce(m, PS[4][:].rearrange("p (c d) -> p d c", d=D), AX.X, ALU.add).then_inc(q, 1)
                nc.vector.tensor_reduce(m2, PS[5][:].rearrange("p (c d) -> p d c", d=D), AX.X, ALU.add).then_inc(q, 1)
                dve.wait_ge(q, 2)
                nc.vector.tensor_scalar(m, m, 1.0 / N, None, ALU.mult).then_inc(q, 1)
                dve.wait_ge(q, 3)
                nc.vector.tensor_tensor(sq, m, m, ALU.mult).then_inc(q, 1)
                dve.wait_ge(q, 4)
                nc.vector.scalar_tensor_tensor(out=v, in0=m2, scalar=1.0 / N, in1=sq, op0=ALU.mult, op1=ALU.subtract).then_inc(q, 1)
                dve.wait_ge(q, 5)
                nc.vector.tensor_scalar(bn[:, 256:320], v, 0.0, None, ALU.max).then_inc(q, 1)
                dve.wait_ge(sem("bn rstd"), 2)
                dve.wait_ge(sem("bn loaded"), 32)
                nc.vector.tensor_tensor(AB[:], bn[:, 384:448], gb[:, 0:D], ALU.mult).then_inc(q, 1)
                dve.wait_ge(q, 7)
                nc.vector.tensor_tensor(sq, m, AB[:], ALU.mult).then_inc(q, 1)
                dve.wait_ge(q, 8)
                nc.vector.tensor_tensor(CB[:], gb[:, D:2 * D], sq, ALU.subtract).then_inc(q, 1)

                def body(i, r, k):
                    nc.vector.tensor_tensor(Y[k][:], rows(HH[:, bass.ds(i * 512, 512)]), bcd(AB[:]), ALU.mult).then_inc(sem("ah"), 1)
                    dve.wait_ge(sem("ah"), i + 1)
                    xd = rows(XD[:, bass.ds(i * 512, 512)])
                    nc.vector.tensor_tensor(xd, xd, Y[k][:], ALU.add).then_inc(sem("z made"), 1)
                rounds(dve, body)
                dve.wait_ge(q, 9)

        def spread(name):
            stage_over()
            with nc.Block() as block:
                @block.sync
                def _(sp):
                    load_flags(sp, FL[0], same_next_d, NPAIR - 1, name + " flags landed 0")
                    load_flags(sp, FL[1], same_next_d, NPAIR - 2, name + " flags landed 1")

                    def body(i, r, k):
                        if exists(i + 2):
                            down = i * -1 + (NPAIR - 3)
                            sp.wait_ge(sem(name + " spread"), 4 * i + 4)
                            load_flags(sp, FL[k], same_next_d, down, f"{name} flags landed {k}")
                    rounds(sp, body)

                @block.scalar
                def _(act):
                    act.sem_inc(sem(name + " kept"), 2)
                    ln_square(act, 0, name, 0)
                    ln_rstd(act, 0, name, 0)

                    def body(i, r, k):
                        down = i * -1 + (NPAIR - 1)
                        if exists(i + 1):
                            ln_square(act, 1 - k, name, i + 1)
                            ln_rstd(act, 1 - k, name, i + 1)
                        act.wait_ge(sem(name + " spread"), 4 * i + 4)
                        nc.scalar.activation(HH[:, bass.ds(down * 512, 512)], big[k][:, 0:512], ACT.Copy).then_inc(sem(name + " kept"), 1)
                    rounds(act, body)

                @block.tensor
                def _(pe):
                    def body(i, r, k):
                        pe.wait_ge(sem(name + " h"), i + 1)
                        turn_rows(pe, k, i, name, PS[k])
                    rounds(pe, body)

                @block.vector
                def _(dve):
                    def normed(i, k, last):
                        dve.wait_ge(sem(name + " rstd"), i + 1)
                        nc.vector.tensor_tensor(SM[k][:, 3, :], SM[k][:, 3, :], LASTF[:, bass.ds(last, 8)], ALU.mult).then_inc(sem(name + " last"), 1)
                        dve.wait_ge(sem(name + " last"), i + 1)
                        ln_out(dve, k, name, i)
                    nc.vector.memset(CR[:], 0.0).then_inc(sem(name + " carry clear"), 1)
                    ln_sum(dve, rows(XD[:, (NPAIR - 1) * 512:NPAIR * 512]), 0, name, 0, bias=True)
                    ln_var(dve, 0, name, 0)
                    normed(0, 0, (NPAIR - 1) * 8)
                    dve.wait_ge(sem(name + " carry clear"), 1)

                    def body(i, r, k):
                        nk = 1 - k
                        more = exists(i + 1)
                        down = i * -1 + (NPAIR - 1)
                        if more:
                            ln_sum(dve, rows(XD[:, bass.ds((down - 1) * 512, 512)]), nk, name, i + 1, bias=True)
                        dve.wait_ge(sem(name + " turned"), i + 1)
                        dve.wait_ge(sem(f"{name} flags landed {k}"), 32 * r + 32)
                        dve.wait_ge(sem(name + " kept"), i + 1)
                        for n, h in enumerate((1, 0)):
                            q = slice(h * D, (h + 1) * D)
                            o = slice((1 - h) * D, (2 - h) * D)
                            out = big[k][q, 0:512]
                            nc.vector.tensor_tensor_scan(out[:, ::-1], FL[k][q, ::-1], PS[k][q, ::-1], CR[q, 0:1], ALU.mult, ALU.add).then_inc(sem(name + " spread"), 1)
                            dve.wait_ge(sem(name + " spread"), 4 * i + 2 * n + 1)
                            nc.vector.tensor_copy(CR[o, 0:1], out[:, 0:1]).then_inc(sem(name + " spread"), 1)
                            dve.wait_ge(sem(name + " spread"), 4 * i + 2 * n + 2)
                            if n == 0 and more:
                                ln_var(dve, nk, name, i + 1)
                        if more:
                            normed(i + 1, nk, (down - 1) * 8)
                    rounds(dve, body)
        spread("s2")

        stage_over()

        HS = sb("HS", [P, 512])
        X = SQ[0][:].rearrange("p c d -> p (c d)")
        XA, XB = big[0][:, 0:512], big[0][:, 512:1024]
        EE = big[1][:, 0:512]
        QU, WW = big[1][:, 512:1024], big[2][:, 0:512]
        LQ = big[2][:, 512:1024]
        LG = big[3][:, 0:512]
        LIM = big[3][:, 512:1024]
        DIF = big[4]
        AW = big[5]
        VV = big[6][:, 0:512]
        MX = sb("MX", [P, 513])
        SS = big[7][:].rearrange("p (n c) -> p n c", n=2)
        MSG = XG
        with nc.Block() as block:
            @block.gpsimd
            def _(pool):
                rounds(pool, lambda i, r, k: gather(pool, i, k, "l2", ta))

            @block.sync
            def _(sp):
                load_flags(sp, FL[0], same_prev_d, 0, "l2 flags landed 0")
                load_flags(sp, FL[1], same_prev_d, 1, "l2 flags landed 1")

                def body(i, r, k):
                    sp.wait_ge(sem("l2 z"), i + 1)
                    sp.dma_start(edge_rows(tb, i), XD[:, bass.ds(i * 512, 512)]).then_inc(sem("l2 rows written"), 16)
                    if exists(i + 2):
                        load_flags(sp, FL[k], same_prev_d, i + 2, f"l2 flags landed {k}")
                rounds(sp, body)
                sp.wait_ge(sem("l2 rows written"), 16 * NPAIR)

            @block.scalar
            def _(act):
                gather_stage(act, 0, 0, "l2")
                gather_stage(act, 1, 1, "l2")
                ln_square(act, 0, "l2", 0)
                ln_rstd(act, 0, "l2", 0)

                def body(i, r, k):
                    act.wait_ge(sem("l2 turned"), i + 1)
                    nc.scalar.activation(HS[:], PS[0][:], ACT.Copy).then_inc(sem("l2 hs"), 1)
                    act.wait_ge(sem(f"l2 flags landed {k}"), 32 * r + 32)
                    nc.scalar.activation(LIM, FL[k][:], ACT.Identity, scale=2 * LIMIT, bias=col(C_NLIM)).then_inc(sem("l2 lim"), 1)
                    act.wait_ge(sem("l2 products"), i + 1)
                    nc.scalar.activation(XA, PS[1][:], ACT.Identity, bias=col(C_ATT)).then_inc(sem("l2 pre"), 1)
                    nc.scalar.activation(EE, PS[2][:], ACT.Identity, bias=col(C_WEB)).then_inc(sem("l2 edges"), 1)
                    act.wait_ge(sem("l2 cut"), i + 1)
                    nc.scalar.activation(XB, XB, ACT.Exp).then_inc(sem("l2 u"), 1)
                    act.wait_ge(sem("l2 q"), i + 1)
                    nc.scalar.activation(LQ, QU, ACT.Ln, bias=col(C_TWO)).then_inc(sem("l2 log q"), 1)
                    act.wait_ge(sem("l2 log q"), i + 1)
                    nc.scalar.activation(LQ, LQ, ACT.Exp, scale=-1.0).then_inc(sem("l2 inverse"), 1)
                    if exists(i + 1):
                        ln_square(act, 1 - k, "l2", i + 1)
                        if exists(i + 2):
                            gather_stage(act, i + 2, k, "l2")
                        ln_rstd(act, 1 - k, "l2", i + 1)
                    act.wait_ge(sem("l2 logits"), i + 1)
                    nc.scalar.activation(LG, PS[3][:], ACT.Identity, bias=col(C_WAB)).then_inc(sem("l2 lg"), 1)
                    act.wait_ge(sem("l2 dif"), 2 * i + 2)
                    nc.scalar.activation(AW[:], DIF[:], ACT.Exp).then_inc(sem("l2 weights"), 1)
                rounds(act, body)

            @block.tensor
            def _(pe):
                def body(i, r, k):
                    pe.wait_ge(sem("l2 h"), i + 1)
                    turn_rows(pe, k, i, "l2", PS[0])
                    hd = HH[:, bass.ds(i * 512, 512)]
                    nc.tensor.matmul(PS[1][:], bd["wr"][:], hd, start=True, stop=False)
                    pe.wait_ge(sem("l2 hs"), i + 1)
                    nc.tensor.matmul(PS[1][:], bd["wews"][:], HS[:], start=False, stop=True)
                    nc.tensor.matmul(PS[2][:], bd["we"][:], HS[:], start=True, stop=True).then_inc(sem("l2 products"), 1)
                    pe.wait_ge(sem("l2 mish"), i + 1)
                    nc.tensor.matmul(PS[3][:], bd["wa"][:], XB, start=True, stop=True).then_inc(sem("l2 logits"), 1)
                    pe.wait_ge(sem("l2 summed"), 4 * i + 4)
                    for j in range(4):
                        nc.tensor.transpose(PS[4][:, j * P:(j + 1) * P], SS[:, 0, j * P:(j + 1) * P], ident[:])
                    for j in range(4):
                        ins = nc.tensor.matmul(PS[5][:, 2 * j:2 * j + 2], SS[:, 1, j * P:(j + 1) * P], sel[:], start=True, stop=True)
                    ins.then_inc(sem("l2 back"), 1)
                rounds(pe, body)

            @block.vector
            def _(dve):
                nc.vector.memset(CR[:], 0.0).then_inc(sem("l2 clear"), 1)
                nc.vector.memset(MX[:, 512:513], -LIMIT).then_inc(sem("l2 clear"), 1)
                dve.wait_ge(sem("l2 landed 0"), 128)
                ln_sum(dve, G[0][:], 0, "l2", 0, bias=True)
                ln_var(dve, 0, "l2", 0)
                ln_out(dve, 0, "l2", 0)
                dve.wait_ge(sem("l2 clear"), 2)

                def body(i, r, k):
                    nk, nr = 1 - k, r + k
                    more = exists(i + 1)
                    dve.wait_ge(sem("l2 pre"), i + 1)
                    nc.vector.tensor_scalar(XB, XA, 20.0, None, ALU.min).then_inc(sem("l2 cut"), 1)
                    if more:
                        dve.wait_ge(sem(f"l2 landed {nk}"), 128 * nr + 128)
                        ln_sum(dve, G[nk][:], nk, "l2", i + 1, bias=True)
                    dve.wait_ge(sem("l2 u"), i + 1)
                    nc.vector.scalar_tensor_tensor(out=QU, in0=XB, scalar=2.0, in1=XB, op0=ALU.add, op1=ALU.mult).then_inc(sem("l2 q"), 1)
                    dve.wait_ge(sem("l2 q"), i + 1)
                    nc.vector.tensor_tensor(WW, QU, XA, ALU.mult).then_inc(sem("l2 qx"), 1)
                    if more:
                        ln_var(dve, nk, "l2", i + 1)
                    dve.wait_ge(sem("l2 inverse"), i + 1)
                    dve.wait_ge(sem("l2 qx"), i + 1)
                    nc.vector.tensor_tensor(XB, WW, LQ, ALU.mult).then_inc(sem("l2 mish"), 1)
                    if more:
                        ln_out(dve, nk, "l2", i + 1)
                    dve.wait_ge(sem("l2 lg"), i + 1)
                    dve.wait_ge(sem("l2 lim"), i + 1)
                    mx = sem("l2 max")
                    for h in range(2):
                        q = slice(h * D, (h + 1) * D)
                        o = slice((1 - h) * D, (2 - h) * D)
                        nc.vector.tensor_copy(MX[q, 0:1], MX[o, 512:513]).then_inc(mx, 1)
                        dve.wait_ge(mx, 4 * i + 2 * h + 1)
                        nc.vector.tensor_tensor_scan(MX[q, 1:513], LIM[q, :], LG[q, :], MX[q, 0:1], ALU.min, ALU.max).then_inc(mx, 1)
                        dve.wait_ge(mx, 4 * i + 2 * h + 2)
                    nc.vector.tensor_tensor(VV, MX[:, 0:512], LIM, ALU.min).then_inc(sem("l2 before"), 1)
                    nc.vector.tensor_tensor(DIF[:, 512:1024], LG, MX[:, 1:513], ALU.subtract).then_inc(sem("l2 dif"), 1)
                    dve.wait_ge(sem("l2 before"), i + 1)
                    nc.vector.tensor_tensor(DIF[:, 0:512], VV, MX[:, 1:513], ALU.subtract).then_inc(sem("l2 dif"), 1)
                    dve.wait_ge(sem("l2 weights"), i + 1)
                    nc.vector.tensor_tensor(VV, AW[:, 512:1024], EE, ALU.mult).then_inc(sem("l2 weighted"), 1)
                    dve.wait_ge(sem("l2 weighted"), i + 1)
                    for h in range(2):
                        q = slice(h * D, (h + 1) * D)
                        o = slice((1 - h) * D, (2 - h) * D)
                        for n, v in enumerate((VV, AW[:, 512:1024])):
                            nc.vector.tensor_tensor_scan(SS[q, n, :], AW[q, 0:512], v[q, :], CR[q, n:n + 1], ALU.mult, ALU.add).then_inc(sem("l2 summed"), 1)
                        dve.wait_ge(sem("l2 summed"), 4 * i + 2 * h + 2)
                        nc.vector.tensor_copy(CR[o, :], SS[q, :, 511]).then_inc(sem("l2 carried"), 1)
                        dve.wait_ge(sem("l2 carried"), 2 * i + h + 1)
                    dve.wait_ge(sem("l2 back"), i + 1)
                    nc.vector.reciprocal(SM[k][:, 0, :], PS[5][:, 0:8]).then_inc(sem("l2 rden"), 1)
                    dve.wait_ge(sem("l2 rden"), i + 1)
                    nc.vector.tensor_tensor(MSG[k][:], rows(PS[4][:]), bc8(SM[k][:, 0, :]), ALU.mult).then_inc(sem("l2 msg"), 1)
                    dve.wait_ge(sem("l2 msg"), i + 1)
                    xd = rows(XD[:, bass.ds(i * 512, 512)])
                    nc.vector.tensor_tensor(xd, xd, MSG[k][:], ALU.add).then_inc(sem("l2 z"), 1)
                    dve.wait_ge(sem("l2 z"), i + 1)
                rounds(dve, body)

        spread("s3")

        OT = HS

        def gru_tensor(pe, i, name, into, h, w, width=512, parts=P, back=0):
            c = slice(0, width)
            if into is None:
                for ps, b, s in ((4, w[0], "z"), (5, w[1], "r"), (6, bd["hn"], "hn")):
                    ins = nc.tensor.matmul(PS[ps][:, c], b[:], h, start=True, stop=True)
                ins.then_inc(sem(name + " gates"), 1)
            else:
                nc.tensor.matmul(PS[6][:, c], bd["hn"][:], h, start=True, stop=True)
                nc.tensor.matmul(PS[4][:, c], bd["hz"][:], h, start=True, stop=False)
                nc.tensor.matmul(PS[5][:, c], bd["hr"][:], h, start=True, stop=False)
                pe.wait_ge(sem(name + " out"), i + 1)
                nc.tensor.matmul(PS[5][:, c], w[1][:], into, start=False, stop=True)
                nc.tensor.matmul(PS[4][:, c], w[0][:], into, start=False, stop=True).then_inc(sem(name + " gates"), 1)
            nc.tensor.matmul(PS[7][:, c], w[2][:], h if into is None else into, start=True, stop=False)
            pe.wait_ge(sem(name + " rh"), i + 1)
            nc.tensor.matmul(PS[7][:, c], ident[:], RH[:, c], start=False, stop=True).then_inc(sem(name + " n sum"), 1)
            pe.wait_ge(sem(name + " f"), i + 1)
            for j in range(4):
                ins = nc.tensor.transpose(PS[back][0:parts, j * P:(j + 1) * P], FF[:, j * parts:(j + 1) * parts], ident[:])
            ins.then_inc(sem(name + " back"), 1)

        def gru_scalar(act, i, name, cz, cr, cn, width=512):
            c = slice(0, width)
            act.wait_ge(sem(name + " gates"), i + 1)
            nc.scalar.activation(ZR[:, 0:width], PS[4][:, c], ACT.Sigmoid, bias=col(cz)).then_inc(sem(name + " sz"), 1)
            nc.scalar.activation(ZR[:, 512:512 + width], PS[5][:, c], ACT.Sigmoid, bias=col(cr)).then_inc(sem(name + " sr"), 1)
            act.wait_ge(sem(name + " n sum"), i + 1)
            nc.scalar.activation(NT[:, c], PS[7][:, c], ACT.Tanh, bias=col(cn)).then_inc(sem(name + " n"), 1)

        def gru_vector_rh(dve, i, name, width=512):
            c = slice(0, width)
            dve.wait_ge(sem(name + " sr"), i + 1)
            nc.vector.scalar_tensor_tensor(out=RH[:, c], in0=PS[6][:, c], scalar=col(C_HN), in1=ZR[:, 512:512 + width],
                                           op0=ALU.add, op1=ALU.mult).then_inc(sem(name + " rh"), 1)

        def gru_vector_f(dve, i, name, h, width=512):
            c = slice(0, width)
            dve.wait_ge(sem(name + " n"), i + 1)
            nc.vector.tensor_tensor(FF[:, c], h, NT[:, c], ALU.subtract).then_inc(sem(name + " h - n"), 1)
            dve.wait_ge(sem(name + " h - n"), i + 1)
            nc.vector.tensor_tensor(FF[:, c], FF[:, c], ZR[:, 0:width], ALU.mult).then_inc(sem(name + " z(h - n)"), 1)
            dve.wait_ge(sem(name + " z(h - n)"), i + 1)
            nc.vector.tensor_tensor(FF[:, c], FF[:, c], NT[:, c], ALU.add).then_inc(sem(name + " f"), 1)

        ZR, RH, NT = big[7], S, MX[:, 0:512]
        FF = TY[0][:, 1, :].bitcast(F32)

        DU = UNITS // 2
        DP = 125
        OD = [XG[k][0:DP] for k in range(2)]
        x_u = x.rearrange("(u p c) d -> p u (c d)", p=DP, c=8)
        out_u = out.rearrange("(u p c) d -> p u (c d)", p=DP, c=8)
        HT = big[0][:, 0:500]
        with nc.Block() as block:
            def units(eng, body):
                with eng.Fori(0, DU - 1) as r:
                    body(2 * r, r, 0)
                    body(2 * r + 1, r, 1)
                body(UNITS - 2, DU - 1, 0)
                body(UNITS - 1, DU - 1, 1)

            def unit_exists(i):
                return not isinstance(i, int) or i < UNITS

            @block.sync
            def _(sp):
                def load(i, k):
                    sp.dma_start(G[k][0:DP].rearrange("p c d -> p (c d)"), x_u[:, bass.ds(i, 1), :].rearrange("p a c -> p (a c)")).then_inc(sem(f"d landed {k}"), 16)
                load(0, 0)
                load(1, 1)

                def body(i, r, k):
                    sp.wait_ge(sem("d o"), i + 1)
                    sp.dma_start(out_u[:, bass.ds(i, 1), :].rearrange("p a c -> p (a c)"), OD[k].rearrange("p c d -> p (c d)")).then_inc(sem(f"d written {k}"), 16)
                    if not isinstance(i, int):
                        load(i + 2, k)
                units(sp, body)
                for k in range(2):
                    sp.wait_ge(sem(f"d written {k}"), 16 * DU)

            @block.scalar
            def _(act):
                for i in range(1):
                    ln_square(act, 0, "d", 0)
                    ln_rstd(act, 0, "d", 0)

                def body(i, r, k):
                    act.wait_ge(sem("d turned"), i + 1)
                    nc.scalar.activation(HT, PS[1][:, 0:500], ACT.Copy).then_inc(sem("d ht"), 1)
                    if unit_exists(i + 1):
                        ln_square(act, 1 - k, "d", i + 1)
                    gru_scalar(act, i, "d", C_DZ, C_DR, C_DIN, 500)
                    if unit_exists(i + 1):
                        ln_rstd(act, 1 - k, "d", i + 1)
                units(act, body)

            @block.tensor
            def _(pe):
                def body(i, r, k):
                    pe.wait_ge(sem("d h"), i + 1)
                    for j in range(4):
                        ins = nc.tensor.transpose(PS[1][:, j * DP:(j + 1) * DP], hrow(k, j)[0:DP, :], ident[0:DP, 0:DP])
                    ins.then_inc(sem("d turned"), 1)
                    pe.wait_ge(sem("d ht"), i + 1)
                    gru_tensor(pe, i, "d", None, HT, (bd["dz"], bd["dr"], bd["din"]), 500, DP)
                units(pe, body)

            @block.vector
            def _(dve):
                def norm_sum(i, k, r):
                    dve.wait_ge(sem(f"d landed {k}"), 16 * r + 16)
                    ln_sum(dve, G[k][:], k, "d", i, bias=True)
                norm_sum(0, 0, 0)
                ln_var(dve, 0, "d", 0)
                ln_out(dve, 0, "d", 0)

                def body(i, r, k):
                    nk, nr = 1 - k, r + k
                    more = unit_exists(i + 1)
                    if more:
                        norm_sum(i + 1, nk, nr)
                    gru_vector_rh(dve, i, "d", 500)
                    if more:
                        ln_var(dve, nk, "d", i + 1)
                    gru_vector_f(dve, i, "d", HT, 500)
                    if more:
                        ln_out(dve, nk, "d", i + 1)
                    dve.wait_ge(sem("d back"), i + 1)
                    nc.vector.tensor_tensor(OD[k], rows(PS[0][:])[0:DP], Y[k][0:DP], ALU.add).then_inc(sem("d o"), 1)
                units(dve, body)

        stage_over()

        TT, V1, V2, LIMD, S1, S2, MM = (big[n] for n in range(7))
        ZZ = big[0]
        FD = TY[0][:, 0, :]
        EW = W0S[:].rearrange("p a b d -> p (a b d)")
        RC = TY[1][:].rearrange("p a b -> p (a b)").bitcast(F32)
        SC = sb("SC", [P, 1024])
        AT = [H[k][0:4].rearrange("p a b d -> p (a b d)")[:, 512:1024] for k in range(2)]
        SCT = sb("SCT", [P, 8], I32)
        VAR = S1[D:P, :]
        ROW = [XG[k] for k in range(2)]
        with nc.Block() as block:
            @block.gpsimd
            def _(pool):
                pool.sem_inc(sem("l3 rows free"), 2)
                gather(pool, 0, 0, "l3", tb)
                gather(pool, 1, 1, "l3", tb)

                def body(i, r, k):
                    nc.gpsimd.tensor_copy(SCT[:], LI[:, bass.ds(i, 1), 2, :].rearrange("p a c -> p (a c)")).then_inc(sem("l3 dst staged"), 1)
                    pool.wait_ge(sem("l3 dst staged"), i + 1)
                    pool.wait_ge(sem("l3 rows"), i + 1)
                    pool.sem_inc(sem("l3 out turn"), 1)
                    for c in range(8):
                        nc.gpsimd.indirect_dma_start(out, bass.IndirectOffsetOnAxis(ap=SCT[:, c:c + 1], axis=0), ROW[k][:, c, :], None,
                                                     bounds_check=N - 1, oob_is_err=False).then_inc(sem(f"l3 written {k}"), 16)
                    pool.wait_ge(sem(f"l3 written {k}"), 128 * r + 128)
                    pool.sem_inc(sem("l3 rows free"), 1)
                    if exists(i + 2):
                        gather(pool, i + 2, k, "l3", tb)
                rounds(pool, body)

            @block.sync
            def _(sp):
                def spread_line(t, d, i, name):
                    sp.dma_start(t, d[bass.ds(i * PAIR, PAIR)].rearrange("(o c) -> o c", o=1).broadcast_to([t.shape[0], PAIR])).then_inc(sem(name), 16)

                def load_a(i):
                    spread_line(EW, ew_d, i, "l3 ew landed")
                    for h in range(2):
                        sp.dma_start(AT[h], comp_d[:, bass.ds(i * PAIR + h * HALF, HALF)]).then_inc(sem("l3 attr landed"), 16)

                def load_b(i):
                    spread_line(RC, rcnt_d, i, "l3 rcnt landed")
                    spread_line(FD, same_prev_d, i, "l3 flags landed")

                def load_c(i):
                    spread_line(SC[0:D, :], amp_d, i, "l3 scalers landed")
                    spread_line(SC[D:P, :], att_amp_d, i, "l3 scalers landed")
                load_a(0)
                load_b(0)
                load_c(0)

                def body(i, r, k):
                    if exists(i + 1):
                        sp.wait_ge(sem("l3 t"), 2 * i + 2)
                        load_a(i + 1)
                        sp.wait_ge(sem("l3 mean"), i + 1)
                        load_b(i + 1)
                        sp.wait_ge(sem("l3 scaled"), 2 * i + 2)
                        load_c(i + 1)
                rounds(sp, body)

            @block.scalar
            def _(act):
                gather_stage(act, 0, 0, "l3")
                gather_stage(act, 1, 1, "l3")
                ln_square(act, 0, "l3", 0)
                ln_rstd(act, 0, "l3", 0)

                def body(i, r, k):
                    act.wait_ge(sem("l3 turned"), i + 1)
                    nc.scalar.activation(HS[:], PS[0][:], ACT.Copy).then_inc(sem("l3 hs"), 1)
                    act.wait_ge(sem("l3 flags landed"), 16 * i + 16)
                    nc.scalar.activation(LIMD[:], FD, ACT.Identity, scale=2 * LIMIT, bias=col(C_NLIM)).then_inc(sem("l3 lim"), 1)
                    act.wait_ge(sem("l3 t"), 2 * i + 2)
                    nc.scalar.activation(V1[0:D, :], TT[0:D, :], ACT.Identity, bias=col(C_PRE, 0, D)).then_inc(sem("l3 v1"), 1)
                    nc.scalar.activation(V1[D:P, :], TT[D:P, :], ACT.Square, bias=col(C_PRE, D, P)).then_inc(sem("l3 v1"), 1)
                    nc.scalar.activation(V2[:], TT[:], ACT.Identity, scale=col(C_SGN), bias=col(C_SPRE)).then_inc(sem("l3 v2"), 1)
                    if exists(i + 1):
                        ln_square(act, 1 - k, "l3", i + 1)
                        if exists(i + 2):
                            gather_stage(act, i + 2, k, "l3")
                    act.wait_ge(sem("l3 mean"), i + 1)
                    nc.scalar.activation(VAR, MM[0:D, :], ACT.Square).then_inc(sem("l3 mean squared"), 1)
                    act.wait_ge(sem("l3 variance"), i + 1)
                    nc.scalar.activation(VAR, VAR, ACT.Relu).then_inc(sem("l3 var relu"), 1)
                    act.wait_ge(sem("l3 var relu"), i + 1)
                    nc.scalar.activation(VAR, VAR, ACT.Ln, bias=col(C_EPS, D, P)).then_inc(sem("l3 var log"), 1)
                    act.wait_ge(sem("l3 var log"), i + 1)
                    nc.scalar.activation(MM[D:P, :], VAR, ACT.Exp, scale=0.5).then_inc(sem("l3 std"), 1)
                    act.wait_ge(sem("l3 total"), i + 1)
                    nc.scalar.activation(OT[:], PS[3][:], ACT.Identity, bias=col(C_POST)).then_inc(sem("l3 out"), 1)
                    gru_scalar(act, i, "l3", C_Z, C_R, C_IN)
                    if exists(i + 1):
                        ln_rstd(act, 1 - k, "l3", i + 1)
                rounds(act, body)

            @block.tensor
            def _(pe):
                def body(i, r, k):
                    pe.wait_ge(sem("l3 h"), i + 1)
                    turn_rows(pe, k, i, "l3", PS[0])
                    hd = HH[:, bass.ds(i * 512, 512)]
                    pe.wait_ge(sem("l3 attr landed"), 32 * i + 32)
                    for h in range(2):
                        nc.tensor.matmul(PS[1 + h][:], attw[:], AT[h], start=True, stop=False)
                        nc.tensor.matmul(PS[1 + h][:], bd[("hdA", "hdB")[h]][:], hd, start=False, stop=False)
                    pe.wait_ge(sem("l3 hs"), i + 1)
                    for h in range(2):
                        nc.tensor.matmul(PS[1 + h][:], bd[("hsA", "hsB")[h]][:], HS[:], start=False, stop=True).then_inc(sem("l3 raw"), 1)
                    nc.tensor.matmul(PS[3][:], bd["u0"][:], hd, start=True, stop=False)
                    pe.wait_ge(sem("l3 std"), i + 1)
                    for h in range(2):
                        c = slice(h * 512, (h + 1) * 512)
                        nc.tensor.matmul(PS[1 + h][:], bd["mq"][:], MM[:, c], start=True, stop=False)
                        nc.tensor.matmul(PS[1 + h][:], bd["xq"][:], S2[:, c], start=False, stop=True).then_inc(sem("l3 q"), 1)
                    for h in range(2):
                        c = slice(h * 512, (h + 1) * 512)
                        nc.tensor.matmul(PS[3][:], bd[("mmA", "mmB")[h]][:], MM[:, c], start=False, stop=False)
                        nc.tensor.matmul(PS[3][:], bd[("xxA", "xxB")[h]][:], S2[:, c], start=False, stop=False)
                    for h in range(2):
                        pe.wait_ge(sem("l3 scaled"), 2 * i + h + 1)
                        ins = nc.tensor.matmul(PS[3][:], bd[("sumA", "sumB")[h]][:], ZZ[:, h * 512:(h + 1) * 512], start=False, stop=(h == 1))
                    ins.then_inc(sem("l3 total"), 1)
                    gru_tensor(pe, i, "l3", OT[:], hd, (bd["z"], bd["r"], bd["in"]), back=4)
                rounds(pe, body)

            @block.vector
            def _(dve):
                nc.vector.memset(CR[:, 0:1], 0.0).then_inc(sem("l3 clear"), 1)
                nc.vector.memset(CR[:, 1:2], -LIMIT).then_inc(sem("l3 clear"), 1)
                dve.wait_ge(sem("l3 landed 0"), 128)
                ln_sum(dve, G[0][:], 0, "l3", 0, bias=True)
                ln_var(dve, 0, "l3", 0)
                ln_out(dve, 0, "l3", 0)
                dve.wait_ge(sem("l3 clear"), 2)

                def body(i, r, k):
                    nk, nr = 1 - k, r + k
                    more = exists(i + 1)
                    dve.wait_ge(sem("l3 ew landed"), 16 * i + 16)
                    for h in range(2):
                        dve.wait_ge(sem("l3 raw"), 2 * i + h + 1)
                        c = slice(h * 512, (h + 1) * 512)
                        nc.vector.tensor_tensor(TT[:, c], PS[1 + h][:], EW[:, c], ALU.mult).then_inc(sem("l3 t"), 1)
                    if more:
                        dve.wait_ge(sem(f"l3 landed {nk}"), 128 * nr + 128)
                        ln_sum(dve, G[nk][:], nk, "l3", i + 1, bias=True)
                    dve.wait_ge(sem("l3 v1"), 2 * i + 2)
                    dve.wait_ge(sem("l3 flags landed"), 16 * i + 16)
                    nc.vector.tensor_tensor_scan(S1[:], FD, V1[:], CR[:, 0:1], ALU.mult, ALU.add).then_inc(sem("l3 sums"), 1)
                    dve.wait_ge(sem("l3 v2"), i + 1)
                    dve.wait_ge(sem("l3 lim"), i + 1)
                    nc.vector.tensor_tensor_scan(S2[:], LIMD[:], V2[:], CR[:, 1:2], ALU.min, ALU.max).then_inc(sem("l3 maxima"), 1)
                    dve.wait_ge(sem("l3 sums"), i + 1)
                    dve.wait_ge(sem("l3 rcnt landed"), 16 * i + 16)
                    nc.vector.tensor_copy(CR[:, 0:1], S1[:, 1023:1024]).then_inc(sem("l3 carried"), 1)
                    nc.vector.tensor_tensor(MM[:], S1[:], RC, ALU.mult).then_inc(sem("l3 mean"), 1)
                    dve.wait_ge(sem("l3 maxima"), i + 1)
                    nc.vector.tensor_copy(CR[:, 1:2], S2[:, 1023:1024]).then_inc(sem("l3 carried"), 1)
                    if more:
                        ln_var(dve, nk, "l3", i + 1)
                    dve.wait_ge(sem("l3 mean squared"), i + 1)
                    nc.vector.tensor_tensor(VAR, MM[D:P, :], VAR, ALU.subtract).then_inc(sem("l3 variance"), 1)
                    dve.wait_ge(sem("l3 scalers landed"), 32 * i + 32)
                    for h in range(2):
                        dve.wait_ge(sem("l3 q"), 2 * i + h + 1)
                        c = slice(h * 512, (h + 1) * 512)
                        nc.vector.tensor_tensor(ZZ[:, c], PS[1 + h][:], SC[:, c], ALU.mult).then_inc(sem("l3 scaled"), 1)
                    gru_vector_rh(dve, i, "l3")
                    gru_vector_f(dve, i, "l3", HH[:, bass.ds(i * 512, 512)])
                    if more:
                        ln_out(dve, nk, "l3", i + 1)
                    dve.wait_ge(sem("l3 back"), i + 1)
                    dve.wait_ge(sem("l3 rows free"), i + 1)
                    nc.vector.tensor_tensor(ROW[k][:], rows(PS[4][:]), rows(XD[:, bass.ds(i * 512, 512)]), ALU.add).then_inc(sem("l3 row sums"), 1)
                    dve.wait_ge(sem("l3 row sums"), i + 1)
                    nc.vector.tensor_tensor(ROW[k][:], ROW[k][:], bcd(CB[:]), ALU.add).then_inc(sem("l3 rows"), 1)
                    dve.wait_ge(sem("l3 carried"), 2 * i + 2)
                rounds(dve, body)
        stage_over()


_INS = ['x', 'src', 'dst', 'edge_attr_4', 'edge_type_32', 'node_vec', 'L0_gnn_weight', 'L1_gnn_W', 'L1_gnn_gamma',
        'L1_gnn_beta', 'L2_gnn_We_k', 'L2_gnn_We_b', 'L2_gnn_Ws_k', 'L2_gnn_Ws_b', 'L2_gnn_Wr_k', 'L2_gnn_Wr_b',
        'L2_gnn_Wa_k', 'L2_gnn_Wa_b', 'L3_gnn_W', 'L3_gnn_We', 'L3_gnn_be', 'L3_gnn_Wpre', 'L3_gnn_bpre',
        'L3_gnn_Wpost', 'L3_gnn_bpost', 'L3_gnn_Wih', 'L3_gnn_bih', 'L3_gnn_Whh', 'L3_gnn_bhh']
_OUTS = [((50000, 64), 'float32')]


def kernel(**inputs):
    import numpy as _np
    import concourse.bacc as _bacc
    from concourse import mybir as _mybir
    from concourse.bass_utils import run_bass_kernel_spmd as _run

    nc = _bacc.Bacc("TRN2", target_bir_lowering=False, num_devices=1)
    arrays, args = {}, []
    for name in _INS:
        a = _np.ascontiguousarray(inputs[name])
        arrays[f"in_{name}_dram"] = a
        args.append(nc.dram_tensor(f"in_{name}_dram", a.shape, _mybir.dt.from_np(a.dtype), kind="ExternalInput").ap())
    for i, (shape, dtype) in enumerate(_OUTS):
        dt = _mybir.dt.from_np(_np.dtype(dtype))
        args.append(nc.dram_tensor(f"out_{i}_dram", shape, dt, kind="ExternalOutput").ap())
    gnn_kernel(nc, *args)
    r = _run(nc, [arrays], core_ids=[0])
    got = tuple(r.results[0][f"out_{i}_dram"] for i in range(len(_OUTS)))
    return got[0]
```

```python
from contextlib import ExitStack

import concourse.bass as bass
from concourse import mybir

F32 = mybir.dt.float32
BF16 = mybir.dt.bfloat16
I32 = mybir.dt.int32
ALU = mybir.AluOpType
ACT = mybir.ActivationFunctionType
AX = mybir.AxisListType

P = 128
D = 64
EPS = 1e-5
LIMIT = 1e38
FAR = float(1 << 20)


def gnn_kernel(nc, x, src, dst, attr, etype, node_vec, w0, w1, gamma, beta,
               we_k, we_b, ws_k, ws_b, wr_k, wr_b, wa_k, wa_b,
               w3, w3e, b3e, wpre, bpre, wpost, bpost, wih, bih, whh, bhh, out, debug=None):
    N = x.shape[0]
    E = src.shape[0]
    PAIR = 8 * P
    HALF = PAIR // 2
    NPAIR = -(-E // PAIR)
    EP = NPAIR * PAIR
    RQ = EP // 256
    NREL = w0.shape[0]
    assert NPAIR % 2 == 1 and NREL == 32 and N % 1000 == 0 and RQ <= P
    UNITS = N // 1000
    ROUNDS = (NPAIR - 3) // 2

    with ExitStack() as ctx:
        def sb(name, shape, dt=F32):
            return ctx.enter_context(nc.sbuf_tensor(name, shape, dt))

        def dram(name, shape, dt=F32):
            return nc.dram_tensor(name, shape, dt).ap()

        sems = {}

        def sem(name):
            if name not in sems:
                sems[name] = nc.alloc_semaphore(name=name.replace(" ", "_"))
            return sems[name]

        def stage_over():
            nc.clear_and_free_semaphores(list(sems.values()))
            sems.clear()
            nc.all_engine_barrier()

        def load_log_exp(act):
            nc.scalar.preload_act_table_set("natural_log_exp_and_others")

        def rounds(eng, body):
            with eng.Fori(0, ROUNDS) as r:
                body(2 * r, r, 0)
                body(2 * r + 1, r, 1)
            for i in range(2 * ROUNDS, NPAIR):
                body(i, i // 2, i % 2)

        def exists(i):
            return not isinstance(i, int) or i < NPAIR

        src_d = dram("src_d", (EP,), I32)
        dst_d = dram("dst_d", (EP + 2,), I32)
        typ_d = dram("typ_d", (EP,), I32)
        att_d = dram("att_d", (EP, 4))
        same_prev_d = dram("same_prev_d", (EP,), BF16)
        same_next_d = dram("same_next_d", (EP,), BF16)
        thi_d = dram("thi_d", (EP,), BF16)
        tlo_d = dram("tlo_d", (EP,), BF16)
        lim_d = dram("lim_d", (EP,), BF16)
        rcnt_d = dram("rcnt_d", (EP,))
        amp_d = dram("amp_d", (EP,))
        att_amp_d = dram("att_amp_d", (EP,))
        ew_d = dram("ew_d", (EP,))
        comp_d = dram("comp_d", (4, EP))
        where_d = dram("where_d", (N, 1), I32)
        ta = dram("ta", (N + EP, D))
        tb = dram("tb", (N + EP, D))

        def flat(t, p):
            return t.rearrange("(p c) -> p c", p=p)

        def edge_rows(t, i):
            return t[N:N + EP, :].rearrange("(a p c) d -> p a (c d)", p=P, c=8)[:, bass.ds(i, 1), :] \
                .rearrange("p a c -> p (a c)")

        ident = sb("ident", [P, P])
        ones = sb("ones", [P, P])
        XD = sb("XD", [P, NPAIR * 512])
        HH = sb("HH", [P, NPAIR * 512])
        LI = sb("LI", [P, NPAIR, 4, 8], I32)
        IX = sb("IX", [P, NPAIR * 8], I32)
        LASTF = sb("LASTF", [P, NPAIR * 8])
        RCL = sb("RCL", [P, NPAIR * 8])
        CB = sb("CB", [P, D])
        AB = sb("AB", [P, D])
        cols = sb("cols", [P, 32])
        (C_EPS, C_NLIM, C_ATT, C_WEB, C_WAB, C_SGN, C_PRE, C_SPRE, C_POST, C_Z, C_R, C_IN, C_HN,
         C_DZ, C_DR, C_DIN, C_AVG, C_RAVG, C_ONE, C_G0, C_G1, C_G2, C_G3, C_L0, C_L1,
         C_EMPTY, C_TWO, C_C) = range(28)

        def col(n, a=0, b=P):
            return cols[a:b, n:n + 1]

        PS = [ctx.enter_context(nc.psum_tensor(f"ps{n}", [P, 512], F32)) for n in range(8)]

        W0S = sb("W0S", [P, 4, 4, D])
        bd = {n: sb("bd_" + n, [P, P]) for n in (
            "sumA", "sumB", "w1", "wews", "wr", "we", "wa",
            "hsA", "hsB", "hdA", "hdB", "mmA", "mmB", "xxA", "xxB", "mq", "xq", "u0",
            "z", "r", "in", "hz", "hr", "hn", "dz", "dr", "din")}
        attw = sb("attw", [4, P])
        sel = sb("sel", [P, 2])

        G = [sb(f"G{k}", [P, 8, D]) for k in range(2)]
        XG = [sb(f"XG{k}", [P, 8, D]) for k in range(2)]
        MST = sb("MST", [P, 2, 8], I32)
        MG = [sb(f"MG{k}", [P, 8], I32) for k in range(2)]
        ST = [sb(f"ST{k}", [P, 4, 8], I32) for k in range(2)]
        Y = [sb(f"Y{k}", [P, 8, D]) for k in range(2)]
        XC = [sb(f"XC{k}", [P, 8, D]) for k in range(2)]
        SQ = [sb(f"SQ{k}", [P, 8, D]) for k in range(2)]
        H = [sb(f"H{k}", [P, 8, 2, D]) for k in range(2)]
        SM = [sb(f"SM{k}", [P, 4, 8]) for k in range(2)]
        big = [sb(f"big{k}", [P, 1024]) for k in range(8)]

        def bc8(t):
            return t.rearrange("p (c o) -> p c o", o=1).broadcast_to([t.shape[0], 8, D])

        def bcd(t, p=P):
            return t.rearrange("p (o d) -> p o d", o=1).broadcast_to([p, 8, D])

        def rows(t):
            return t.rearrange("p (c d) -> p c d", d=D)

        stage_over()

        zeros_i = HH[0:1, 0:4 * (EP - E)].bitcast(I32)
        node_n = HH[0:1, 2400:2400 + EP - E + 1].bitcast(I32)
        minus1 = HH[0:1, 3008:3010].bitcast(I32)
        iota_w = HH[0:125, 3072:3072 + N // 125].bitcast(I32)
        with nc.Block() as block:
            @block.gpsimd
            def _(pool):
                nc.gpsimd.memset(zeros_i[:], 0).then_inc(sem("pads made"), 1)
                nc.gpsimd.memset(node_n[:], N).then_inc(sem("pads made"), 1)
                nc.gpsimd.memset(minus1[:], -1).then_inc(sem("pads made"), 1)
                nc.gpsimd.iota(iota_w[:], [[1, N // 125]], base=0, channel_multiplier=N // 125).then_inc(sem("pads made"), 1)
                nc.gpsimd.memset(ident[:], 0.0).then_inc(sem("ident zero"), 1)
                nc.gpsimd.memset(ones[:], 1.0)
                pool.wait_ge(sem("ident zero"), 1)
                nc.gpsimd.affine_select(out=ident[:], in_=ident[:], compare_op=ALU.not_equal, fill=1.0,
                                        base=0, pattern=[[-1, P]], channel_multiplier=1)
                nc.gpsimd.iota(LI[:, :, 3, :], [[PAIR, NPAIR], [1, 8]], base=N, channel_multiplier=8)

            @block.sync
            def _(sp):
                s = sem("lists copied")
                sp.dma_start(flat(src_d[0:E], 125), flat(src, 125)).then_inc(s, 16)
                sp.dma_start(flat(dst_d[1:E + 1], 125), flat(dst, 125)).then_inc(s, 16)
                sp.dma_start(flat(typ_d[0:E], 125), flat(etype, 125)).then_inc(s, 16)
                sp.dma_start(att_d[0:E, :].rearrange("(p c) d -> p (c d)", p=125),
                             attr.rearrange("(p c) d -> p (c d)", p=125)).then_inc(s, 16)
                sp.wait_ge(sem("pads made"), 4)

                def line(t):
                    return t.rearrange("(o c) -> o c", o=1)
                sp.dma_start(line(src_d[E:EP]), zeros_i[:, 0:EP - E]).then_inc(s, 16)
                sp.dma_start(line(typ_d[E:EP]), zeros_i[:, 0:EP - E]).then_inc(s, 16)
                sp.dma_start(line(att_d[E:EP, :].rearrange("e d -> (e d)")), zeros_i[:].bitcast(F32)).then_inc(s, 16)
                sp.dma_start(line(dst_d[E + 1:EP + 2]), node_n[:]).then_inc(s, 16)
                sp.dma_start(line(dst_d[0:1]), minus1[:, 0:1]).then_inc(s, 16)
                sp.dma_start(where_d.rearrange("(p c) o -> p (c o)", p=125), iota_w[:]).then_inc(s, 16)
                sp.wait_ge(s, 160)

        stage_over()

        rec_d = dram("rec_d", (EP, 8), I32)
        sorted_d = dram("sorted_d", (EP, 8), I32)
        ent = big[0][0:RQ, 0:256].bitcast(I32), big[1][0:RQ, 0:256].bitcast(I32)
        descents = sb("descents", [RQ, 1])
        unsorted = sb("unsorted", [1, 1], I32)
        with nc.Block() as block:
            @block.sync
            def _(sp):
                sp.dma_start(ent[0], flat(dst_d[1:EP + 1], RQ)).then_inc(sem("neighbours loaded"), 16)
                sp.dma_start(ent[1], flat(dst_d[0:EP], RQ)).then_inc(sem("neighbours loaded"), 16)

            @block.vector
            def _(dve):
                dve.wait_ge(sem("neighbours loaded"), 32)
                nc.vector.tensor_tensor(big[2][0:RQ, 0:256], ent[1], ent[0], ALU.is_gt).then_inc(sem("descents marked"), 1)
                dve.wait_ge(sem("descents marked"), 1)
                nc.vector.tensor_reduce(descents[:], big[2][0:RQ, 0:256], AX.X, ALU.add).then_inc(sem("descents counted"), 1)
                dve.wait_ge(sem("descents summed"), 1)
                nc.vector.tensor_copy(unsorted[:], PS[0][0:1, 0:1])

            @block.tensor
            def _(pe):
                pe.wait_ge(sem("descents counted"), 1)
                nc.tensor.matmul(PS[0][0:1, 0:1], ones[0:RQ, 0:1], descents[:], start=True, stop=True).then_inc(sem("descents summed"), 1)
        stage_over()

        COLS = EP // P
        CHUNK = 1600
        halves = (XD, HH)
        HE = EP // 2
        assert HE % CHUNK == 0 and HE % P == 0
        records = [big[h][:, 0:COLS // 2 * 8].bitcast(I32).rearrange("p (c k) -> p c k", k=8) for h in range(2)]
        compared = big[2][:, :].bitcast(BF16)[:, 0:CHUNK]
        earlier = big[3][:, 0:P]
        mine, ties = big[3][:, 128:256], big[3][:, 256:384]
        key, counts, rank = big[4][:, 0:1], big[4][:, 1:2 + EP // CHUNK], big[4][:, 32:33]
        rank_i, record = big[4][:, 40:41].bitcast(I32), big[4][:, 48:56].bitcast(I32)
        NC = EP // CHUNK
        lists = [big[7][0:RQ, n * 256:(n + 1) * 256].bitcast(I32) for n in range(3)]
        attrs_f = H[0][0:RQ].rearrange("p a b d -> p (a b d)")
        attrs = attrs_f.bitcast(I32)
        mixed = [big[5 + h][0:RQ].bitcast(I32).rearrange("p (c k) -> p c k", k=8) for h in range(2)]
        mixed_attrs = [big[5 + h][0:RQ].rearrange("p (c k) -> p c k", k=8)[:, :, 4:8] for h in range(2)]
        attrs_of = [attrs_f[:, h * 512:(h + 1) * 512].rearrange("p (c k) -> p c k", k=4) for h in range(2)]
        with nc.Block() as block:
            @block.sync
            def _(sp):
                with sp.If(sp.value_load(unsorted[0:1, 0:1]) != 0):
                    for t, d in zip(lists, (src_d, dst_d[1:EP + 1], typ_d)):
                        sp.dma_start(t, flat(d, RQ)).then_inc(sem("lists loaded"), 16)
                    sp.dma_start(attrs, att_d[:, :].rearrange("(p c) d -> p (c d)", p=RQ).bitcast(I32)).then_inc(sem("lists loaded"), 16)
                    for h in range(2):
                        sp.dma_start(halves[h][:].bitcast(I32), dst_d[1 + h * HE:1 + (h + 1) * HE].rearrange("(o c) -> o c", o=1)
                                     .broadcast_to([P, HE])).then_inc(sem("all destinations landed"), 16)
                    sp.wait_ge(sem("interleaved"), 10)
                    rows_of = lambda t, h: t.rearrange("(p h c) k -> p h (c k)", h=2, c=P)[:, h, :]
                    for h in range(2):
                        sp.dma_start(rows_of(rec_d, h), mixed[h].rearrange("p c k -> p (c k)")).then_inc(sem("records filled"), 16)
                    sp.wait_ge(sem("records filled"), 32)
                    for h in range(2):
                        sp.dma_start(records[h], rec_d[h * HE:(h + 1) * HE, :].rearrange("(c p) k -> p c k", p=P)).then_inc(sem("records landed"), 16)
                    sp.wait_ge(sem("records moved"), 1)
                    for h in range(2):
                        sp.dma_start(mixed[h].rearrange("p c k -> p (c k)"), rows_of(sorted_d, h)).then_inc(sem("sorted loaded"), 16)
                    sp.wait_ge(sem("separated"), 8)
                    b = sem("lists replaced")
                    for t, d in zip(lists, (src_d, dst_d[1:EP + 1], typ_d)):
                        sp.dma_start(flat(d, RQ), t).then_inc(b, 16)
                    sp.dma_start(att_d[:, :].rearrange("(p c) d -> p (c d)", p=RQ).bitcast(I32), attrs).then_inc(b, 16)
                    sp.wait_ge(b, 64)

            @block.scalar
            def _(act):
                with act.If(act.value_load(unsorted[0:1, 0:1]) != 0):
                    act.wait_ge(sem("lists loaded"), 64)
                    for h in range(2):
                        for n, t in enumerate((*lists, lists[0])):
                            nc.scalar.activation(mixed[h][:, :, n], t[:, h * P:(h + 1) * P], ACT.Copy).then_inc(sem("interleaved"), 1)
                        nc.scalar.activation(mixed_attrs[h], attrs_of[h], ACT.Copy).then_inc(sem("interleaved"), 1)
                    act.wait_ge(sem("sorted loaded"), 32)
                    for h in range(2):
                        for n, t in enumerate(lists):
                            nc.scalar.activation(t[:, h * P:(h + 1) * P], mixed[h][:, :, n], ACT.Copy).then_inc(sem("separated"), 1)
                        nc.scalar.activation(attrs_of[h], mixed_attrs[h], ACT.Copy).then_inc(sem("separated"), 1)

            @block.vector
            def _(dve):
                with dve.If(dve.value_load(unsorted[0:1, 0:1]) != 0):
                    dve.wait_ge(sem("all destinations landed"), 32)
                    for h in range(2):
                        nc.vector.tensor_copy(halves[h][:], halves[h][:].bitcast(I32)).then_inc(sem("destinations"), 1)
                    dve.wait_ge(sem("destinations"), 2)
                    dve.wait_ge(sem("order mask"), 2)
                    for h in range(2):
                        with dve.Fori(0, COLS // 2) as c:
                            n = c + h * (COLS // 2)
                            here = halves[h][:, bass.ds(c * P, P)]
                            nc.vector.tensor_tensor(mine, here, ident[:], ALU.mult).then_inc(sem("mine"), 1)
                            dve.wait_ge(sem("mine"), n + 1)
                            nc.vector.tensor_reduce(key, mine, AX.X, ALU.add).then_inc(sem("key"), 1)
                            dve.wait_ge(sem("key"), n + 1)
                            nc.vector.scalar_tensor_tensor(out=ties, in0=here, scalar=key, in1=earlier,
                                                           op0=ALU.is_equal, op1=ALU.mult).then_inc(sem("ties"), 1)
                            dve.wait_ge(sem("ties"), n + 1)
                            nc.vector.tensor_reduce(counts[:, 0:1], ties, AX.X, ALU.add).then_inc(sem("tie count"), 1)
                            for m in range(NC):
                                f = halves[m // (NC // 2)][:, (m % (NC // 2)) * CHUNK:(m % (NC // 2) + 1) * CHUNK]
                                nc.vector.tensor_scalar(compared, f, key, None, ALU.is_lt, ALU.add,
                                                        accum_out=counts[:, 1 + m:2 + m]).then_inc(sem("compared"), 1)
                                dve.wait_ge(sem("compared"), n * NC + m + 1)
                            nc.vector.tensor_scalar(here, here, -0.5, None, ALU.add).then_inc(sem("passed"), 1)
                            dve.wait_ge(sem("passed"), n + 1)
                            dve.wait_ge(sem("tie count"), n + 1)
                            nc.vector.tensor_reduce(rank, counts[:], AX.X, ALU.add).then_inc(sem("rank"), 1)
                            dve.wait_ge(sem("rank"), n + 1)
                            dve.wait_ge(sem("rank free"), n + 1)
                            nc.vector.tensor_copy(rank_i, rank).then_inc(sem("ranked"), 1)

            @block.gpsimd
            def _(pool):
                with pool.If(pool.value_load(unsorted[0:1, 0:1]) != 0):
                    nc.gpsimd.memset(earlier, 1.0).then_inc(sem("order mask"), 1)
                    pool.wait_ge(sem("order mask"), 1)
                    nc.gpsimd.affine_select(out=earlier, in_=earlier, compare_op=ALU.is_gt, fill=0.0,
                                            base=0, pattern=[[-1, P]], channel_multiplier=1).then_inc(sem("order mask"), 1)
                    pool.sem_inc(sem("rank free"), 1)
                    pool.wait_ge(sem("records landed"), 32)
                    for h in range(2):
                        with pool.Fori(0, COLS // 2) as c:
                            n = c + h * (COLS // 2)
                            nc.gpsimd.tensor_copy(record, records[h][:, bass.ds(c, 1), :].rearrange("p a k -> p (a k)")).then_inc(sem("record staged"), 1)
                            pool.wait_ge(sem("record staged"), n + 1)
                            pool.wait_ge(sem("ranked"), n + 1)
                            pool.sem_inc(sem("record turn"), 1)
                            nc.gpsimd.indirect_dma_start(sorted_d, bass.IndirectOffsetOnAxis(ap=rank_i, axis=0), record, None).then_inc(sem("record moved"), 16)
                            pool.wait_ge(sem("record moved"), 16 * n + 16)
                            pool.sem_inc(sem("rank free"), 1)
                    pool.sem_inc(sem("records moved"), 1)


        stage_over()

        taken = [0]

        def rl(name, dt=F32, w=256):
            words = w * (2 if dt == BF16 else 4) // 4
            t = XD[0:RQ, taken[0]:taken[0] + words]
            taken[0] += words
            return t if dt == F32 else t.bitcast(dt)
        r_src, r_typ, r_dst, r_prev, r_next = (rl(n, I32) for n in ("r_src", "r_typ", "r_dst", "r_prev", "r_next"))
        r_att = rl("r_att", F32, 1024)
        r_e = rl("r_e", I32)
        r_sp, r_sn, r_hi, r_lo, r_lim = (rl(n, BF16) for n in ("r_sp", "r_sn", "r_hi", "r_lo", "r_lim"))
        f_src, f_dst, f_sc, f_cnt, f_last = (big[n][0:RQ, 0:256] for n in range(5))
        r_ef, r_st, r_loc = (big[n][0:RQ, 256:512] for n in range(3))
        r_hii, r_loi = (rl(n, I32) for n in ("r_hii", "r_loi"))
        r_rc, r_lg, r_s, r_q, r_rl = (big[n][0:RQ, 512:768] for n in range(5))
        r_ew, r_c0, r_c1, r_c2, r_one = (big[n][0:RQ, 768:1024] for n in range(5))
        carry_row = sb("carry_row", [1, RQ + 1])
        carry_col = sb("carry_col", [RQ, 1])
        nv = big[6][0:125, 0:400]
        nvl = big[7][0:125, 0:400]
        nvs = sb("nvs", [125, 1])
        with nc.Block() as block:
            @block.sync
            def _(sp):
                s = sem("rows loaded")
                for t, d in ((r_src, src_d), (r_typ, typ_d), (r_dst, dst_d[1:EP + 1]), (r_prev, dst_d[0:EP]),
                             (r_next, dst_d[2:EP + 2])):
                    sp.dma_start(t[:], flat(d, RQ)).then_inc(s, 16)
                sp.dma_start(r_att[:], att_d.rearrange("(p c) d -> p (c d)", p=RQ)).then_inc(s, 16)
                sp.dma_start(nv, flat(node_vec, 125)).then_inc(sem("node_vec loaded"), 16)
                w = sem("edge values written")
                sp.wait_ge(sem("flags"), 10)
                sp.dma_start(flat(same_prev_d, RQ), r_sp[:]).then_inc(w, 16)
                sp.dma_start(flat(same_next_d, RQ), r_sn[:]).then_inc(w, 16)
                sp.dma_start(flat(thi_d, RQ), r_hi[:]).then_inc(w, 16)
                sp.dma_start(flat(tlo_d, RQ), r_lo[:]).then_inc(w, 16)
                sp.dma_start(flat(lim_d, RQ), r_lim[:]).then_inc(w, 16)
                sp.wait_ge(sem("components"), 5)
                sp.dma_start(flat(ew_d, RQ), r_ew).then_inc(w, 16)
                for n, t in enumerate((r_c0, r_c1, r_c2, r_one)):
                    sp.dma_start(flat(comp_d[n, :], RQ), t).then_inc(w, 16)
                sp.wait_ge(sem("scalers"), 4)
                sp.dma_start(flat(rcnt_d, RQ), r_rc).then_inc(w, 16)
                sp.dma_start(flat(amp_d, RQ), r_s).then_inc(w, 16)
                sp.dma_start(flat(att_amp_d, RQ), r_q).then_inc(w, 16)
                sp.wait_ge(w, 16 * 13)

            @block.gpsimd
            def _(pool):
                nc.gpsimd.iota(r_e[:], [[1, 256]], base=0, channel_multiplier=256).then_inc(sem("edge numbers"), 1)

            @block.vector
            def _(dve):
                dve.wait_ge(sem("rows loaded"), 96)
                f = sem("flags")
                nc.vector.tensor_tensor(r_sp[:], r_dst[:], r_prev[:], ALU.is_equal).then_inc(f, 1)
                nc.vector.tensor_tensor(r_sn[:], r_dst[:], r_next[:], ALU.is_equal).then_inc(f, 1)
                nc.vector.tensor_scalar(r_hii[:], r_typ[:], 2, None, ALU.logical_shift_right).then_inc(f, 1)
                nc.vector.tensor_scalar(r_loi[:], r_typ[:], 3, None, ALU.bitwise_and).then_inc(f, 1)
                dve.wait_ge(f, 4)
                nc.vector.tensor_copy(r_hi[:], r_hii[:]).then_inc(f, 1)
                nc.vector.tensor_copy(r_lo[:], r_loi[:]).then_inc(f, 1)
                nc.vector.tensor_copy(f_src, r_src[:]).then_inc(f, 1)
                nc.vector.tensor_scalar(f_dst, r_dst[:], float(N - 1), None, ALU.min).then_inc(f, 1)
                nc.vector.tensor_scalar(r_lim[:], r_sp[:], 2 * LIMIT, -LIMIT, ALU.mult, ALU.add).then_inc(f, 1)
                nc.vector.tensor_scalar(f_last, r_sn[:], -1.0, 1.0, ALU.mult, ALU.add).then_inc(f, 1)
                nc.vector.scalar_tensor_tensor(out=f_sc, in0=r_sn[:], scalar=FAR, in1=r_dst[:],
                                               op0=ALU.mult, op1=ALU.add).then_inc(sem("far"), 1)
                c = sem("components")
                av = r_att[:].rearrange("p (e c) -> p e c", c=4)
                nc.vector.tensor_copy(r_ew, av[:, :, 3]).then_inc(c, 1)
                for n, t in enumerate((r_c0, r_c1, r_c2)):
                    nc.vector.tensor_copy(t, av[:, :, n]).then_inc(c, 1)
                nc.vector.memset(r_one, 1.0).then_inc(c, 1)
                q = sem("count steps")
                dve.wait_ge(sem("edge numbers"), 1)
                nc.vector.tensor_copy(r_ef, r_e[:]).then_inc(q, 1)
                nc.vector.tensor_scalar(r_st, r_sp[:], -1.0, 1.0, ALU.mult, ALU.add).then_inc(q, 1)
                dve.wait_ge(q, 2)
                nc.vector.tensor_tensor(r_st, r_st, r_ef, ALU.mult).then_inc(q, 1)
                dve.wait_ge(q, 3)
                nc.vector.tensor_tensor_scan(r_loc, r_st, r_st, 0.0, ALU.max, ALU.max).then_inc(q, 1)
                nc.vector.memset(carry_row[:, 0:1], 0.0).then_inc(q, 1)
                dve.wait_ge(sem("carry turned"), 1)
                dve.wait_ge(q, 5)
                nc.vector.tensor_copy(carry_row[:, 1:RQ + 1], PS[0][0:1, 0:RQ]).then_inc(q, 1)
                dve.wait_ge(q, 6)
                nc.vector.tensor_tensor_scan(carry_row[:, 1:RQ + 1], carry_row[:, 1:RQ + 1], carry_row[:, 1:RQ + 1],
                                             0.0, ALU.max, ALU.max).then_inc(q, 1)
                dve.wait_ge(sem("carry turned"), 2)
                nc.vector.tensor_copy(carry_col[:], PS[1][0:RQ, 0:1]).then_inc(q, 1)
                dve.wait_ge(q, 8)
                nc.vector.tensor_scalar(r_loc, r_loc, carry_col[:, 0:1], None, ALU.max).then_inc(q, 1)
                dve.wait_ge(q, 9)
                nc.vector.tensor_tensor(f_cnt, r_ef, r_loc, ALU.subtract).then_inc(q, 1)
                dve.wait_ge(q, 10)
                nc.vector.tensor_scalar(f_cnt, f_cnt, 1.0, None, ALU.add).then_inc(sem("counts"), 1)
                dve.wait_ge(sem("log sum"), 1)
                nc.vector.tensor_scalar(col(C_AVG), PS[2][:, 0:1], 1.0 / N, None, ALU.mult).then_inc(q, 1)
                dve.wait_ge(q, 11)
                nc.vector.reciprocal(col(C_RAVG), col(C_AVG)).then_inc(q, 1)
                dve.wait_ge(sem("counts"), 1)
                nc.vector.reciprocal(r_rc, f_cnt).then_inc(sem("scalers"), 1)
                dve.wait_ge(sem("log counts"), 1)
                nc.vector.reciprocal(r_rl, r_lg).then_inc(sem("scalers"), 1)
                dve.wait_ge(q, 12)
                nc.vector.tensor_scalar(r_s, r_lg, col(C_RAVG, 0, RQ), None, ALU.mult).then_inc(sem("scalers"), 1)
                dve.wait_ge(sem("scalers"), 3)
                nc.vector.scalar_tensor_tensor(out=r_q, in0=r_rl, scalar=col(C_AVG, 0, RQ), in1=r_s,
                                               op0=ALU.mult, op1=ALU.mult).then_inc(sem("scalers"), 1)
                dve.wait_ge(sem("lists turned"), 10)

                def turned(n, half):
                    return PS[3 + n // 2][:, (n % 2) * 256 + half * 100:(n % 2) * 256 + half * 100 + RQ] \
                        .rearrange("p (a h j) -> p a j h", h=2, j=2)

                def placed(t, half):
                    return t.rearrange("p a (j k h) -> p a j k h", j=2, k=2)[:, :, :, half, :]
                for half in range(2):
                    for n in range(3):
                        nc.vector.tensor_copy(placed(LI[:, :, n, :], half), turned(n, half)).then_inc(sem("lists"), 1)
                    nc.vector.tensor_copy(placed(RCL[:].rearrange("p (a c) -> p a c", c=8), half), turned(3, half)).then_inc(sem("lists"), 1)
                    nc.vector.tensor_copy(placed(LASTF[:].rearrange("p (a c) -> p a c", c=8), half), turned(4, half)).then_inc(sem("lists"), 1)
                dve.wait_ge(sem("lists"), 10)
                nc.vector.reciprocal(RCL[:], RCL[:]).then_inc(sem("lists"), 1)
                dve.wait_ge(sem("lists"), 11)
                nc.vector.tensor_tensor(RCL[:], RCL[:], LASTF[:], ALU.mult)

            @block.scalar
            def _(act):
                load_log_exp(act)
                act.wait_ge(sem("node_vec loaded"), 16)
                nc.scalar.activation(nvl, nv, ACT.Ln, bias=1.0, accum_out=nvs[:]).then_inc(sem("logs"), 1)
                act.wait_ge(sem("counts"), 1)
                nc.scalar.activation(r_lg, f_cnt, ACT.Ln, bias=1.0).then_inc(sem("log counts"), 1)

            @block.tensor
            def _(pe):
                pe.wait_ge(sem("logs"), 1)
                nc.tensor.matmul(PS[2][:, 0:1], ones[0:125, :], nvs[:], start=True, stop=True).then_inc(sem("log sum"), 1)
                pe.wait_ge(sem("count steps"), 4)
                nc.tensor.transpose(PS[0][0:1, 0:RQ], r_loc[:, 255:256], ident[0:RQ, 0:RQ]).then_inc(sem("carry turned"), 1)
                pe.wait_ge(sem("count steps"), 7)
                nc.tensor.transpose(PS[1][0:RQ, 0:1], carry_row[:, 0:RQ], ident[0:1, 0:1]).then_inc(sem("carry turned"), 1)
                pe.wait_ge(sem("flags"), 10)
                pe.wait_ge(sem("far"), 1)
                pe.wait_ge(sem("counts"), 1)
                for n, t in enumerate((f_src, f_dst, f_sc, f_cnt, f_last)):
                    for half in range(2):
                        o = (n % 2) * 256 + half * 100
                        nc.tensor.transpose(PS[3 + n // 2][:, o:o + RQ], t[:, half * P:(half + 1) * P],
                                            ident[0:RQ, 0:RQ]).then_inc(sem("lists turned"), 1)

        stage_over()

        used = [4096]

        def wt(name, a, b):
            t = HH[0:a, used[0]:used[0] + b]
            used[0] += b
            return t
        t_we, t_ws2, t_w3, t_p3, t_wih, t_whh = (wt(n, D, w) for n, w in (
            ("we", 64), ("ws2", 128), ("w3", 64), ("p3", 128), ("wih", 192), ("whh", 192)))
        t_pre = wt("pre", D, 192)
        t_e3 = wt("e3", 4, D)
        t_web, t_post_col = wt("web", D, 1), wt("bpost", D, 1)
        t_std = wt("std", D, 192)
        t_big = [big[n][:, :] for n in range(8)]
        o_mm, o_xx, q_mm, q_xx = t_big[0][:, 0:64], t_big[1][:, 0:64], t_big[2][:, 0:128], t_big[3][:, 0:128]
        t_wet, t_w3t, t_ut = t_big[4][0:D, 0:64], t_big[4][0:D, 64:128], t_big[4][0:D, 128:192]
        t_e3t = t_big[4][0:D, 192:196]
        t_w3p = t_big[5][0:D, 0:192]
        t_gin = t_big[6][0:D, 0:192]
        t_bias = t_big[7][:, 0:16]
        t_co, t_sc = wt("co", D, 1), wt("sc", D, 3)
        NAT = D

        def wpost_rows(scaling, aggregate):
            o = NAT * (1 + 4 * scaling + aggregate)
            return wpost[o:o + NAT, :]
        MEAN, MIN, MAX, STD = range(4)

        def column(v):
            return v.rearrange("(p o) -> p o", o=1)
        loads = []
        for g2 in range(2):
            for k in range(4):
                r0 = 8 * k + 4 * g2
                loads.append((W0S[g2 * D:(g2 + 1) * D, k, :, :], w0[r0:r0 + 4].rearrange("x i o -> i x o")))
        for h in range(2):
            q = slice(h * D, (h + 1) * D)
            loads += [(bd["w1"][q, q], w1), (bd["wr"][q, q], wr_k.rearrange("f h d -> f (h d)")),
                      (bd["we"][q, q], we_k.rearrange("f h d -> f (h d)")),
                      (bd["z"][q, q], wih[:, 64:128]), (bd["r"][q, q], wih[:, 0:64]), (bd["in"][q, q], wih[:, 128:192]),
                      (bd["hz"][q, q], whh[:, 64:128]), (bd["hr"][q, q], whh[:, 0:64]), (bd["hn"][q, q], whh[:, 128:192]),
                      (t_ws2[:, q], ws_k), (t_p3[:, q], wpre[128:192, :])]
            for n, v in enumerate((ws_b, wr_b.rearrange("h d -> (h d)"), we_b.rearrange("h d -> (h d)"), bpre, bpost,
                                   bih[64:128], bhh[64:128], bih[0:64], bhh[0:64], bih[128:192], bhh[128:192])):
                loads.append((t_bias[q, n:n + 1], column(v)))
            loads += [(o_mm[q, :], wpost_rows(0, (MEAN, STD)[h])), (o_xx[q, :], wpost_rows(0, (MAX, MIN)[h]))]
            for n in range(2):
                loads += [(q_mm[q, n * D:(n + 1) * D], wpost_rows(1 + n, (MEAN, STD)[h])),
                          (q_xx[q, n * D:(n + 1) * D], wpost_rows(1 + n, (MAX, MIN)[h]))]
        loads += [(t_we[:], we_k.rearrange("f h d -> f (h d)")), (t_w3[:], w3), (t_wih[:], wih), (t_whh[:], whh),
                  (t_pre[:, 0:64], wpre[0:64, :]), (t_pre[:, 64:128], wpre[64:128, :]), (t_pre[:, 128:192], wpost[0:64, :]),
                  (t_e3[0:3, :], w3e), (t_e3[3:4, :], b3e.rearrange("(o d) -> o d", o=1)),
                  (t_web[:], column(we_b.rearrange("h d -> (h d)"))), (t_post_col[:], column(bpost)),
                  (col(C_WAB), wa_b.rearrange("(o d) -> o d", o=1).broadcast_to([P, 1]))]
        for n in range(3):
            loads.append((t_std[:, n * D:(n + 1) * D], wpost_rows(n, STD)))
        t_wa = wt("wa", P, 1)
        loads += [(t_wa[h * D:(h + 1) * D, :], wa_k) for h in range(2)]
        BLOCKS = ("w1", "wr", "we", "z", "r", "in", "hz", "hr", "hn")
        with nc.Block() as block:
            @block.gpsimd
            def _(pool):
                for t in BLOCKS:
                    nc.gpsimd.memset(bd[t][:], 0.0).then_inc(sem("blocks cleared"), 1)
                for t in ("sumA", "sumB", "wews", "wa", "hsA", "hsB", "hdA", "hdB", "mmA", "mmB", "xxA", "xxB", "u0",
                          "dz", "dr", "din"):
                    nc.gpsimd.memset(bd[t][:], 0.0).then_inc(sem("products cleared"), 1)
                nc.gpsimd.memset(sel[:], 0.0).then_inc(sem("products cleared"), 1)

            @block.sync
            def _(sp):
                sp.wait_ge(sem("blocks cleared"), len(BLOCKS))
                for t, v in loads[::2]:
                    sp.dma_start(t, v).then_inc(sem("weights loaded"), 16)

            @block.scalar
            def _(act):
                act.wait_ge(sem("blocks cleared"), len(BLOCKS))
                for t, v in loads[1::2]:
                    act.dma_start(t, v).then_inc(sem("weights loaded"), 16)

            @block.tensor
            def _(pe):
                pe.wait_ge(sem("weights loaded"), 16 * len(loads))
                i64 = ident[0:D, 0:D]
                nc.tensor.transpose(PS[0][0:D, 0:64], t_we[:], i64)
                nc.tensor.transpose(PS[0][0:D, 64:128], t_w3[:], i64)
                nc.tensor.transpose(PS[0][0:D, 192:196], t_e3[:], ident[0:4, 0:4]).then_inc(sem("products"), 1)
                pe.wait_ge(sem("factors"), 1)
                nc.tensor.matmul(PS[1][0:D, 0:64], t_wet, t_ws2[:, 0:64], start=True, stop=True)
                nc.tensor.matmul(PS[1][0:D, 64:256], t_w3t, t_pre[:], start=True, stop=True)
                nc.tensor.matmul(PS[1][0:4, 256:384], t_e3t, t_p3[:], start=True, stop=True)
                nc.tensor.matmul(PS[1][:, 384:385], t_ws2[:], t_web[:], start=True, stop=True).then_inc(sem("products"), 1)
                pe.wait_ge(sem("factors"), 2)
                nc.tensor.transpose(PS[2][0:D, 0:64], t_w3p[:, 128:192], i64).then_inc(sem("products"), 1)
                pe.wait_ge(sem("factors"), 3)
                nc.tensor.matmul(PS[3][0:D, 0:192], t_ut, t_wih[:], start=True, stop=True).then_inc(sem("products"), 1)
                for n in range(3):
                    nc.tensor.matmul(PS[4][0:D, 0:1], t_std[:, n * D:(n + 1) * D], t_sc[:, n:n + 1],
                                     start=(n == 0), stop=(n == 2))
                nc.tensor.matmul(PS[5][:, 0:1], ident[:], t_bias[:, 0:1], start=True, stop=True).then_inc(sem("products"), 1)
                pe.wait_ge(sem("factors"), 4)
                for n, g in enumerate((1, 0, 2)):
                    for h in range(2):
                        nc.tensor.matmul(PS[6][h * D:(h + 1) * D, n:n + 1], t_wih[:, g * D:(g + 1) * D], t_co[:],
                                         start=True, stop=True).then_inc(sem("empty gates"), 1)

            @block.vector
            def _(dve):
                f = sem("factors")
                b = sem("stationaries")
                nc.vector.memset(col(C_EPS), EPS).then_inc(sem("constants"), 1)
                nc.vector.memset(col(C_NLIM), -LIMIT).then_inc(sem("constants"), 1)
                nc.vector.memset(col(C_ONE), 1.0).then_inc(sem("constants"), 1)
                nc.vector.memset(col(C_TWO), 2.0).then_inc(sem("constants"), 1)
                nc.vector.memset(col(C_EMPTY), EPS ** 0.5).then_inc(sem("constants"), 1)
                nc.vector.memset(col(C_SGN, 0, D), 1.0).then_inc(sem("constants"), 1)
                nc.vector.memset(col(C_SGN, D, P), -1.0).then_inc(sem("constants"), 1)
                for h in range(2):
                    for k in range(4):
                        nc.vector.memset(col(C_G0 + k, h * D, (h + 1) * D), float(2 * k + h)).then_inc(sem("constants"), 1)
                    for m in range(2):
                        nc.vector.memset(col(C_L0 + m, h * D, (h + 1) * D), float(2 * m + h)).then_inc(sem("constants"), 1)
                dve.wait_ge(sem("constants"), 19)
                dve.wait_ge(sem("products"), 1)
                nc.vector.tensor_copy(t_big[4][0:D, 0:128], PS[0][0:D, 0:128]).then_inc(b, 1)
                nc.vector.tensor_copy(t_e3t, PS[0][0:D, 192:196]).then_inc(f, 1)
                nc.vector.tensor_copy(t_sc[:, 0:1], col(C_EMPTY, 0, D)).then_inc(b, 1)
                dve.wait_ge(b, 2)
                import math
                ln2 = math.log(2.0)
                nc.vector.scalar_tensor_tensor(out=t_sc[:, 1:2], in0=col(C_RAVG, 0, D), scalar=ln2, in1=t_sc[:, 0:1],
                                               op0=ALU.mult, op1=ALU.mult).then_inc(b, 1)
                dve.wait_ge(b, 3)
                nc.vector.scalar_tensor_tensor(out=t_sc[:, 2:3], in0=col(C_AVG, 0, D), scalar=1.0 / ln2, in1=t_sc[:, 1:2],
                                               op0=ALU.mult, op1=ALU.mult).then_inc(b, 1)
                dve.wait_ge(sem("products"), 2)
                nc.vector.tensor_copy(t_w3p, PS[1][0:D, 64:256]).then_inc(f, 1)
                dve.wait_ge(sem("products cleared"), 17)
                for h in range(2):
                    q = slice(h * D, (h + 1) * D)
                    i64 = ident[q, q]
                    nc.vector.tensor_copy(bd["wews"][q, q], PS[1][0:D, 0:64]).then_inc(b, 1)
                    for n in range(2):
                        c = slice(n * D, (n + 1) * D)
                        t = bd[("hdA", "hdB")[h]]
                        nc.vector.tensor_copy(t[q, c], PS[1][0:D, 64:128]).then_inc(b, 1)
                        t = bd[("hsA", "hsB")[h]]
                        nc.vector.tensor_copy(t[q, c], PS[1][0:D, 128:192]).then_inc(b, 1)
                    nc.vector.tensor_copy(bd["u0"][q, q], PS[1][0:D, 192:256]).then_inc(b, 1)
                    nc.vector.tensor_copy(bd["sumA"][q, 0:D], i64).then_inc(b, 1)
                    nc.vector.tensor_copy(bd["sumB"][q, D:P], i64).then_inc(b, 1)
                    nc.vector.tensor_copy(sel[h * D:h * D + 1, h:h + 1], ones[h * D:h * D + 1, 0:1]).then_inc(b, 1)
                    nc.vector.tensor_copy(bd["wa"][q, q], t_wa[q, 0:1].broadcast_to([D, D])).then_inc(b, 1)
                nc.vector.tensor_copy(attw[:], PS[1][0:4, 256:384]).then_inc(b, 1)
                nc.vector.tensor_copy(bd["mmA"][:, 0:D], o_mm).then_inc(b, 1)
                nc.vector.tensor_copy(bd["mmB"][:, D:P], o_mm).then_inc(b, 1)
                nc.vector.tensor_copy(bd["mq"][:], q_mm).then_inc(b, 1)
                nc.vector.tensor_scalar(bd["xxA"][:, 0:D], o_xx, col(C_SGN), None, ALU.mult).then_inc(b, 1)
                nc.vector.tensor_scalar(bd["xxB"][:, D:P], o_xx, col(C_SGN), None, ALU.mult).then_inc(b, 1)
                nc.vector.tensor_scalar(bd["xq"][:], q_xx, col(C_SGN), None, ALU.mult).then_inc(b, 1)
                nc.vector.tensor_tensor(col(C_ATT), PS[1][:, 384:385], t_bias[:, 0:1], ALU.add).then_inc(b, 1)
                dve.wait_ge(b, 4 + 20 + 8)
                nc.vector.tensor_tensor(col(C_ATT), col(C_ATT), t_bias[:, 1:2], ALU.add).then_inc(b, 1)
                nc.vector.tensor_copy(col(C_WEB), t_bias[:, 2:3]).then_inc(b, 1)
                nc.vector.tensor_copy(col(C_PRE), t_bias[:, 3:4]).then_inc(b, 1)
                nc.vector.tensor_scalar(col(C_SPRE), t_bias[:, 3:4], col(C_SGN), None, ALU.mult).then_inc(b, 1)
                nc.vector.tensor_copy(col(C_POST), t_bias[:, 4:5]).then_inc(b, 1)
                nc.vector.tensor_tensor(col(C_Z), t_bias[:, 5:6], t_bias[:, 6:7], ALU.add).then_inc(b, 1)
                nc.vector.tensor_tensor(col(C_R), t_bias[:, 7:8], t_bias[:, 8:9], ALU.add).then_inc(b, 1)
                nc.vector.tensor_copy(col(C_IN), t_bias[:, 9:10]).then_inc(b, 1)
                nc.vector.tensor_copy(col(C_HN), t_bias[:, 10:11]).then_inc(b, 1)
                dve.wait_ge(sem("products"), 3)
                nc.vector.tensor_copy(t_ut, PS[2][0:D, 0:64]).then_inc(f, 1)
                dve.wait_ge(sem("products"), 4)
                nc.vector.tensor_copy(t_gin, PS[3][0:D, 0:192]).then_inc(b, 1)
                dve.wait_ge(sem("products"), 5)
                nc.vector.tensor_tensor(t_co[:], PS[4][0:D, 0:1], t_post_col[:], ALU.add).then_inc(f, 1)
                dve.wait_ge(b, 4 + 20 + 8 + 10)
                for h in range(2):
                    q = slice(h * D, (h + 1) * D)
                    nc.vector.tensor_tensor(t_big[7][0:D, 64 + 192 * h:128 + 192 * h], t_gin[:, 64:128], t_whh[:, 64:128], ALU.add).then_inc(b, 1)
                    nc.vector.tensor_tensor(t_big[7][0:D, 128 + 192 * h:192 + 192 * h], t_gin[:, 0:64], t_whh[:, 0:64], ALU.add).then_inc(b, 1)
                    dve.wait_ge(b, 42 + 5 * h + 2)
                    nc.vector.tensor_copy(bd["dz"][q, q], t_big[7][0:D, 64 + 192 * h:128 + 192 * h]).then_inc(b, 1)
                    nc.vector.tensor_copy(bd["dr"][q, q], t_big[7][0:D, 128 + 192 * h:192 + 192 * h]).then_inc(b, 1)
                    nc.vector.tensor_copy(bd["din"][q, q], t_gin[:, 128:192]).then_inc(b, 1)
                dve.wait_ge(sem("empty gates"), 6)
                for n, (o, i) in enumerate(((C_DZ, C_Z), (C_DR, C_R), (C_DIN, C_IN))):
                    nc.vector.tensor_tensor(col(o), PS[6][:, n:n + 1], col(i), ALU.add)

        stage_over()

        TY = [sb(f"TY{k}", [P, 2, 1024], BF16) for k in range(2)]
        FL = [sb(f"FL{k}", [P, 512], BF16) for k in range(2)]
        S = sb("S", [P, 512])
        CR = sb("CR", [P, 2])
        MASKED = [[big[2 * h + k // 2][:, (k % 2) * 512:(k % 2 + 1) * 512] for k in range(4)] for h in range(2)]
        CHOSEN = [[big[4 + h][:, m * 512:(m + 1) * 512] for m in range(2)] for h in range(2)]

        def load_flags(sp, t, flags, i, name):
            for h in range(2):
                sp.dma_start(t[h * D:(h + 1) * D, :],
                             flags[bass.ds(i * PAIR + h * HALF, HALF)].rearrange("(o c) -> o c", o=1)
                             .broadcast_to([D, HALF])).then_inc(sem(name), 16)

        def ln_sum(dve, t, k, name, i, bias=False):
            v = t
            if bias:
                nc.vector.tensor_tensor(Y[k][:], t, bcd(CB[:]), ALU.add).then_inc(sem(name + " y"), 1)
                dve.wait_ge(sem(name + " y"), i + 1)
                v = Y[k][:]
            nc.vector.tensor_reduce(SM[k][:, 0, :], v, AX.X, ALU.add).then_inc(sem(name + " sum"), 1)
            dve.wait_ge(sem(name + " sum"), i + 1)
            nc.vector.scalar_tensor_tensor(out=XC[k][:], in0=bc8(SM[k][:, 0, :]), scalar=-1.0 / D, in1=v,
                                           op0=ALU.mult, op1=ALU.add).then_inc(sem(name + " centred"), 1)

        def ln_square(act, k, name, i):
            act.wait_ge(sem(name + " centred"), i + 1)
            nc.scalar.activation(SQ[k][:], XC[k][:], ACT.Square).then_inc(sem(name + " squares"), 1)

        def ln_var(dve, k, name, i):
            dve.wait_ge(sem(name + " squares"), i + 1)
            nc.vector.tensor_reduce(SM[k][:, 1, :], SQ[k][:], AX.X, ALU.add).then_inc(sem(name + " var"), 1)

        def ln_rstd(act, k, name, i):
            act.wait_ge(sem(name + " var"), i + 1)
            nc.scalar.activation(SM[k][:, 2, :], SM[k][:, 1, :], ACT.Ln, scale=1.0 / D, bias=col(C_EPS)).then_inc(sem(name + " log"), 1)
            act.wait_ge(sem(name + " log"), i + 1)
            nc.scalar.activation(SM[k][:, 3, :], SM[k][:, 2, :], ACT.Exp, scale=-0.5).then_inc(sem(name + " rstd"), 1)

        def ln_out(dve, k, name, i, twice=False):
            dve.wait_ge(sem(name + " rstd"), i + 1)
            for c in range(2 if twice else 1):
                nc.vector.scalar_tensor_tensor(out=H[k][:, :, c, :] if twice else H[k][:].rearrange("p a b d -> p (a b d)")[:, 0:512].rearrange("p (c d) -> p c d", d=D),
                                               in0=XC[k][:], scalar=0.0, in1=bc8(SM[k][:, 3, :]),
                                               op0=ALU.max, op1=ALU.mult).then_inc(sem(name + " h"), 1)

        def hrow(k, j):
            return H[k][:].rearrange("p a b d -> p (a b d)")[:, j * P:(j + 1) * P]

        def scan_pair(dve, out, flags, data, carry, name, n):
            for h in range(2):
                q = slice(h * D, (h + 1) * D)
                o = slice((1 - h) * D, (2 - h) * D)
                nc.vector.tensor_tensor_scan(out[q, :], flags[q, :], data[q, :], carry[q, 0:1], ALU.mult, ALU.add).then_inc(sem(name), 1)
                dve.wait_ge(sem(name), n + 2 * h + 1)
                nc.vector.tensor_copy(carry[o, 0:1], out[q, 511:512]).then_inc(sem(name), 1)
                dve.wait_ge(sem(name), n + 2 * h + 2)

        with nc.Block() as block:
            @block.scalar
            def _(act):
                load_log_exp(act)
                for t in (ta, tb):
                    act.dma_start(t[0:N, :].rearrange("n d -> (n d)").rearrange("(p c) -> p c", p=1280),
                                  x.rearrange("n d -> (n d)").rearrange("(p c) -> p c", p=1280)).then_inc(sem("tables filled"), 16)

                def stage(i, k):
                    nc.scalar.activation(ST[k][:], LI[:, bass.ds(i, 1), :, :].rearrange("p a b c -> p (a b) c"), ACT.Copy).then_inc(sem("l0 staged"), 1)
                stage(0, 0)
                stage(1, 1)
                ln_square(act, 0, "l0", 0)
                ln_rstd(act, 0, "l0", 0)

                def body(i, r, k):
                    if exists(i + 1):
                        ln_square(act, 1 - k, "l0", i + 1)
                        ln_rstd(act, 1 - k, "l0", i + 1)
                    act.wait_ge(sem(f"l0 where landed {k}"), 128 * r + 128)
                    nc.scalar.activation(IX[:, bass.ds(i * 8, 8)], MG[k][:], ACT.Copy).then_inc(sem("l0 where kept"), 1)
                    if exists(i + 2):
                        act.wait_ge(sem("l0 x1"), i + 1)
                        stage(i + 2, k)
                rounds(act, body)

            @block.gpsimd
            def _(pool):
                with pool.Fori(0, NPAIR) as i:
                    nc.gpsimd.tensor_copy(MST[:], LI[:, bass.ds(i, 1), 2:4, :].rearrange("p a b c -> p (a b) c")).then_inc(sem("where staged"), 1)
                    pool.wait_ge(sem("where staged"), i + 1)
                    pool.sem_inc(sem("where turn"), 1)
                    for c in range(8):
                        nc.gpsimd.indirect_dma_start(where_d, bass.IndirectOffsetOnAxis(ap=MST[:, 0, c:c + 1], axis=0),
                                                     MST[:, 1, c:c + 1], None, bounds_check=N - 1, oob_is_err=False).then_inc(sem("where written"), 16)
                    pool.wait_ge(sem("where written"), 128 * i + 128)

                def body(i, r, k):
                    pool.wait_ge(sem("l0 staged"), i + 1)
                    pool.sem_inc(sem("l0 turn"), 1)
                    for c in range(8):
                        nc.gpsimd.indirect_dma_start(G[k][:, c, :], None, x, bass.IndirectOffsetOnAxis(ap=ST[k][:, 0, c:c + 1], axis=0)).then_inc(sem(f"l0 src landed {k}"), 16)
                    for c in range(8):
                        nc.gpsimd.indirect_dma_start(XG[k][:, c, :], None, x, bass.IndirectOffsetOnAxis(ap=ST[k][:, 1, c:c + 1], axis=0)).then_inc(sem(f"l0 dst landed {k}"), 16)
                    for c in range(8):
                        nc.gpsimd.indirect_dma_start(MG[k][:, c:c + 1], None, where_d, bass.IndirectOffsetOnAxis(ap=ST[k][:, 0, c:c + 1], axis=0)).then_inc(sem(f"l0 where landed {k}"), 16)
                rounds(pool, body)

            @block.sync
            def _(sp):
                def load(i, k):
                    for n, t in enumerate((thi_d, tlo_d)):
                        sp.dma_start(TY[k][:, n, :], t[bass.ds(i * PAIR, PAIR)].rearrange("(o c) -> o c", o=1).broadcast_to([P, PAIR])).then_inc(sem(f"l0 types landed {k}"), 16)
                    load_flags(sp, FL[k], same_prev_d, i, f"l0 flags landed {k}")
                load(0, 0)
                load(1, 1)

                def body(i, r, k):
                    sp.wait_ge(sem("l0 x1"), i + 1)
                    sp.dma_start(edge_rows(ta, i), XD[:, bass.ds(i * 512, 512)]).then_inc(sem("l0 rows written"), 16)
                    if exists(i + 2):
                        load(i + 2, k)
                rounds(sp, body)
                sp.wait_ge(sem("l0 rows written"), 16 * NPAIR)
                sp.wait_ge(sem("tables filled"), 32)

            @block.tensor
            def _(pe):
                def body(i, r, k):
                    pe.wait_ge(sem("l0 h"), 2 * i + 2)
                    for h in range(2):
                        for j in range(4):
                            ins = nc.tensor.transpose(PS[h][:, j * P:(j + 1) * P],
                                                      H[k][:, 2 * j + h, :, :].rearrange("p b d -> p (b d)"), ident[:])
                        ins.then_inc(sem("l0 turned"), 1)
                    for h in range(2):
                        pe.wait_ge(sem("l0 masked"), 8 * i + 4 * h + 4)
                        for m in range(2):
                            for g in range(4):
                                ins = nc.tensor.matmul(PS[2 + 2 * h + m][:], W0S[:, g, 2 * m:2 * m + 2, :].rearrange("p l o -> p (l o)"),
                                                       MASKED[h][g], start=(g == 0), stop=(g == 3))
                        ins.then_inc(sem("l0 products"), 1)
                    for h in range(2):
                        pe.wait_ge(sem("l0 chosen"), 4 * i + 2 * h + 2)
                        for m in range(2):
                            ins = nc.tensor.matmul(PS[6][:], bd[("sumA", "sumB")[h]][:], CHOSEN[h][m],
                                                   start=(h + m == 0), stop=(h + m == 2))
                    ins.then_inc(sem("l0 messages"), 1)
                    pe.wait_ge(sem("l0 scanned"), 4 * i + 4)
                    for j in range(4):
                        ins = nc.tensor.transpose(PS[7][:, j * P:(j + 1) * P], S[:, j * P:(j + 1) * P], ident[:])
                    ins.then_inc(sem("l0 sums back"), 1)
                rounds(pe, body)

            @block.vector
            def _(dve):
                nc.vector.memset(CR[:], 0.0).then_inc(sem("l0 carry clear"), 1)
                dve.wait_ge(sem("l0 src landed 0"), 128)
                ln_sum(dve, G[0][:], 0, "l0", 0)
                ln_var(dve, 0, "l0", 0)
                ln_out(dve, 0, "l0", 0, twice=True)

                def body(i, r, k):
                    nk, nr = 1 - k, r + k
                    dve.wait_ge(sem(f"l0 types landed {k}"), 32 * r + 32)
                    for h in range(2):
                        dve.wait_ge(sem("l0 turned"), 2 * i + h + 1)
                        for g in range(4):
                            nc.vector.scalar_tensor_tensor(out=MASKED[h][g], in0=TY[k][:, 0, h * 512:(h + 1) * 512],
                                                           scalar=col(C_G0 + g), in1=PS[h][:],
                                                           op0=ALU.is_equal, op1=ALU.mult).then_inc(sem("l0 masked"), 1)
                    if exists(i + 1):
                        dve.wait_ge(sem(f"l0 src landed {nk}"), 128 * nr + 128)
                        ln_sum(dve, G[nk][:], nk, "l0", i + 1)
                    for h in range(2):
                        dve.wait_ge(sem("l0 products"), 2 * i + h + 1)
                        for m in range(2):
                            nc.vector.scalar_tensor_tensor(out=CHOSEN[h][m], in0=TY[k][:, 1, h * 512:(h + 1) * 512],
                                                           scalar=col(C_L0 + m), in1=PS[2 + 2 * h + m][:],
                                                           op0=ALU.is_equal, op1=ALU.mult).then_inc(sem("l0 chosen"), 1)
                        if h == 0 and exists(i + 1):
                            ln_var(dve, nk, "l0", i + 1)
                    if exists(i + 1):
                        ln_out(dve, nk, "l0", i + 1, twice=True)
                    dve.wait_ge(sem("l0 messages"), i + 1)
                    dve.wait_ge(sem(f"l0 flags landed {k}"), 32 * r + 32)
                    scan_pair(dve, S, FL[k], PS[6], CR, "l0 scanned", 4 * i)
                    dve.wait_ge(sem("l0 sums back"), i + 1)
                    dve.wait_ge(sem(f"l0 dst landed {k}"), 128 * r + 128)
                    nc.vector.tensor_tensor(rows(XD[:, bass.ds(i * 512, 512)]), rows(PS[7][:]), XG[k][:], ALU.add).then_inc(sem("l0 x1"), 1)
                rounds(dve, body)

        stage_over()

        U = [XG[k][:] for k in range(2)]
        EX = [big[k][:, 0:512] for k in range(2)]
        RU = [big[k][:, 512:1024] for k in range(2)]
        H2 = [big[2 + k][:, 0:512] for k in range(2)]

        def gather_stage(act, i, k, name):
            nc.scalar.activation(ST[k][:, 0, :], IX[:, bass.ds(i * 8, 8)], ACT.Copy).then_inc(sem(name + " staged"), 1)

        def gather(pool, i, k, name, table):
            pool.wait_ge(sem(name + " staged"), i + 1)
            pool.sem_inc(sem(name + " turn"), 1)
            for c in range(8):
                nc.gpsimd.indirect_dma_start(G[k][:, c, :], None, table, bass.IndirectOffsetOnAxis(ap=ST[k][:, 0, c:c + 1], axis=0)).then_inc(sem(f"{name} landed {k}"), 16)

        def turn_rows(pe, k, i, name, out):
            for j in range(4):
                ins = nc.tensor.transpose(out[:, j * P:(j + 1) * P], hrow(k, j), ident[:])
            ins.then_inc(sem(name + " turned"), 1)

        with nc.Block() as block:
            @block.gpsimd
            def _(pool):
                rounds(pool, lambda i, r, k: gather(pool, i, k, "l1", ta))

            @block.sync
            def _(sp):
                load_flags(sp, FL[0], same_prev_d, 0, "l1 flags landed 0")
                load_flags(sp, FL[1], same_prev_d, 1, "l1 flags landed 1")

                def body(i, r, k):
                    if exists(i + 2):
                        sp.wait_ge(sem("l1 scanned"), 4 * i + 4)
                        load_flags(sp, FL[k], same_prev_d, i + 2, f"l1 flags landed {k}")
                rounds(sp, body)

            @block.scalar
            def _(act):
                load_log_exp(act)
                gather_stage(act, 0, 0, "l1")
                gather_stage(act, 1, 1, "l1")
                ln_square(act, 0, "l1", 0)
                ln_rstd(act, 0, "l1", 0)

                def body(i, r, k):
                    if exists(i + 1):
                        ln_square(act, 1 - k, "l1", i + 1)
                        if exists(i + 2):
                            gather_stage(act, i + 2, k, "l1")
                        ln_rstd(act, 1 - k, "l1", i + 1)
                    act.wait_ge(sem("l1 u"), i + 1)
                    nc.scalar.activation(rows(EX[k]), U[k], ACT.Exp).then_inc(sem("l1 exp"), 1)
                    act.wait_ge(sem("l1 elu"), i + 1)
                    nc.scalar.activation(H2[k], HH[:, bass.ds(i * 512, 512)], ACT.Square).then_inc(sem("l1 squared"), 1)
                rounds(act, body)

            @block.tensor
            def _(pe):
                def total(ps, rhs, first, last):
                    return nc.tensor.matmul(ps[:], ones[:], rhs, start=first, stop=last, skip_group_check=True)
                pe.wait_ge(sem("l1 zeros"), 1)
                total(PS[4], H2[0], True, False)
                total(PS[5], H2[0], True, False).then_inc(sem("l1 sums open"), 1)

                def body(i, r, k):
                    pe.wait_ge(sem("l1 h"), i + 1)
                    turn_rows(pe, k, i, "l1", PS[0])
                    pe.wait_ge(sem("l1 scanned"), 4 * i + 4)
                    for j in range(4):
                        ins = nc.tensor.matmul(PS[1][:, j * P:(j + 1) * P], S[:, j * P:(j + 1) * P], bd["w1"][:], start=True, stop=True)
                    ins.then_inc(sem("l1 products"), 1)
                    last = isinstance(i, int) and i == NPAIR - 1
                    pe.wait_ge(sem("l1 elu"), i + 1)
                    total(PS[4], HH[:, bass.ds(i * 512, 512)], False, last)
                    pe.wait_ge(sem("l1 squared"), i + 1)
                    total(PS[5], H2[k], False, last).then_inc(sem("l1 summed"), 1)
                rounds(pe, body)

            @block.vector
            def _(dve):
                nc.vector.memset(CR[:], 0.0).then_inc(sem("l1 carry clear"), 1)
                nc.vector.memset(H2[0], 0.0).then_inc(sem("l1 zeros"), 1)
                dve.wait_ge(sem("l1 landed 0"), 128)
                ln_sum(dve, G[0][:], 0, "l1", 0)
                ln_var(dve, 0, "l1", 0)
                ln_out(dve, 0, "l1", 0)
                dve.wait_ge(sem("l1 sums open"), 1)

                def body(i, r, k):
                    nk, nr = 1 - k, r + k
                    more = exists(i + 1)
                    if more:
                        dve.wait_ge(sem(f"l1 landed {nk}"), 128 * nr + 128)
                        ln_sum(dve, G[nk][:], nk, "l1", i + 1)
                    dve.wait_ge(sem("l1 turned"), i + 1)
                    dve.wait_ge(sem(f"l1 flags landed {k}"), 32 * r + 32)
                    scan_pair(dve, S, FL[k], PS[0], CR, "l1 scanned", 4 * i)
                    if more:
                        ln_var(dve, nk, "l1", i + 1)
                    dve.wait_ge(sem("l1 products"), i + 1)
                    nc.vector.tensor_tensor(U[k], rows(PS[1][:]), bc8(RCL[:, bass.ds(i * 8, 8)]), ALU.mult).then_inc(sem("l1 u"), 1)
                    if more:
                        ln_out(dve, nk, "l1", i + 1)
                    dve.wait_ge(sem("l1 u"), i + 1)
                    nc.vector.tensor_scalar(rows(RU[k]), U[k], 0.0, -1.0, ALU.max, ALU.add).then_inc(sem("l1 relu"), 1)
                    dve.wait_ge(sem("l1 exp"), i + 1)
                    dve.wait_ge(sem("l1 relu"), i + 1)
                    nc.vector.scalar_tensor_tensor(out=HH[:, bass.ds(i * 512, 512)], in0=EX[k], scalar=1.0, in1=RU[k],
                                                   op0=ALU.min, op1=ALU.add).then_inc(sem("l1 elu"), 1)
                rounds(dve, body)

        gb = big[0][:, 0:128]
        bn = big[1][:, 0:64 * 8]
        with nc.Block() as block:
            @block.sync
            def _(sp):
                sp.dma_start(gb[:, 0:D], gamma.rearrange("(o d) -> o d", o=1).broadcast_to([P, D])).then_inc(sem("bn loaded"), 16)
                sp.dma_start(gb[:, D:2 * D], beta.rearrange("(o d) -> o d", o=1).broadcast_to([P, D])).then_inc(sem("bn loaded"), 16)

                def body(i, r, k):
                    sp.wait_ge(sem("z made"), i + 1)
                    sp.dma_start(edge_rows(ta, i), XD[:, bass.ds(i * 512, 512)]).then_inc(sem("z written"), 16)
                rounds(sp, body)
                sp.wait_ge(sem("z written"), 16 * NPAIR)

            @block.scalar
            def _(act):
                load_log_exp(act)
                act.wait_ge(sem("bn steps"), 6)
                nc.scalar.activation(bn[:, 320:384], bn[:, 256:320], ACT.Ln, bias=col(C_EPS)).then_inc(sem("bn rstd"), 1)
                act.wait_ge(sem("bn rstd"), 1)
                nc.scalar.activation(bn[:, 384:448], bn[:, 320:384], ACT.Exp, scale=-0.5).then_inc(sem("bn rstd"), 1)

            @block.tensor
            def _(pe):
                pe.wait_ge(sem("bn steps"), 9)
                for h in range(2):
                    nc.tensor.matmul(PS[0][h * D:(h + 1) * D, 0:1], CB[0:1, :], ones[0:1, 0:1], start=True, stop=True).then_inc(sem("c turned"), 1)

            @block.vector
            def _(dve):
                q = sem("bn steps")
                m, m2, sq, v = (bn[:, n * D:(n + 1) * D] for n in range(4))
                nc.vector.tensor_reduce(m, PS[4][:].rearrange("p (c d) -> p d c", d=D), AX.X, ALU.add).then_inc(q, 1)
                nc.vector.tensor_reduce(m2, PS[5][:].rearrange("p (c d) -> p d c", d=D), AX.X, ALU.add).then_inc(q, 1)
                dve.wait_ge(q, 2)
                nc.vector.tensor_scalar(m, m, 1.0 / N, None, ALU.mult).then_inc(q, 1)
                dve.wait_ge(q, 3)
                nc.vector.tensor_tensor(sq, m, m, ALU.mult).then_inc(q, 1)
                dve.wait_ge(q, 4)
                nc.vector.scalar_tensor_tensor(out=v, in0=m2, scalar=1.0 / N, in1=sq, op0=ALU.mult, op1=ALU.subtract).then_inc(q, 1)
                dve.wait_ge(q, 5)
                nc.vector.tensor_scalar(bn[:, 256:320], v, 0.0, None, ALU.max).then_inc(q, 1)
                dve.wait_ge(sem("bn rstd"), 2)
                y, yy, half_v = bn[:, 384:448], bn[:, 448:512], bn[:, 256:320]
                n = sem("bn newton")
                nc.vector.tensor_scalar(half_v, half_v, EPS, -0.5, ALU.add, ALU.mult).then_inc(n, 1)
                nc.vector.tensor_tensor(yy, y, y, ALU.mult).then_inc(n, 1)
                dve.wait_ge(n, 2)
                nc.vector.tensor_tensor(yy, yy, half_v, ALU.mult).then_inc(n, 1)
                dve.wait_ge(n, 3)
                nc.vector.scalar_tensor_tensor(out=y, in0=yy, scalar=1.5, in1=y, op0=ALU.add, op1=ALU.mult).then_inc(n, 1)
                dve.wait_ge(n, 4)
                dve.wait_ge(sem("bn loaded"), 32)
                nc.vector.tensor_tensor(AB[:], y, gb[:, 0:D], ALU.mult).then_inc(q, 1)
                dve.wait_ge(q, 7)
                nc.vector.tensor_tensor(sq, m, AB[:], ALU.mult).then_inc(q, 1)
                dve.wait_ge(q, 8)
                nc.vector.tensor_tensor(CB[:], gb[:, D:2 * D], sq, ALU.subtract).then_inc(q, 1)
                dve.wait_ge(sem("c turned"), 2)
                nc.vector.tensor_copy(col(C_C), PS[0][:, 0:1])

                def body(i, r, k):
                    nc.vector.tensor_tensor(Y[k][:], rows(HH[:, bass.ds(i * 512, 512)]), bcd(AB[:]), ALU.mult).then_inc(sem("ah"), 1)
                    dve.wait_ge(sem("ah"), i + 1)
                    xd = rows(XD[:, bass.ds(i * 512, 512)])
                    nc.vector.tensor_tensor(xd, xd, Y[k][:], ALU.add).then_inc(sem("z made"), 1)
                rounds(dve, body)
                dve.wait_ge(q, 9)

        def spread(name):
            stage_over()
            with nc.Block() as block:
                @block.sync
                def _(sp):
                    load_flags(sp, FL[0], same_next_d, NPAIR - 1, name + " flags landed 0")
                    load_flags(sp, FL[1], same_next_d, NPAIR - 2, name + " flags landed 1")

                    def body(i, r, k):
                        if exists(i + 2):
                            down = i * -1 + (NPAIR - 3)
                            sp.wait_ge(sem(name + " spread"), 4 * i + 4)
                            load_flags(sp, FL[k], same_next_d, down, f"{name} flags landed {k}")
                    rounds(sp, body)

                @block.scalar
                def _(act):
                    load_log_exp(act)
                    act.sem_inc(sem(name + " kept"), 2)
                    ln_square(act, 0, name, 0)
                    ln_rstd(act, 0, name, 0)

                    def body(i, r, k):
                        down = i * -1 + (NPAIR - 1)
                        if exists(i + 1):
                            ln_square(act, 1 - k, name, i + 1)
                            ln_rstd(act, 1 - k, name, i + 1)
                        act.wait_ge(sem(name + " spread"), 4 * i + 4)
                        nc.scalar.activation(HH[:, bass.ds(down * 512, 512)], big[k][:, 0:512], ACT.Copy).then_inc(sem(name + " kept"), 1)
                    rounds(act, body)

                @block.tensor
                def _(pe):
                    def body(i, r, k):
                        pe.wait_ge(sem(name + " h"), i + 1)
                        turn_rows(pe, k, i, name, PS[k])
                    rounds(pe, body)

                @block.vector
                def _(dve):
                    def normed(i, k, last):
                        dve.wait_ge(sem(name + " rstd"), i + 1)
                        nc.vector.tensor_tensor(SM[k][:, 3, :], SM[k][:, 3, :], LASTF[:, bass.ds(last, 8)], ALU.mult).then_inc(sem(name + " last"), 1)
                        dve.wait_ge(sem(name + " last"), i + 1)
                        ln_out(dve, k, name, i)
                    nc.vector.memset(CR[:], 0.0).then_inc(sem(name + " carry clear"), 1)
                    ln_sum(dve, rows(XD[:, (NPAIR - 1) * 512:NPAIR * 512]), 0, name, 0, bias=True)
                    ln_var(dve, 0, name, 0)
                    normed(0, 0, (NPAIR - 1) * 8)
                    dve.wait_ge(sem(name + " carry clear"), 1)

                    def body(i, r, k):
                        nk = 1 - k
                        more = exists(i + 1)
                        down = i * -1 + (NPAIR - 1)
                        if more:
                            ln_sum(dve, rows(XD[:, bass.ds((down - 1) * 512, 512)]), nk, name, i + 1, bias=True)
                        dve.wait_ge(sem(name + " turned"), i + 1)
                        dve.wait_ge(sem(f"{name} flags landed {k}"), 32 * r + 32)
                        dve.wait_ge(sem(name + " kept"), i + 1)
                        for n, h in enumerate((1, 0)):
                            q = slice(h * D, (h + 1) * D)
                            o = slice((1 - h) * D, (2 - h) * D)
                            out = big[k][q, 0:512]
                            nc.vector.tensor_tensor_scan(out[:, ::-1], FL[k][q, ::-1], PS[k][q, ::-1], CR[q, 0:1], ALU.mult, ALU.add).then_inc(sem(name + " spread"), 1)
                            dve.wait_ge(sem(name + " spread"), 4 * i + 2 * n + 1)
                            nc.vector.tensor_copy(CR[o, 0:1], out[:, 0:1]).then_inc(sem(name + " spread"), 1)
                            dve.wait_ge(sem(name + " spread"), 4 * i + 2 * n + 2)
                            if n == 0 and more:
                                ln_var(dve, nk, name, i + 1)
                        if more:
                            normed(i + 1, nk, (down - 1) * 8)
                    rounds(dve, body)
        spread("s2")

        stage_over()

        HS = sb("HS", [P, 512])
        X = SQ[0][:].rearrange("p c d -> p (c d)")
        XA, XB = big[0][:, 0:512], big[0][:, 512:1024]
        EE = big[1][:, 0:512]
        QU, WW = big[1][:, 512:1024], big[2][:, 0:512]
        LQ = big[2][:, 512:1024]
        LG = big[3][:, 0:512]
        LIM = big[3][:, 512:1024]
        DIF = big[4]
        AW = big[5]
        VV = big[6][:, 0:512]
        MX = sb("MX", [P, 513])
        SS = big[7][:].rearrange("p (n c) -> p n c", n=2)
        MSG = XG
        with nc.Block() as block:
            @block.gpsimd
            def _(pool):
                rounds(pool, lambda i, r, k: gather(pool, i, k, "l2", ta))

            @block.sync
            def _(sp):
                load_flags(sp, FL[0], same_prev_d, 0, "l2 flags landed 0")
                load_flags(sp, FL[1], same_prev_d, 1, "l2 flags landed 1")

                def body(i, r, k):
                    sp.wait_ge(sem("l2 z"), i + 1)
                    sp.dma_start(edge_rows(tb, i), XD[:, bass.ds(i * 512, 512)]).then_inc(sem("l2 rows written"), 16)
                    if exists(i + 2):
                        load_flags(sp, FL[k], same_prev_d, i + 2, f"l2 flags landed {k}")
                rounds(sp, body)
                sp.wait_ge(sem("l2 rows written"), 16 * NPAIR)

            @block.scalar
            def _(act):
                load_log_exp(act)
                gather_stage(act, 0, 0, "l2")
                gather_stage(act, 1, 1, "l2")
                ln_square(act, 0, "l2", 0)
                ln_rstd(act, 0, "l2", 0)

                def body(i, r, k):
                    act.wait_ge(sem("l2 turned"), i + 1)
                    nc.scalar.activation(HS[:], PS[0][:], ACT.Copy).then_inc(sem("l2 hs"), 1)
                    act.wait_ge(sem(f"l2 flags landed {k}"), 32 * r + 32)
                    nc.scalar.activation(LIM, FL[k][:], ACT.Identity, scale=2 * LIMIT, bias=col(C_NLIM)).then_inc(sem("l2 lim"), 1)
                    act.wait_ge(sem("l2 products"), i + 1)
                    nc.scalar.activation(XA, PS[1][:], ACT.Identity, bias=col(C_ATT)).then_inc(sem("l2 pre"), 1)
                    nc.scalar.activation(EE, PS[2][:], ACT.Identity, bias=col(C_WEB)).then_inc(sem("l2 edges"), 1)
                    act.wait_ge(sem("l2 cut"), i + 1)
                    nc.scalar.activation(XB, XB, ACT.Exp).then_inc(sem("l2 u"), 1)
                    act.wait_ge(sem("l2 q"), i + 1)
                    nc.scalar.activation(LQ, QU, ACT.Ln, bias=col(C_TWO)).then_inc(sem("l2 log q"), 1)
                    act.wait_ge(sem("l2 log q"), i + 1)
                    nc.scalar.activation(LQ, LQ, ACT.Exp, scale=-1.0).then_inc(sem("l2 inverse"), 1)
                    if exists(i + 1):
                        ln_square(act, 1 - k, "l2", i + 1)
                        if exists(i + 2):
                            gather_stage(act, i + 2, k, "l2")
                        ln_rstd(act, 1 - k, "l2", i + 1)
                    act.wait_ge(sem("l2 logits"), i + 1)
                    nc.scalar.activation(LG, PS[3][:], ACT.Identity, bias=col(C_WAB)).then_inc(sem("l2 lg"), 1)
                    act.wait_ge(sem("l2 dif"), 2 * i + 2)
                    nc.scalar.activation(AW[:], DIF[:], ACT.Exp).then_inc(sem("l2 weights"), 1)
                rounds(act, body)

            @block.tensor
            def _(pe):
                def body(i, r, k):
                    pe.wait_ge(sem("l2 h"), i + 1)
                    turn_rows(pe, k, i, "l2", PS[0])
                    hd = HH[:, bass.ds(i * 512, 512)]
                    nc.tensor.matmul(PS[1][:], bd["wr"][:], hd, start=True, stop=False)
                    pe.wait_ge(sem("l2 hs"), i + 1)
                    nc.tensor.matmul(PS[1][:], bd["wews"][:], HS[:], start=False, stop=True)
                    nc.tensor.matmul(PS[2][:], bd["we"][:], HS[:], start=True, stop=True).then_inc(sem("l2 products"), 1)
                    pe.wait_ge(sem("l2 mish"), i + 1)
                    nc.tensor.matmul(PS[3][:], bd["wa"][:], XB, start=True, stop=True).then_inc(sem("l2 logits"), 1)
                    pe.wait_ge(sem("l2 summed"), 4 * i + 4)
                    for j in range(4):
                        nc.tensor.transpose(PS[4][:, j * P:(j + 1) * P], SS[:, 0, j * P:(j + 1) * P], ident[:])
                    for j in range(4):
                        ins = nc.tensor.matmul(PS[5][:, 2 * j:2 * j + 2], SS[:, 1, j * P:(j + 1) * P], sel[:], start=True, stop=True)
                    ins.then_inc(sem("l2 back"), 1)
                rounds(pe, body)

            @block.vector
            def _(dve):
                nc.vector.memset(CR[:], 0.0).then_inc(sem("l2 clear"), 1)
                nc.vector.memset(MX[:, 512:513], -LIMIT).then_inc(sem("l2 clear"), 1)
                dve.wait_ge(sem("l2 landed 0"), 128)
                ln_sum(dve, G[0][:], 0, "l2", 0, bias=True)
                ln_var(dve, 0, "l2", 0)
                ln_out(dve, 0, "l2", 0)
                dve.wait_ge(sem("l2 clear"), 2)

                def body(i, r, k):
                    nk, nr = 1 - k, r + k
                    more = exists(i + 1)
                    dve.wait_ge(sem("l2 pre"), i + 1)
                    nc.vector.tensor_scalar(XB, XA, 20.0, None, ALU.min).then_inc(sem("l2 cut"), 1)
                    if more:
                        dve.wait_ge(sem(f"l2 landed {nk}"), 128 * nr + 128)
                        ln_sum(dve, G[nk][:], nk, "l2", i + 1, bias=True)
                    dve.wait_ge(sem("l2 u"), i + 1)
                    nc.vector.scalar_tensor_tensor(out=QU, in0=XB, scalar=2.0, in1=XB, op0=ALU.add, op1=ALU.mult).then_inc(sem("l2 q"), 1)
                    dve.wait_ge(sem("l2 q"), i + 1)
                    nc.vector.tensor_tensor(WW, QU, XA, ALU.mult).then_inc(sem("l2 qx"), 1)
                    if more:
                        ln_var(dve, nk, "l2", i + 1)
                    dve.wait_ge(sem("l2 inverse"), i + 1)
                    dve.wait_ge(sem("l2 qx"), i + 1)
                    nc.vector.tensor_tensor(XB, WW, LQ, ALU.mult).then_inc(sem("l2 mish"), 1)
                    if more:
                        ln_out(dve, nk, "l2", i + 1)
                    dve.wait_ge(sem("l2 lg"), i + 1)
                    dve.wait_ge(sem("l2 lim"), i + 1)
                    mx = sem("l2 max")
                    for h in range(2):
                        q = slice(h * D, (h + 1) * D)
                        o = slice((1 - h) * D, (2 - h) * D)
                        nc.vector.tensor_copy(MX[q, 0:1], MX[o, 512:513]).then_inc(mx, 1)
                        dve.wait_ge(mx, 4 * i + 2 * h + 1)
                        nc.vector.tensor_tensor_scan(MX[q, 1:513], LIM[q, :], LG[q, :], MX[q, 0:1], ALU.min, ALU.max).then_inc(mx, 1)
                        dve.wait_ge(mx, 4 * i + 2 * h + 2)
                    nc.vector.tensor_tensor(VV, MX[:, 0:512], LIM, ALU.min).then_inc(sem("l2 before"), 1)
                    nc.vector.tensor_tensor(DIF[:, 512:1024], LG, MX[:, 1:513], ALU.subtract).then_inc(sem("l2 dif"), 1)
                    dve.wait_ge(sem("l2 before"), i + 1)
                    nc.vector.tensor_tensor(DIF[:, 0:512], VV, MX[:, 1:513], ALU.subtract).then_inc(sem("l2 dif"), 1)
                    dve.wait_ge(sem("l2 weights"), i + 1)
                    nc.vector.tensor_tensor(VV, AW[:, 512:1024], EE, ALU.mult).then_inc(sem("l2 weighted"), 1)
                    dve.wait_ge(sem("l2 weighted"), i + 1)
                    for h in range(2):
                        q = slice(h * D, (h + 1) * D)
                        o = slice((1 - h) * D, (2 - h) * D)
                        for n, v in enumerate((VV, AW[:, 512:1024])):
                            nc.vector.tensor_tensor_scan(SS[q, n, :], AW[q, 0:512], v[q, :], CR[q, n:n + 1], ALU.mult, ALU.add).then_inc(sem("l2 summed"), 1)
                        dve.wait_ge(sem("l2 summed"), 4 * i + 2 * h + 2)
                        nc.vector.tensor_copy(CR[o, :], SS[q, :, 511]).then_inc(sem("l2 carried"), 1)
                        dve.wait_ge(sem("l2 carried"), 2 * i + h + 1)
                    dve.wait_ge(sem("l2 back"), i + 1)
                    nc.vector.reciprocal(SM[k][:, 0, :], PS[5][:, 0:8]).then_inc(sem("l2 rden"), 1)
                    dve.wait_ge(sem("l2 rden"), i + 1)
                    nc.vector.tensor_tensor(MSG[k][:], rows(PS[4][:]), bc8(SM[k][:, 0, :]), ALU.mult).then_inc(sem("l2 msg"), 1)
                    dve.wait_ge(sem("l2 msg"), i + 1)
                    xd = rows(XD[:, bass.ds(i * 512, 512)])
                    nc.vector.tensor_tensor(xd, xd, MSG[k][:], ALU.add).then_inc(sem("l2 z"), 1)
                    dve.wait_ge(sem("l2 z"), i + 1)
                rounds(dve, body)

        spread("s3")

        ZR, RH, NT = big[7], S, MX[:, 0:512]
        FF = TY[0][:, 1, :].bitcast(F32)

        DP = 125
        DW = 4 * DP
        CYCLE = 4
        DROUNDS = (UNITS - 6) // CYCLE
        assert UNITS == CYCLE * DROUNDS + 6
        OD = [XG[k][0:DP] for k in range(2)]
        W0F = W0S[:].rearrange("p a b d -> p (a b d)")
        YD = [Y[0][:], Y[1][:], rows(W0F[:, 0:512]), rows(W0F[:, 512:1024])]
        x_u = x.rearrange("(u p c) d -> p u (c d)", p=DP, c=8)
        out_u = out.rearrange("(u p c) d -> p u (c d)", p=DP, c=8)
        HTD = [big[0][:, k * 512:k * 512 + DW] for k in range(2)]
        ZD = [big[7][:, k * 512:k * 512 + DW] for k in range(2)]
        RD = [big[6][:, k * 512:k * 512 + DW] for k in range(2)]
        ND, RHD, FD0 = NT[:, 0:DW], RH[:, 0:DW], FF[:, 0:DW]
        NEWTON = [big[5][:, k * 64:(k + 1) * 64].rearrange("p (n c) -> p n c", c=8) for k in range(2)]
        GUESS = float(0x5f3759df)
        with nc.Block() as block:
            def units(eng, body):
                with eng.Fori(0, DROUNDS) as r:
                    for j in range(CYCLE):
                        body(CYCLE * r + j, 2 * r + j // 2, j)
                for i in range(CYCLE * DROUNDS, UNITS):
                    body(i, i // 2, i % CYCLE)

            def unit_exists(i):
                return not isinstance(i, int) or i < UNITS

            @block.sync
            def _(sp):
                def load(i, k):
                    sp.dma_start(G[k][0:DP].rearrange("p c d -> p (c d)"), x_u[:, bass.ds(i, 1), :].rearrange("p a c -> p (a c)")).then_inc(sem(f"d landed {k}"), 16)
                load(0, 0)
                load(1, 1)
                for k in range(2):
                    sp.wait_ge(sem("d y"), k + 1)
                    load(2 + k, k)

                def body(i, n, j):
                    k = j % 2
                    if unit_exists(i + 4):
                        sp.wait_ge(sem("d y"), i + 3)
                        load(i + 4, k)
                    sp.wait_ge(sem("d o"), i + 1)
                    sp.dma_start(out_u[:, bass.ds(i, 1), :].rearrange("p a c -> p (a c)"), OD[k].rearrange("p c d -> p (c d)")).then_inc(sem(f"d written {k}"), 16)
                units(sp, body)
                for k in range(2):
                    sp.wait_ge(sem(f"d written {k}"), 16 * (UNITS // 2 + 1))

            @block.gpsimd
            def _(pool):
                for k in range(2):
                    pool.sem_inc(sem(f"d written {k}"), 16)

                def body(i, n, j):
                    k = j % 2
                    v, y, a, b = (NEWTON[k][:, m, :] for m in range(4))
                    step = sem("d newton")
                    pool.wait_ge(sem("d var"), i + 1)
                    pool.sem_inc(sem("d pool turn"), 1)
                    nc.gpsimd.tensor_scalar(v, SM[k][:, 1, :], 1.0 / D, EPS, ALU.mult, ALU.add).then_inc(step, 1)
                    count = i * 14 + 1
                    pool.wait_ge(step, count)
                    pool.sem_inc(sem("d pool turn"), 1)
                    nc.gpsimd.tensor_scalar(y.bitcast(I32), v.bitcast(I32), -0.5, GUESS, ALU.mult, ALU.add).then_inc(step, 1)
                    pool.wait_ge(step, count + 1)
                    for m in range(3):
                        nc.gpsimd.tensor_tensor(a, y, y, ALU.mult).then_inc(step, 1)
                        pool.wait_ge(step, count + 4 * m + 2)
                        nc.gpsimd.tensor_tensor(b, a, v, ALU.mult).then_inc(step, 1)
                        pool.wait_ge(step, count + 4 * m + 3)
                        pool.sem_inc(sem("d pool turn"), 1)
                        nc.gpsimd.tensor_scalar(a, b, -0.5, 1.5, ALU.mult, ALU.add).then_inc(step, 1)
                        pool.wait_ge(step, count + 4 * m + 4)
                        nc.gpsimd.tensor_tensor(SM[k][:, 3, :] if m == 2 else y, a, y, ALU.mult).then_inc(sem("d rstd") if m == 2 else step, 1)
                        if m < 2:
                            pool.wait_ge(step, count + 4 * m + 5)
                    pool.sem_inc(step, 1)
                units(pool, body)

            @block.scalar
            def _(act):
                def gates(i, k):
                    act.wait_ge(sem("d gates"), 2 * i + 1)
                    nc.scalar.activation(RD[k], PS[5][:, 0:DW], ACT.Sigmoid, bias=col(C_DR)).then_inc(sem("d r"), 1)
                    act.wait_ge(sem("d gates"), 2 * i + 2)
                    nc.scalar.activation(ZD[k], PS[4][:, 0:DW], ACT.Sigmoid, bias=col(C_DZ)).then_inc(sem("d z"), 1)

                def ht(i, k):
                    act.wait_ge(sem("d turned"), i + 1)
                    nc.scalar.activation(HTD[k], PS[1][:, 0:DW], ACT.Copy).then_inc(sem("d ht"), 1)
                ln_square(act, 0, "d", 0)
                ln_square(act, 1, "d", 1)
                ht(0, 0)
                gates(0, 0)

                def body(i, n, j):
                    k = j % 2
                    act.wait_ge(sem("d n sum"), i + 1)
                    nc.scalar.activation(ND, PS[7][:, 0:DW], ACT.Tanh, bias=col(C_DIN)).then_inc(sem("d n"), 1)
                    if unit_exists(i + 1):
                        ht(i + 1, 1 - k)
                    if unit_exists(i + 2):
                        ln_square(act, k, "d", i + 2)
                    if unit_exists(i + 1):
                        gates(i + 1, 1 - k)
                units(act, body)

            @block.tensor
            def _(pe):
                def start(i, k):
                    pe.wait_ge(sem("d h"), i + 1)
                    for j in range(4):
                        ins = nc.tensor.transpose(PS[1][:, j * DP:(j + 1) * DP], hrow(k, j)[0:DP, :], ident[0:DP, 0:DP])
                    ins.then_inc(sem("d turned"), 1)
                    pe.wait_ge(sem("d ht"), i + 1)
                    nc.tensor.matmul(PS[5][:, 0:DW], bd["dr"][:], HTD[k], start=True, stop=True).then_inc(sem("d gates"), 1)
                    nc.tensor.matmul(PS[6][:, 0:DW], bd["hn"][:], HTD[k], start=True, stop=True).then_inc(sem("d hn"), 1)
                    nc.tensor.matmul(PS[4][:, 0:DW], bd["dz"][:], HTD[k], start=True, stop=True).then_inc(sem("d gates"), 1)
                    if not (isinstance(i, int) and i == 0):
                        pe.wait_ge(sem("d n"), i)
                    nc.tensor.matmul(PS[7][:, 0:DW], bd["din"][:], HTD[k], start=True, stop=False)
                start(0, 0)

                def body(i, n, j):
                    pe.wait_ge(sem("d rh"), i + 1)
                    nc.tensor.matmul(PS[7][:, 0:DW], ident[:], RHD, start=False, stop=True).then_inc(sem("d n sum"), 1)
                    if unit_exists(i + 1):
                        start(i + 1, 1 - j % 2)
                    pe.wait_ge(sem("d f"), i + 1)
                    for j in range(4):
                        ins = nc.tensor.transpose(PS[0][0:DP, j * P:(j + 1) * P], FD0[:, j * DP:(j + 1) * DP], ident[:])
                    ins.then_inc(sem("d back"), 1)
                units(pe, body)

            @block.vector
            def _(dve):
                def centre(i, n, j):
                    k = j % 2
                    dve.wait_ge(sem(f"d landed {k}"), 16 * n + 16)
                    nc.vector.tensor_tensor(YD[j], G[k][:], bcd(CB[:]), ALU.add).then_inc(sem("d y"), 1)
                    dve.wait_ge(sem("d y"), i + 1)
                    nc.vector.tensor_reduce(SM[k][:, 0, :], YD[j], AX.X, ALU.add).then_inc(sem("d sum"), 1)
                    dve.wait_ge(sem("d sum"), i + 1)
                    nc.vector.scalar_tensor_tensor(out=XC[k][:], in0=bc8(SM[k][:, 0, :]), scalar=-1.0 / D, in1=YD[j],
                                                   op0=ALU.mult, op1=ALU.add).then_inc(sem("d centred"), 1)
                for i in range(2):
                    centre(i, 0, i)
                for i in range(2):
                    ln_var(dve, i, "d", i)
                ln_out(dve, 0, "d", 0)

                def body(i, n, j):
                    k = j % 2
                    dve.wait_ge(sem("d hn"), i + 1)
                    dve.wait_ge(sem("d r"), i + 1)
                    nc.vector.scalar_tensor_tensor(out=RHD, in0=PS[6][:, 0:DW], scalar=col(C_HN), in1=RD[k],
                                                   op0=ALU.add, op1=ALU.mult).then_inc(sem("d rh"), 1)
                    if unit_exists(i + 1):
                        ln_out(dve, 1 - k, "d", i + 1)
                    if unit_exists(i + 2):
                        centre(i + 2, n + 1, (j + 2) % CYCLE)
                    dve.wait_ge(sem("d n"), i + 1)
                    nc.vector.tensor_tensor(FD0, HTD[k], ND, ALU.subtract).then_inc(sem("d h - n"), 1)
                    if unit_exists(i + 2):
                        ln_var(dve, k, "d", i + 2)
                    dve.wait_ge(sem("d z"), i + 1)
                    dve.wait_ge(sem("d h - n"), i + 1)
                    nc.vector.tensor_tensor(FD0, FD0, ZD[k], ALU.mult).then_inc(sem("d z(h - n)"), 1)
                    dve.wait_ge(sem("d z(h - n)"), i + 1)
                    nc.vector.tensor_tensor(FD0, FD0, ND, ALU.add).then_inc(sem("d f"), 1)
                    dve.wait_ge(sem("d back"), i + 1)
                    dve.wait_ge(sem(f"d written {k}"), 16 * n + 16)
                    nc.vector.tensor_tensor(OD[k], rows(PS[0][:])[0:DP], YD[j][0:DP], ALU.add).then_inc(sem("d o"), 1)
                units(dve, body)

        stage_over()

        TT, V1, V2, S1, S2, MM = (big[n] for n in (0, 1, 2, 4, 5, 6))
        OT = big[3][:, 0:512]
        LIMD = big[3][:, 512:1024].bitcast(BF16)
        ZZ = big[0]
        FD = TY[0][:, 0, :]
        EW = W0S[:].rearrange("p a b d -> p (a b d)")
        RC = TY[1][:].rearrange("p a b -> p (a b)").bitcast(F32)
        SC = sb("SC", [P, 1024])
        AT = [H[k][0:4].rearrange("p a b d -> p (a b d)")[:, 512:1024] for k in range(2)]
        SCT = sb("SCT", [P, 2, 8], I32)
        VAR = S1[D:P, :]
        ROW = [XG[k] for k in range(2)]
        both = [slice(h * 512, (h + 1) * 512) for h in range(2)]
        with nc.Block() as block:
            @block.gpsimd
            def _(pool):
                pool.sem_inc(sem("l3 rows free"), 2)
                for i in range(3):
                    gather(pool, i, i % 2, "l3", tb)

                def body(i, r, k):
                    if exists(i + 3):
                        gather(pool, i + 3, 1 - k, "l3", tb)
                    nc.gpsimd.tensor_copy(SCT[:, k, :], LI[:, bass.ds(i, 1), 2, :].rearrange("p a c -> p (a c)")).then_inc(sem("l3 dst staged"), 1)
                    pool.wait_ge(sem("l3 dst staged"), i + 1)
                    pool.wait_ge(sem("l3 rows"), i + 1)
                    pool.sem_inc(sem("l3 out turn"), 1)
                    for c in range(8):
                        nc.gpsimd.indirect_dma_start(out, bass.IndirectOffsetOnAxis(ap=SCT[:, k, c:c + 1], axis=0), ROW[k][:, c, :], None,
                                                     bounds_check=N - 1, oob_is_err=False).then_inc(sem(f"l3 written {k}"), 16)
                    pool.wait_ge(sem(f"l3 written {k}"), 128 * r + 128)
                    pool.sem_inc(sem("l3 rows free"), 1)
                rounds(pool, body)

            @block.sync
            def _(sp):
                def spread_line(t, d, i, name):
                    sp.dma_start(t, d[bass.ds(i * PAIR, PAIR)].rearrange("(o c) -> o c", o=1).broadcast_to([t.shape[0], PAIR])).then_inc(sem(name), 16)

                def load_a(i):
                    spread_line(EW, ew_d, i, "l3 ew landed")
                    for h in range(2):
                        sp.dma_start(AT[h], comp_d[:, bass.ds(i * PAIR + h * HALF, HALF)]).then_inc(sem("l3 attr landed"), 16)

                def load_b(i):
                    spread_line(RC, rcnt_d, i, "l3 rcnt landed")
                    spread_line(FD, same_prev_d, i, "l3 flags landed")
                    spread_line(LIMD, lim_d, i, "l3 limits landed")

                def load_c(i):
                    spread_line(SC[0:D, :], amp_d, i, "l3 scalers landed")
                    spread_line(SC[D:P, :], att_amp_d, i, "l3 scalers landed")
                load_a(0)
                load_b(0)
                load_c(0)
                sp.wait_ge(sem("l3 t"), 2)
                load_a(1)
                sp.wait_ge(sem("l3 carried"), 4)
                load_b(1)

                def body(i, r, k):
                    if exists(i + 1):
                        sp.wait_ge(sem("l3 scaled"), 2 * i + 2)
                        load_c(i + 1)
                    if exists(i + 2):
                        sp.wait_ge(sem("l3 t"), 2 * i + 4)
                        load_a(i + 2)
                        sp.wait_ge(sem("l3 carried"), 2 * i + 6)
                        load_b(i + 2)
                rounds(sp, body)

            @block.scalar
            def _(act):
                def source(i):
                    act.wait_ge(sem("l3 turned"), i + 1)
                    nc.scalar.activation(HS[:], PS[0][:], ACT.Copy).then_inc(sem("l3 hs"), 1)

                def operands(i):
                    act.wait_ge(sem("l3 t"), 2 * i + 2)
                    nc.scalar.activation(V1[0:D, :], TT[0:D, :], ACT.Identity, bias=col(C_PRE, 0, D)).then_inc(sem("l3 v1"), 1)
                    nc.scalar.activation(V1[D:P, :], TT[D:P, :], ACT.Square, bias=col(C_PRE, D, P)).then_inc(sem("l3 v1"), 1)
                    nc.scalar.activation(V2[:], TT[:], ACT.Identity, scale=col(C_SGN), bias=col(C_SPRE)).then_inc(sem("l3 v2"), 1)

                def mean_squared(i):
                    act.wait_ge(sem("l3 mean"), i + 1)
                    nc.scalar.activation(VAR, MM[0:D, :], ACT.Square).then_inc(sem("l3 mean squared"), 1)

                def std(i):
                    act.wait_ge(sem("l3 variance"), i + 1)
                    nc.scalar.activation(VAR, VAR, ACT.Ln).then_inc(sem("l3 var log"), 1)
                    act.wait_ge(sem("l3 var log"), i + 1)
                    nc.scalar.activation(MM[D:P, :], VAR, ACT.Exp, scale=0.5).then_inc(sem("l3 std"), 1)
                load_log_exp(act)
                gather_stage(act, 0, 0, "l3")
                gather_stage(act, 1, 1, "l3")
                ln_square(act, 0, "l3", 0)
                gather_stage(act, 2, 0, "l3")
                ln_rstd(act, 0, "l3", 0)
                ln_square(act, 1, "l3", 1)
                ln_rstd(act, 1, "l3", 1)
                source(0)
                operands(0)
                mean_squared(0)
                std(0)

                def body(i, r, k):
                    if exists(i + 3):
                        gather_stage(act, i + 3, 1 - k, "l3")
                    if exists(i + 1):
                        source(i + 1)
                    act.wait_ge(sem("l3 total"), i + 1)
                    nc.scalar.activation(OT, PS[3][:], ACT.Identity, bias=col(C_POST)).then_inc(sem("l3 out"), 1)
                    act.wait_ge(sem("l3 gate r"), i + 1)
                    nc.scalar.activation(ZR[:, 512:1024], PS[5][:], ACT.Sigmoid, bias=col(C_R)).then_inc(sem("l3 sr"), 1)
                    act.wait_ge(sem("l3 gate z"), i + 1)
                    nc.scalar.activation(ZR[:, 0:512], PS[4][:], ACT.Sigmoid, bias=col(C_Z)).then_inc(sem("l3 sz"), 1)
                    if exists(i + 1):
                        operands(i + 1)
                    act.wait_ge(sem("l3 n sum"), i + 1)
                    nc.scalar.activation(NT, PS[7][:], ACT.Tanh, bias=col(C_IN)).then_inc(sem("l3 n"), 1)
                    if exists(i + 2):
                        ln_square(act, k, "l3", i + 2)
                    if exists(i + 1):
                        load_log_exp(act)
                        mean_squared(i + 1)
                        std(i + 1)
                    if exists(i + 2):
                        ln_rstd(act, k, "l3", i + 2)
                rounds(act, body)

            @block.tensor
            def _(pe):
                def dst(i):
                    return HH[:, bass.ds(i * 512, 512)]

                def raw_dst(i):
                    pe.wait_ge(sem("l3 attr landed"), 32 * i + 32)
                    for h in range(2):
                        nc.tensor.matmul(PS[1 + h][:], attw[:], AT[h], start=True, stop=False)
                        nc.tensor.matmul(PS[1 + h][:], bd[("hdA", "hdB")[h]][:], dst(i), start=False, stop=False)

                def raw_src(i):
                    pe.wait_ge(sem("l3 hs"), i + 1)
                    for h in range(2):
                        nc.tensor.matmul(PS[1 + h][:], bd[("hsA", "hsB")[h]][:], HS[:], start=False, stop=True).then_inc(sem("l3 raw"), 1)
                pe.wait_ge(sem("l3 h"), 1)
                turn_rows(pe, 0, 0, "l3", PS[0])
                raw_dst(0)
                raw_src(0)

                def body(i, r, k):
                    pe.wait_ge(sem("l3 std"), i + 1)
                    for h, c in enumerate(both):
                        nc.tensor.matmul(PS[1 + h][:], bd["mq"][:], MM[:, c], start=True, stop=False)
                        nc.tensor.matmul(PS[1 + h][:], bd["xq"][:], S2[:, c], start=False, stop=True).then_inc(sem("l3 q"), 1)
                    if exists(i + 1):
                        pe.wait_ge(sem("l3 h"), i + 2)
                        turn_rows(pe, 1 - k, i + 1, "l3", PS[0])
                    nc.tensor.matmul(PS[3][:], bd["u0"][:], dst(i), start=True, stop=False)
                    for h, c in enumerate(both):
                        nc.tensor.matmul(PS[3][:], bd[("mmA", "mmB")[h]][:], MM[:, c], start=False, stop=False)
                        nc.tensor.matmul(PS[3][:], bd[("xxA", "xxB")[h]][:], S2[:, c], start=False, stop=False)
                    for h, c in enumerate(both):
                        pe.wait_ge(sem("l3 scaled"), 2 * i + h + 1)
                        ins = nc.tensor.matmul(PS[3][:], bd[("sumA", "sumB")[h]][:], ZZ[:, c], start=False, stop=(h == 1))
                    ins.then_inc(sem("l3 total"), 1)
                    if exists(i + 1):
                        raw_dst(i + 1)
                        raw_src(i + 1)
                    nc.tensor.matmul(PS[6][:], bd["hn"][:], dst(i), start=True, stop=True)
                    nc.tensor.matmul(PS[5][:], bd["hr"][:], dst(i), start=True, stop=False)
                    pe.wait_ge(sem("l3 out"), i + 1)
                    nc.tensor.matmul(PS[5][:], bd["r"][:], OT, start=False, stop=True).then_inc(sem("l3 gate r"), 1)
                    nc.tensor.matmul(PS[4][:], bd["hz"][:], dst(i), start=True, stop=False)
                    nc.tensor.matmul(PS[4][:], bd["z"][:], OT, start=False, stop=True).then_inc(sem("l3 gate z"), 1)
                    nc.tensor.matmul(PS[7][:], bd["in"][:], OT, start=True, stop=False)
                    pe.wait_ge(sem("l3 rh"), i + 1)
                    nc.tensor.matmul(PS[7][:], ident[:], RH[:], start=False, stop=True).then_inc(sem("l3 n sum"), 1)
                    pe.wait_ge(sem("l3 f"), i + 1)
                    for j in range(4):
                        ins = nc.tensor.transpose(PS[4][:, j * P:(j + 1) * P], FF[:, j * P:(j + 1) * P], ident[:])
                    ins.then_inc(sem("l3 back"), 1)
                rounds(pe, body)

            @block.vector
            def _(dve):
                def centre(i, n, k):
                    dve.wait_ge(sem(f"l3 landed {k}"), 128 * n + 128)
                    ln_sum(dve, G[k][:], k, "l3", i, bias=True)

                def weighted(i):
                    dve.wait_ge(sem("l3 ew landed"), 16 * i + 16)
                    for h, c in enumerate(both):
                        dve.wait_ge(sem("l3 raw"), 2 * i + h + 1)
                        nc.vector.tensor_tensor(TT[:, c], PS[1 + h][:], EW[:, c], ALU.mult).then_inc(sem("l3 t"), 1)

                def scans(i):
                    dve.wait_ge(sem("l3 v1"), 2 * i + 2)
                    dve.wait_ge(sem("l3 flags landed"), 16 * i + 16)
                    dve.wait_ge(sem("l3 carried"), 2 * i + 2)
                    nc.vector.tensor_tensor_scan(S1[:], FD, V1[:], CR[:, 0:1], ALU.mult, ALU.add).then_inc(sem("l3 sums"), 1)
                    dve.wait_ge(sem("l3 v2"), i + 1)
                    dve.wait_ge(sem("l3 limits landed"), 16 * i + 16)
                    nc.vector.tensor_tensor_scan(S2[:], LIMD, V2[:], CR[:, 1:2], ALU.min, ALU.max).then_inc(sem("l3 maxima"), 1)
                    dve.wait_ge(sem("l3 rcnt landed"), 16 * i + 16)
                    dve.wait_ge(sem("l3 sums"), i + 1)
                    nc.vector.tensor_copy(CR[:, 0:1], S1[:, 1023:1024]).then_inc(sem("l3 carried"), 1)
                    nc.vector.tensor_tensor(MM[:], S1[:], RC, ALU.mult).then_inc(sem("l3 mean"), 1)
                    dve.wait_ge(sem("l3 maxima"), i + 1)
                    nc.vector.tensor_copy(CR[:, 1:2], S2[:, 1023:1024]).then_inc(sem("l3 carried"), 1)

                def variance(i):
                    dve.wait_ge(sem("l3 mean squared"), i + 1)
                    nc.vector.tensor_tensor(VAR, MM[D:P, :], VAR, ALU.subtract).then_inc(sem("l3 raw variance"), 1)
                    dve.wait_ge(sem("l3 raw variance"), i + 1)
                    nc.vector.tensor_scalar(VAR, VAR, 0.0, EPS, ALU.max, ALU.add).then_inc(sem("l3 variance"), 1)
                nc.vector.memset(CR[:, 0:1], 0.0).then_inc(sem("l3 carried"), 1)
                nc.vector.memset(CR[:, 1:2], -LIMIT).then_inc(sem("l3 carried"), 1)
                for k in range(2):
                    centre(k, 0, k)
                    ln_var(dve, k, "l3", k)
                    ln_out(dve, k, "l3", k)
                weighted(0)
                scans(0)
                variance(0)

                def body(i, r, k):
                    dve.wait_ge(sem("l3 scalers landed"), 32 * i + 32)
                    for h, c in enumerate(both):
                        dve.wait_ge(sem("l3 q"), 2 * i + h + 1)
                        nc.vector.tensor_tensor(ZZ[:, c], PS[1 + h][:], SC[:, c], ALU.mult).then_inc(sem("l3 scaled"), 1)
                    if exists(i + 2):
                        centre(i + 2, r + 1, k)
                    if exists(i + 1):
                        weighted(i + 1)
                    dve.wait_ge(sem("l3 sr"), i + 1)
                    nc.vector.scalar_tensor_tensor(out=RH[:], in0=PS[6][:], scalar=col(C_HN), in1=ZR[:, 512:1024],
                                                   op0=ALU.add, op1=ALU.mult).then_inc(sem("l3 rh"), 1)
                    if exists(i + 1):
                        scans(i + 1)
                    dve.wait_ge(sem("l3 n"), i + 1)
                    nc.vector.tensor_tensor(FF, HH[:, bass.ds(i * 512, 512)], NT, ALU.subtract).then_inc(sem("l3 h - n"), 1)
                    if exists(i + 2):
                        ln_var(dve, k, "l3", i + 2)
                    dve.wait_ge(sem("l3 sz"), i + 1)
                    dve.wait_ge(sem("l3 h - n"), i + 1)
                    nc.vector.tensor_tensor(FF, FF, ZR[:, 0:512], ALU.mult).then_inc(sem("l3 z(h - n)"), 1)
                    if exists(i + 1):
                        variance(i + 1)
                    dve.wait_ge(sem("l3 z(h - n)"), i + 1)
                    nc.vector.scalar_tensor_tensor(out=FF, in0=FF, scalar=col(C_C), in1=NT, op0=ALU.add, op1=ALU.add).then_inc(sem("l3 f"), 1)
                    if exists(i + 2):
                        ln_out(dve, k, "l3", i + 2)
                    dve.wait_ge(sem("l3 back"), i + 1)
                    dve.wait_ge(sem("l3 rows free"), i + 1)
                    nc.vector.tensor_tensor(ROW[k][:], rows(PS[4][:]), rows(XD[:, bass.ds(i * 512, 512)]), ALU.add).then_inc(sem("l3 rows"), 1)
                rounds(dve, body)
        stage_over()


_INS = ['x', 'src', 'dst', 'edge_attr_4', 'edge_type_32', 'node_vec', 'L0_gnn_weight', 'L1_gnn_W', 'L1_gnn_gamma',
        'L1_gnn_beta', 'L2_gnn_We_k', 'L2_gnn_We_b', 'L2_gnn_Ws_k', 'L2_gnn_Ws_b', 'L2_gnn_Wr_k', 'L2_gnn_Wr_b',
        'L2_gnn_Wa_k', 'L2_gnn_Wa_b', 'L3_gnn_W', 'L3_gnn_We', 'L3_gnn_be', 'L3_gnn_Wpre', 'L3_gnn_bpre',
        'L3_gnn_Wpost', 'L3_gnn_bpost', 'L3_gnn_Wih', 'L3_gnn_bih', 'L3_gnn_Whh', 'L3_gnn_bhh']
_OUTS = [((50000, 64), 'float32')]


def kernel(**inputs):
    import numpy as _np
    import concourse.bacc as _bacc
    from concourse import mybir as _mybir
    from concourse.bass_utils import run_bass_kernel_spmd as _run

    nc = _bacc.Bacc("TRN2", target_bir_lowering=False, num_devices=1)
    arrays, args = {}, []
    for name in _INS:
        a = _np.ascontiguousarray(inputs[name])
        arrays[f"in_{name}_dram"] = a
        args.append(nc.dram_tensor(f"in_{name}_dram", a.shape, _mybir.dt.from_np(a.dtype), kind="ExternalInput").ap())
    for i, (shape, dtype) in enumerate(_OUTS):
        dt = _mybir.dt.from_np(_np.dtype(dtype))
        args.append(nc.dram_tensor(f"out_{i}_dram", shape, dt, kind="ExternalOutput").ap())
    gnn_kernel(nc, *args)
    r = _run(nc, [arrays], core_ids=[0])
    got = tuple(r.results[0][f"out_{i}_dram"] for i in range(len(_OUTS)))
    return got[0]
```

```python
from contextlib import ExitStack

import concourse.bass as bass
from concourse import mybir

F32 = mybir.dt.float32
BF16 = mybir.dt.bfloat16
I32 = mybir.dt.int32
ALU = mybir.AluOpType
ACT = mybir.ActivationFunctionType
AX = mybir.AxisListType

P = 128
D = 64
EPS = 1e-5
LIMIT = 1e38
FAR = float(1 << 20)


def gnn_kernel(nc, x, src, dst, attr, etype, node_vec, w0, w1, gamma, beta,
               we_k, we_b, ws_k, ws_b, wr_k, wr_b, wa_k, wa_b,
               w3, w3e, b3e, wpre, bpre, wpost, bpost, wih, bih, whh, bhh, out, debug=None):
    N = x.shape[0]
    E = src.shape[0]
    PAIR = 8 * P
    HALF = PAIR // 2
    NPAIR = -(-E // PAIR)
    EP = NPAIR * PAIR
    RQ = EP // 256
    NREL = w0.shape[0]
    assert N % (NPAIR * 80) == 0 and NPAIR % 2 == 1 and NREL == 32 and N % 1000 == 0 and RQ <= P
    UNITS = N // 1000
    EARLY = 6
    ROUNDS = (NPAIR - 3) // 2

    with ExitStack() as ctx:
        def sb(name, shape, dt=F32):
            return ctx.enter_context(nc.sbuf_tensor(name, shape, dt))

        def dram(name, shape, dt=F32):
            return nc.dram_tensor(name, shape, dt).ap()

        sems = {}

        def sem(name):
            if name not in sems:
                sems[name] = nc.alloc_semaphore(name=name.replace(" ", "_"))
            return sems[name]

        def stage_over():
            nc.clear_and_free_semaphores(list(sems.values()))
            sems.clear()
            nc.all_engine_barrier()

        def load_log_exp(act):
            nc.scalar.preload_act_table_set("natural_log_exp_and_others")

        def rounds(eng, body, first=0):
            with eng.Fori(first // 2, ROUNDS) as r:
                body(2 * r, r, 0)
                body(2 * r + 1, r, 1)
            for i in range(2 * ROUNDS, NPAIR):
                body(i, i // 2, i % 2)

        def exists(i):
            return not isinstance(i, int) or i < NPAIR

        src_d = dram("src_d", (EP,), I32)
        dst_d = dram("dst_d", (EP + 2,), I32)
        typ_d = dram("typ_d", (EP,), I32)
        att_d = dram("att_d", (EP, 4))
        same_prev_d = dram("same_prev_d", (EP,), BF16)
        same_next_d = dram("same_next_d", (EP,), BF16)
        thi_d = dram("thi_d", (EP,), BF16)
        tlo_d = dram("tlo_d", (EP,), BF16)
        lim_d = dram("lim_d", (EP,), BF16)
        rcnt_d = dram("rcnt_d", (EP,))
        amp_d = dram("amp_d", (EP,))
        att_amp_d = dram("att_amp_d", (EP,))
        ew_d = dram("ew_d", (EP,))
        comp_d = dram("comp_d", (4, EP))
        where_d = dram("where_d", (N, 1), I32)
        ta = dram("ta", (N + EP, D))
        tb = dram("tb", (N + EP, D))

        def flat(t, p):
            return t.rearrange("(p c) -> p c", p=p)

        def edge_rows(t, i):
            return t[N:N + EP, :].rearrange("(a p c) d -> p a (c d)", p=P, c=8)[:, bass.ds(i, 1), :] \
                .rearrange("p a c -> p (a c)")

        def node_rows(t, i):
            return t[0:N, :].rearrange("(a p c) d -> p a (c d)", a=NPAIR, p=80)[:, bass.ds(i, 1), :] \
                .rearrange("p a c -> p (a c)")

        ident = sb("ident", [P, P])
        ones = sb("ones", [P, P])
        XD = sb("XD", [P, NPAIR * 512])
        HH = sb("HH", [P, NPAIR * 512])
        LI = sb("LI", [P, NPAIR, 4, 8], I32)
        IX = sb("IX", [P, NPAIR * 8], I32)
        LASTF = sb("LASTF", [P, NPAIR * 8])
        RCL = sb("RCL", [P, NPAIR * 8])
        CB = sb("CB", [P, D])
        AB = sb("AB", [P, D])
        cols = sb("cols", [P, 32])
        (C_EPS, C_NLIM, C_ATT, C_WEB, C_WAB, C_SGN, C_PRE, C_SPRE, C_POST, C_Z, C_R, C_IN, C_HN,
         C_DZ, C_DR, C_DIN, C_AVG, C_RAVG, C_ONE, C_G0, C_G1, C_G2, C_G3, C_L0, C_L1,
         C_EMPTY, C_TWO, C_C) = range(28)

        def col(n, a=0, b=P):
            return cols[a:b, n:n + 1]

        PS = [ctx.enter_context(nc.psum_tensor(f"ps{n}", [P, 512], F32)) for n in range(8)]

        W0S = sb("W0S", [P, 4, 4, D])
        bd = {n: sb("bd_" + n, [P, P]) for n in (
            "sumA", "sumB", "ends", "mmA", "mmB", "xxA", "xxB", "mq", "xq", "u0",
            "z", "r", "in", "hz", "hr", "hn")}
        BEFORE = sb("BEFORE", [P, 8 * P])
        for n, name in enumerate(("w1", "wews", "wr", "we", "wa", "dz", "dr", "din")):
            bd[name] = BEFORE[:, n * P:(n + 1) * P]
        attw = sb("attw", [4, P])
        sel = sb("sel", [P, 2])

        G = [sb(f"G{k}", [P, 8, D]) for k in range(2)]
        XG = [sb(f"XG{k}", [P, 8, D]) for k in range(2)]
        MG = [sb(f"MG{k}", [P, 8], I32) for k in range(2)]
        ST = [sb(f"ST{k}", [P, 4, 8], I32) for k in range(2)]
        Y = [sb(f"Y{k}", [P, 8, D]) for k in range(2)]
        XC = [sb(f"XC{k}", [P, 8, D]) for k in range(2)]
        SQ = [sb(f"SQ{k}", [P, 8, D]) for k in range(2)]
        H = [sb(f"H{k}", [P, 8, 2, D]) for k in range(2)]
        SM = [sb(f"SM{k}", [P, 4, 8]) for k in range(2)]
        big = [sb(f"big{k}", [P, 1024]) for k in range(8)]

        def bc8(t):
            return t.rearrange("p (c o) -> p c o", o=1).broadcast_to([t.shape[0], 8, D])

        def bcd(t, p=P):
            return t.rearrange("p (o d) -> p o d", o=1).broadcast_to([p, 8, D])

        def rows(t):
            return t.rearrange("p (c d) -> p c d", d=D)

        stage_over()

        zeros_i = HH[0:1, 0:4 * (EP - E)].bitcast(I32)
        node_n = HH[0:1, 2400:2400 + EP - E + 1].bitcast(I32)
        minus1 = HH[0:1, 3008:3010].bitcast(I32)
        iota_w = HH[0:125, 3072:3072 + N // 125].bitcast(I32)
        with nc.Block() as block:
            @block.gpsimd
            def _(pool):
                nc.gpsimd.memset(zeros_i[:], 0).then_inc(sem("pads made"), 1)
                nc.gpsimd.memset(node_n[:], N).then_inc(sem("pads made"), 1)
                nc.gpsimd.memset(minus1[:], -1).then_inc(sem("pads made"), 1)
                nc.gpsimd.iota(iota_w[:], [[1, N // 125]], base=0, channel_multiplier=N // 125).then_inc(sem("pads made"), 1)
                nc.gpsimd.memset(ident[:], 0.0).then_inc(sem("ident zero"), 1)
                nc.gpsimd.memset(ones[:], 1.0)
                pool.wait_ge(sem("ident zero"), 1)
                nc.gpsimd.affine_select(out=ident[:], in_=ident[:], compare_op=ALU.not_equal, fill=1.0,
                                        base=0, pattern=[[-1, P]], channel_multiplier=1)
                nc.gpsimd.iota(LI[:, :, 3, :], [[PAIR, NPAIR], [1, 8]], base=N, channel_multiplier=8)

            @block.sync
            def _(sp):
                s = sem("lists copied")
                sp.dma_start(flat(src_d[0:E], 125), flat(src, 125)).then_inc(s, 16)
                sp.dma_start(flat(dst_d[1:E + 1], 125), flat(dst, 125)).then_inc(s, 16)
                sp.dma_start(flat(typ_d[0:E], 125), flat(etype, 125)).then_inc(s, 16)
                sp.dma_start(att_d[0:E, :].rearrange("(p c) d -> p (c d)", p=125),
                             attr.rearrange("(p c) d -> p (c d)", p=125)).then_inc(s, 16)
                sp.wait_ge(sem("pads made"), 4)

                def line(t):
                    return t.rearrange("(o c) -> o c", o=1)
                sp.dma_start(line(src_d[E:EP]), zeros_i[:, 0:EP - E]).then_inc(s, 16)
                sp.dma_start(line(typ_d[E:EP]), zeros_i[:, 0:EP - E]).then_inc(s, 16)
                sp.dma_start(line(att_d[E:EP, :].rearrange("e d -> (e d)")), zeros_i[:].bitcast(F32)).then_inc(s, 16)
                sp.dma_start(line(dst_d[E + 1:EP + 2]), node_n[:]).then_inc(s, 16)
                sp.dma_start(line(dst_d[0:1]), minus1[:, 0:1]).then_inc(s, 16)
                sp.dma_start(where_d.rearrange("(p c) o -> p (c o)", p=125), iota_w[:]).then_inc(s, 16)
                sp.wait_ge(s, 160)

        stage_over()

        rec_d = dram("rec_d", (EP, 8), I32)
        sorted_d = dram("sorted_d", (EP, 8), I32)
        ent = big[0][0:RQ, 0:256].bitcast(I32), big[1][0:RQ, 0:256].bitcast(I32)
        descents = sb("descents", [RQ, 1])
        unsorted = sb("unsorted", [1, 1], I32)
        with nc.Block() as block:
            @block.sync
            def _(sp):
                sp.dma_start(ent[0], flat(dst_d[1:EP + 1], RQ)).then_inc(sem("neighbours loaded"), 16)
                sp.dma_start(ent[1], flat(dst_d[0:EP], RQ)).then_inc(sem("neighbours loaded"), 16)

            @block.vector
            def _(dve):
                dve.wait_ge(sem("neighbours loaded"), 32)
                nc.vector.tensor_tensor(big[2][0:RQ, 0:256], ent[1], ent[0], ALU.is_gt).then_inc(sem("descents marked"), 1)
                dve.wait_ge(sem("descents marked"), 1)
                nc.vector.tensor_reduce(descents[:], big[2][0:RQ, 0:256], AX.X, ALU.add).then_inc(sem("descents counted"), 1)
                dve.wait_ge(sem("descents summed"), 1)
                nc.vector.tensor_copy(unsorted[:], PS[0][0:1, 0:1])

            @block.tensor
            def _(pe):
                pe.wait_ge(sem("descents counted"), 1)
                nc.tensor.matmul(PS[0][0:1, 0:1], ones[0:RQ, 0:1], descents[:], start=True, stop=True).then_inc(sem("descents summed"), 1)
        stage_over()

        COLS = EP // P
        CHUNK = 1600
        halves = (XD, HH)
        HE = EP // 2
        assert HE % CHUNK == 0 and HE % P == 0
        records = [big[h][:, 0:COLS // 2 * 8].bitcast(I32).rearrange("p (c k) -> p c k", k=8) for h in range(2)]
        compared = big[2][:, :].bitcast(BF16)[:, 0:CHUNK]
        earlier = big[3][:, 0:P]
        mine, ties = big[3][:, 128:256], big[3][:, 256:384]
        key, counts, rank = big[4][:, 0:1], big[4][:, 1:2 + EP // CHUNK], big[4][:, 32:33]
        rank_i, record = big[4][:, 40:41].bitcast(I32), big[4][:, 48:56].bitcast(I32)
        NC = EP // CHUNK
        lists = [big[7][0:RQ, n * 256:(n + 1) * 256].bitcast(I32) for n in range(3)]
        attrs_f = H[0][0:RQ].rearrange("p a b d -> p (a b d)")
        attrs = attrs_f.bitcast(I32)
        mixed = [big[5 + h][0:RQ].bitcast(I32).rearrange("p (c k) -> p c k", k=8) for h in range(2)]
        mixed_attrs = [big[5 + h][0:RQ].rearrange("p (c k) -> p c k", k=8)[:, :, 4:8] for h in range(2)]
        attrs_of = [attrs_f[:, h * 512:(h + 1) * 512].rearrange("p (c k) -> p c k", k=4) for h in range(2)]
        with nc.Block() as block:
            @block.sync
            def _(sp):
                with sp.If(sp.value_load(unsorted[0:1, 0:1]) != 0):
                    for t, d in zip(lists, (src_d, dst_d[1:EP + 1], typ_d)):
                        sp.dma_start(t, flat(d, RQ)).then_inc(sem("lists loaded"), 16)
                    sp.dma_start(attrs, att_d[:, :].rearrange("(p c) d -> p (c d)", p=RQ).bitcast(I32)).then_inc(sem("lists loaded"), 16)
                    for h in range(2):
                        sp.dma_start(halves[h][:].bitcast(I32), dst_d[1 + h * HE:1 + (h + 1) * HE].rearrange("(o c) -> o c", o=1)
                                     .broadcast_to([P, HE])).then_inc(sem("all destinations landed"), 16)
                    sp.wait_ge(sem("interleaved"), 10)
                    rows_of = lambda t, h: t.rearrange("(p h c) k -> p h (c k)", h=2, c=P)[:, h, :]
                    for h in range(2):
                        sp.dma_start(rows_of(rec_d, h), mixed[h].rearrange("p c k -> p (c k)")).then_inc(sem("records filled"), 16)
                    sp.wait_ge(sem("records filled"), 32)
                    for h in range(2):
                        sp.dma_start(records[h], rec_d[h * HE:(h + 1) * HE, :].rearrange("(c p) k -> p c k", p=P)).then_inc(sem("records landed"), 16)
                    sp.wait_ge(sem("records moved"), 1)
                    for h in range(2):
                        sp.dma_start(mixed[h].rearrange("p c k -> p (c k)"), rows_of(sorted_d, h)).then_inc(sem("sorted loaded"), 16)
                    sp.wait_ge(sem("separated"), 8)
                    b = sem("lists replaced")
                    for t, d in zip(lists, (src_d, dst_d[1:EP + 1], typ_d)):
                        sp.dma_start(flat(d, RQ), t).then_inc(b, 16)
                    sp.dma_start(att_d[:, :].rearrange("(p c) d -> p (c d)", p=RQ).bitcast(I32), attrs).then_inc(b, 16)
                    sp.wait_ge(b, 64)

            @block.scalar
            def _(act):
                with act.If(act.value_load(unsorted[0:1, 0:1]) != 0):
                    act.wait_ge(sem("lists loaded"), 64)
                    for h in range(2):
                        for n, t in enumerate((*lists, lists[0])):
                            nc.scalar.activation(mixed[h][:, :, n], t[:, h * P:(h + 1) * P], ACT.Copy).then_inc(sem("interleaved"), 1)
                        nc.scalar.activation(mixed_attrs[h], attrs_of[h], ACT.Copy).then_inc(sem("interleaved"), 1)
                    act.wait_ge(sem("sorted loaded"), 32)
                    for h in range(2):
                        for n, t in enumerate(lists):
                            nc.scalar.activation(t[:, h * P:(h + 1) * P], mixed[h][:, :, n], ACT.Copy).then_inc(sem("separated"), 1)
                        nc.scalar.activation(attrs_of[h], mixed_attrs[h], ACT.Copy).then_inc(sem("separated"), 1)

            @block.vector
            def _(dve):
                with dve.If(dve.value_load(unsorted[0:1, 0:1]) != 0):
                    dve.wait_ge(sem("all destinations landed"), 32)
                    for h in range(2):
                        nc.vector.tensor_copy(halves[h][:], halves[h][:].bitcast(I32)).then_inc(sem("destinations"), 1)
                    dve.wait_ge(sem("destinations"), 2)
                    dve.wait_ge(sem("order mask"), 2)
                    for h in range(2):
                        with dve.Fori(0, COLS // 2) as c:
                            n = c + h * (COLS // 2)
                            here = halves[h][:, bass.ds(c * P, P)]
                            nc.vector.tensor_tensor(mine, here, ident[:], ALU.mult).then_inc(sem("mine"), 1)
                            dve.wait_ge(sem("mine"), n + 1)
                            nc.vector.tensor_reduce(key, mine, AX.X, ALU.add).then_inc(sem("key"), 1)
                            dve.wait_ge(sem("key"), n + 1)
                            nc.vector.scalar_tensor_tensor(out=ties, in0=here, scalar=key, in1=earlier,
                                                           op0=ALU.is_equal, op1=ALU.mult).then_inc(sem("ties"), 1)
                            dve.wait_ge(sem("ties"), n + 1)
                            nc.vector.tensor_reduce(counts[:, 0:1], ties, AX.X, ALU.add).then_inc(sem("tie count"), 1)
                            for m in range(NC):
                                f = halves[m // (NC // 2)][:, (m % (NC // 2)) * CHUNK:(m % (NC // 2) + 1) * CHUNK]
                                nc.vector.tensor_scalar(compared, f, key, None, ALU.is_lt, ALU.add,
                                                        accum_out=counts[:, 1 + m:2 + m]).then_inc(sem("compared"), 1)
                                dve.wait_ge(sem("compared"), n * NC + m + 1)
                            nc.vector.tensor_scalar(here, here, -0.5, None, ALU.add).then_inc(sem("passed"), 1)
                            dve.wait_ge(sem("passed"), n + 1)
                            dve.wait_ge(sem("tie count"), n + 1)
                            nc.vector.tensor_reduce(rank, counts[:], AX.X, ALU.add).then_inc(sem("rank"), 1)
                            dve.wait_ge(sem("rank"), n + 1)
                            dve.wait_ge(sem("rank free"), n + 1)
                            nc.vector.tensor_copy(rank_i, rank).then_inc(sem("ranked"), 1)

            @block.gpsimd
            def _(pool):
                with pool.If(pool.value_load(unsorted[0:1, 0:1]) != 0):
                    nc.gpsimd.memset(earlier, 1.0).then_inc(sem("order mask"), 1)
                    pool.wait_ge(sem("order mask"), 1)
                    nc.gpsimd.affine_select(out=earlier, in_=earlier, compare_op=ALU.is_gt, fill=0.0,
                                            base=0, pattern=[[-1, P]], channel_multiplier=1).then_inc(sem("order mask"), 1)
                    pool.sem_inc(sem("rank free"), 1)
                    pool.wait_ge(sem("records landed"), 32)
                    for h in range(2):
                        with pool.Fori(0, COLS // 2) as c:
                            n = c + h * (COLS // 2)
                            nc.gpsimd.tensor_copy(record, records[h][:, bass.ds(c, 1), :].rearrange("p a k -> p (a k)")).then_inc(sem("record staged"), 1)
                            pool.wait_ge(sem("record staged"), n + 1)
                            pool.wait_ge(sem("ranked"), n + 1)
                            pool.sem_inc(sem("record turn"), 1)
                            nc.gpsimd.indirect_dma_start(sorted_d, bass.IndirectOffsetOnAxis(ap=rank_i, axis=0), record, None).then_inc(sem("record moved"), 16)
                            pool.wait_ge(sem("record moved"), 16 * n + 16)
                            pool.sem_inc(sem("rank free"), 1)
                    pool.sem_inc(sem("records moved"), 1)


        stage_over()

        taken = [0]

        def rl(name, dt=F32, w=256):
            words = w * (2 if dt == BF16 else 4) // 4
            t = XD[0:RQ, taken[0]:taken[0] + words]
            taken[0] += words
            return t if dt == F32 else t.bitcast(dt)
        r_src, r_typ, r_dst, r_prev, r_next = (rl(n, I32) for n in ("r_src", "r_typ", "r_dst", "r_prev", "r_next"))
        r_att = rl("r_att", F32, 1024)
        r_e = rl("r_e", I32)
        r_sp, r_sn, r_hi, r_lo, r_lim = (rl(n, BF16) for n in ("r_sp", "r_sn", "r_hi", "r_lo", "r_lim"))
        f_src, f_dst, f_sc, f_cnt, f_last = (big[n][0:RQ, 0:256] for n in range(5))
        r_ef, r_st, r_loc = (big[n][0:RQ, 256:512] for n in range(3))
        r_hii, r_loi = (rl(n, I32) for n in ("r_hii", "r_loi"))
        r_rc, r_lg, r_s, r_q, r_rl = (big[n][0:RQ, 512:768] for n in range(5))
        r_ew, r_c0, r_c1, r_c2, r_one = (big[n][0:RQ, 768:1024] for n in range(5))
        carry_row = sb("carry_row", [1, RQ + 1])
        carry_col = sb("carry_col", [RQ, 1])
        nv = big[6][0:125, 0:400]
        nvl = big[7][0:125, 0:400]
        nvs = sb("nvs", [125, 1])
        with nc.Block() as block:
            @block.sync
            def _(sp):
                s = sem("rows loaded")
                for t, d in ((r_src, src_d), (r_typ, typ_d), (r_dst, dst_d[1:EP + 1]), (r_prev, dst_d[0:EP]),
                             (r_next, dst_d[2:EP + 2])):
                    sp.dma_start(t[:], flat(d, RQ)).then_inc(s, 16)
                sp.dma_start(r_att[:], att_d.rearrange("(p c) d -> p (c d)", p=RQ)).then_inc(s, 16)
                sp.dma_start(nv, flat(node_vec, 125)).then_inc(sem("node_vec loaded"), 16)
                w = sem("edge values written")
                sp.wait_ge(sem("flags"), 10)
                sp.dma_start(flat(same_prev_d, RQ), r_sp[:]).then_inc(w, 16)
                sp.dma_start(flat(same_next_d, RQ), r_sn[:]).then_inc(w, 16)
                sp.dma_start(flat(thi_d, RQ), r_hi[:]).then_inc(w, 16)
                sp.dma_start(flat(tlo_d, RQ), r_lo[:]).then_inc(w, 16)
                sp.dma_start(flat(lim_d, RQ), r_lim[:]).then_inc(w, 16)
                sp.wait_ge(sem("components"), 5)
                sp.dma_start(flat(ew_d, RQ), r_ew).then_inc(w, 16)
                for n, t in enumerate((r_c0, r_c1, r_c2, r_one)):
                    sp.dma_start(flat(comp_d[n, :], RQ), t).then_inc(w, 16)
                sp.wait_ge(sem("scalers"), 4)
                sp.dma_start(flat(rcnt_d, RQ), r_rc).then_inc(w, 16)
                sp.dma_start(flat(amp_d, RQ), r_s).then_inc(w, 16)
                sp.dma_start(flat(att_amp_d, RQ), r_q).then_inc(w, 16)
                sp.wait_ge(w, 16 * 13)

            @block.gpsimd
            def _(pool):
                nc.gpsimd.iota(r_e[:], [[1, 256]], base=0, channel_multiplier=256).then_inc(sem("edge numbers"), 1)

            @block.vector
            def _(dve):
                dve.wait_ge(sem("rows loaded"), 96)
                f = sem("flags")
                nc.vector.tensor_tensor(r_sp[:], r_dst[:], r_prev[:], ALU.is_equal).then_inc(f, 1)
                nc.vector.tensor_tensor(r_sn[:], r_dst[:], r_next[:], ALU.is_equal).then_inc(f, 1)
                nc.vector.tensor_scalar(r_hii[:], r_typ[:], 2, None, ALU.logical_shift_right).then_inc(f, 1)
                nc.vector.tensor_scalar(r_loi[:], r_typ[:], 3, None, ALU.bitwise_and).then_inc(f, 1)
                dve.wait_ge(f, 4)
                nc.vector.tensor_copy(r_hi[:], r_hii[:]).then_inc(f, 1)
                nc.vector.tensor_copy(r_lo[:], r_loi[:]).then_inc(f, 1)
                nc.vector.tensor_copy(f_src, r_src[:]).then_inc(f, 1)
                nc.vector.tensor_scalar(f_dst, r_dst[:], float(N - 1), None, ALU.min).then_inc(f, 1)
                nc.vector.tensor_scalar(r_lim[:], r_sp[:], 2 * LIMIT, -LIMIT, ALU.mult, ALU.add).then_inc(f, 1)
                nc.vector.tensor_scalar(f_last, r_sn[:], -1.0, 1.0, ALU.mult, ALU.add).then_inc(f, 1)
                nc.vector.scalar_tensor_tensor(out=f_sc, in0=r_sn[:], scalar=FAR, in1=r_dst[:],
                                               op0=ALU.mult, op1=ALU.add).then_inc(sem("far"), 1)
                c = sem("components")
                av = r_att[:].rearrange("p (e c) -> p e c", c=4)
                nc.vector.tensor_copy(r_ew, av[:, :, 3]).then_inc(c, 1)
                for n, t in enumerate((r_c0, r_c1, r_c2)):
                    nc.vector.tensor_copy(t, av[:, :, n]).then_inc(c, 1)
                nc.vector.memset(r_one, 1.0).then_inc(c, 1)
                q = sem("count steps")
                dve.wait_ge(sem("edge numbers"), 1)
                nc.vector.tensor_copy(r_ef, r_e[:]).then_inc(q, 1)
                nc.vector.tensor_scalar(r_st, r_sp[:], -1.0, 1.0, ALU.mult, ALU.add).then_inc(q, 1)
                dve.wait_ge(q, 2)
                nc.vector.tensor_tensor(r_st, r_st, r_ef, ALU.mult).then_inc(q, 1)
                dve.wait_ge(q, 3)
                nc.vector.tensor_tensor_scan(r_loc, r_st, r_st, 0.0, ALU.max, ALU.max).then_inc(q, 1)
                nc.vector.memset(carry_row[:, 0:1], 0.0).then_inc(q, 1)
                dve.wait_ge(sem("carry turned"), 1)
                dve.wait_ge(q, 5)
                nc.vector.tensor_copy(carry_row[:, 1:RQ + 1], PS[0][0:1, 0:RQ]).then_inc(q, 1)
                dve.wait_ge(q, 6)
                nc.vector.tensor_tensor_scan(carry_row[:, 1:RQ + 1], carry_row[:, 1:RQ + 1], carry_row[:, 1:RQ + 1],
                                             0.0, ALU.max, ALU.max).then_inc(q, 1)
                dve.wait_ge(sem("carry turned"), 2)
                nc.vector.tensor_copy(carry_col[:], PS[1][0:RQ, 0:1]).then_inc(q, 1)
                dve.wait_ge(q, 8)
                nc.vector.tensor_scalar(r_loc, r_loc, carry_col[:, 0:1], None, ALU.max).then_inc(q, 1)
                dve.wait_ge(q, 9)
                nc.vector.tensor_tensor(f_cnt, r_ef, r_loc, ALU.subtract).then_inc(q, 1)
                dve.wait_ge(q, 10)
                nc.vector.tensor_scalar(f_cnt, f_cnt, 1.0, None, ALU.add).then_inc(sem("counts"), 1)
                dve.wait_ge(sem("log sum"), 1)
                nc.vector.tensor_scalar(col(C_AVG), PS[2][:, 0:1], 1.0 / N, None, ALU.mult).then_inc(q, 1)
                dve.wait_ge(q, 11)
                nc.vector.reciprocal(col(C_RAVG), col(C_AVG)).then_inc(q, 1)
                dve.wait_ge(sem("counts"), 1)
                nc.vector.reciprocal(r_rc, f_cnt).then_inc(sem("scalers"), 1)
                dve.wait_ge(sem("log counts"), 1)
                nc.vector.reciprocal(r_rl, r_lg).then_inc(sem("scalers"), 1)
                dve.wait_ge(q, 12)
                nc.vector.tensor_scalar(r_s, r_lg, col(C_RAVG, 0, RQ), None, ALU.mult).then_inc(sem("scalers"), 1)
                dve.wait_ge(sem("scalers"), 3)
                nc.vector.scalar_tensor_tensor(out=r_q, in0=r_rl, scalar=col(C_AVG, 0, RQ), in1=r_s,
                                               op0=ALU.mult, op1=ALU.mult).then_inc(sem("scalers"), 1)
                dve.wait_ge(sem("lists turned"), 10)

                def turned(n, half):
                    return PS[3 + n // 2][:, (n % 2) * 256 + half * 100:(n % 2) * 256 + half * 100 + RQ] \
                        .rearrange("p (a h j) -> p a j h", h=2, j=2)

                def placed(t, half):
                    return t.rearrange("p a (j k h) -> p a j k h", j=2, k=2)[:, :, :, half, :]
                for half in range(2):
                    for n in range(3):
                        nc.vector.tensor_copy(placed(LI[:, :, n, :], half), turned(n, half)).then_inc(sem("lists"), 1)
                    nc.vector.tensor_copy(placed(RCL[:].rearrange("p (a c) -> p a c", c=8), half), turned(3, half)).then_inc(sem("lists"), 1)
                    nc.vector.tensor_copy(placed(LASTF[:].rearrange("p (a c) -> p a c", c=8), half), turned(4, half)).then_inc(sem("lists"), 1)
                dve.wait_ge(sem("lists"), 10)
                nc.vector.reciprocal(RCL[:], RCL[:]).then_inc(sem("lists"), 1)
                dve.wait_ge(sem("lists"), 11)
                nc.vector.tensor_tensor(RCL[:], RCL[:], LASTF[:], ALU.mult)

            @block.scalar
            def _(act):
                load_log_exp(act)
                act.wait_ge(sem("node_vec loaded"), 16)
                nc.scalar.activation(nvl, nv, ACT.Ln, bias=1.0, accum_out=nvs[:]).then_inc(sem("logs"), 1)
                act.wait_ge(sem("counts"), 1)
                nc.scalar.activation(r_lg, f_cnt, ACT.Ln, bias=1.0).then_inc(sem("log counts"), 1)

            @block.tensor
            def _(pe):
                pe.wait_ge(sem("logs"), 1)
                nc.tensor.matmul(PS[2][:, 0:1], ones[0:125, :], nvs[:], start=True, stop=True).then_inc(sem("log sum"), 1)
                pe.wait_ge(sem("count steps"), 4)
                nc.tensor.transpose(PS[0][0:1, 0:RQ], r_loc[:, 255:256], ident[0:RQ, 0:RQ]).then_inc(sem("carry turned"), 1)
                pe.wait_ge(sem("count steps"), 7)
                nc.tensor.transpose(PS[1][0:RQ, 0:1], carry_row[:, 0:RQ], ident[0:1, 0:1]).then_inc(sem("carry turned"), 1)
                pe.wait_ge(sem("flags"), 10)
                pe.wait_ge(sem("far"), 1)
                pe.wait_ge(sem("counts"), 1)
                for n, t in enumerate((f_src, f_dst, f_sc, f_cnt, f_last)):
                    for half in range(2):
                        o = (n % 2) * 256 + half * 100
                        nc.tensor.transpose(PS[3 + n // 2][:, o:o + RQ], t[:, half * P:(half + 1) * P],
                                            ident[0:RQ, 0:RQ]).then_inc(sem("lists turned"), 1)

        stage_over()

        used = [4096]

        def wt(name, a, b):
            t = HH[0:a, used[0]:used[0] + b]
            used[0] += b
            return t
        t_we, t_ws2, t_w3, t_p3, t_wih, t_whh = (wt(n, D, w) for n, w in (
            ("we", 64), ("ws2", 128), ("w3", 64), ("p3", 128), ("wih", 192), ("whh", 192)))
        t_pre = wt("pre", D, 192)
        t_e3 = wt("e3", 4, D)
        t_web, t_post_col = wt("web", D, 1), wt("bpost", D, 1)
        t_std = wt("std", D, 192)
        t_big = [big[n][:, :] for n in range(8)]
        o_mm, o_xx, q_mm, q_xx = t_big[0][:, 0:64], t_big[1][:, 0:64], t_big[2][:, 0:128], t_big[3][:, 0:128]
        t_wet, t_w3t, t_ut = t_big[4][0:D, 0:64], t_big[4][0:D, 64:128], t_big[4][0:D, 128:192]
        t_e3t = t_big[4][0:D, 192:196]
        t_w3p = t_big[5][0:D, 0:192]
        t_gin = t_big[6][0:D, 0:192]
        t_bias = t_big[7][:, 0:16]
        t_co, t_sc = wt("co", D, 1), wt("sc", D, 3)
        NAT = D

        def wpost_rows(scaling, aggregate):
            o = NAT * (1 + 4 * scaling + aggregate)
            return wpost[o:o + NAT, :]
        MEAN, MIN, MAX, STD = range(4)

        def column(v):
            return v.rearrange("(p o) -> p o", o=1)
        loads = []
        for g2 in range(2):
            for k in range(4):
                r0 = 8 * k + 4 * g2
                loads.append((W0S[g2 * D:(g2 + 1) * D, k, :, :], w0[r0:r0 + 4].rearrange("x i o -> i x o")))
        for h in range(2):
            q = slice(h * D, (h + 1) * D)
            loads += [(bd["w1"][q, q], w1), (bd["wr"][q, q], wr_k.rearrange("f h d -> f (h d)")),
                      (bd["we"][q, q], we_k.rearrange("f h d -> f (h d)")),
                      (bd["z"][q, q], wih[:, 64:128]), (bd["r"][q, q], wih[:, 0:64]), (bd["in"][q, q], wih[:, 128:192]),
                      (bd["hz"][q, q], whh[:, 64:128]), (bd["hr"][q, q], whh[:, 0:64]), (bd["hn"][q, q], whh[:, 128:192]),
                      (t_ws2[:, q], ws_k), (t_p3[:, q], wpre[128:192, :])]
            for n, v in enumerate((ws_b, wr_b.rearrange("h d -> (h d)"), we_b.rearrange("h d -> (h d)"), bpre, bpost,
                                   bih[64:128], bhh[64:128], bih[0:64], bhh[0:64], bih[128:192], bhh[128:192])):
                loads.append((t_bias[q, n:n + 1], column(v)))
            loads += [(o_mm[q, :], wpost_rows(0, (MEAN, STD)[h])), (o_xx[q, :], wpost_rows(0, (MAX, MIN)[h]))]
            for n in range(2):
                loads += [(q_mm[q, n * D:(n + 1) * D], wpost_rows(1 + n, (MEAN, STD)[h])),
                          (q_xx[q, n * D:(n + 1) * D], wpost_rows(1 + n, (MAX, MIN)[h]))]
        loads += [(t_we[:], we_k.rearrange("f h d -> f (h d)")), (t_w3[:], w3), (t_wih[:], wih), (t_whh[:], whh),
                  (t_pre[:, 0:64], wpre[0:64, :]), (t_pre[:, 64:128], wpre[64:128, :]), (t_pre[:, 128:192], wpost[0:64, :]),
                  (t_e3[0:3, :], w3e), (t_e3[3:4, :], b3e.rearrange("(o d) -> o d", o=1)),
                  (t_web[:], column(we_b.rearrange("h d -> (h d)"))), (t_post_col[:], column(bpost)),
                  (col(C_WAB), wa_b.rearrange("(o d) -> o d", o=1).broadcast_to([P, 1]))]
        for n in range(3):
            loads.append((t_std[:, n * D:(n + 1) * D], wpost_rows(n, STD)))
        t_wa = wt("wa", P, 1)
        loads += [(t_wa[h * D:(h + 1) * D, :], wa_k) for h in range(2)]
        def map_nodes(k, written):
            for c in range(8):
                nc.gpsimd.indirect_dma_start(where_d, bass.IndirectOffsetOnAxis(ap=ST[k][:, 2, c:c + 1], axis=0),
                                             ST[k][:, 3, c:c + 1], None, bounds_check=N - 1, oob_is_err=False).then_inc(written, 16)

        BLOCKS = ("w1", "wr", "we", "z", "r", "in", "hz", "hr", "hn")
        with nc.Block() as block:
            @block.gpsimd
            def _(pool):
                for t in BLOCKS:
                    nc.gpsimd.memset(bd[t][:], 0.0).then_inc(sem("blocks cleared"), 1)
                for t in ("sumA", "sumB", "wews", "wa", "mmA", "mmB", "xxA", "xxB", "u0",
                          "dz", "dr", "din"):
                    nc.gpsimd.memset(bd[t][:], 0.0).then_inc(sem("products cleared"), 1)
                nc.gpsimd.memset(sel[:], 0.0).then_inc(sem("products cleared"), 1)
                with pool.Fori(0, EARLY // 2) as r:
                    for k in range(2):
                        nc.gpsimd.tensor_copy(ST[k][:, 2:4, :], LI[:, bass.ds(2 * r + k, 1), 2:4, :].rearrange("p a b c -> p (a b) c")).then_inc(sem("map staged"), 1)
                        pool.wait_ge(sem("map staged"), 2 * r + k + 1)
                        pool.sem_inc(sem("map turn"), 1)
                        map_nodes(k, sem(f"map written {k}"))
                    for k in range(2):
                        pool.wait_ge(sem(f"map written {k}"), 128 * r + 128)

            @block.sync
            def _(sp):
                sp.wait_ge(sem("blocks cleared"), len(BLOCKS))
                for t, v in loads[::2]:
                    sp.dma_start(t, v).then_inc(sem("weights loaded"), 16)

            @block.scalar
            def _(act):
                act.wait_ge(sem("blocks cleared"), len(BLOCKS))
                for t, v in loads[1::2]:
                    act.dma_start(t, v).then_inc(sem("weights loaded"), 16)

            @block.tensor
            def _(pe):
                pe.wait_ge(sem("weights loaded"), 16 * len(loads))
                i64 = ident[0:D, 0:D]
                nc.tensor.transpose(PS[0][0:D, 0:64], t_we[:], i64)
                nc.tensor.transpose(PS[0][0:D, 64:128], t_w3[:], i64)
                nc.tensor.transpose(PS[0][0:D, 192:196], t_e3[:], ident[0:4, 0:4]).then_inc(sem("products"), 1)
                pe.wait_ge(sem("factors"), 1)
                nc.tensor.matmul(PS[1][0:D, 0:64], t_wet, t_ws2[:, 0:64], start=True, stop=True)
                nc.tensor.matmul(PS[1][0:D, 64:256], t_w3t, t_pre[:], start=True, stop=True)
                nc.tensor.matmul(PS[1][0:4, 256:384], t_e3t, t_p3[:], start=True, stop=True)
                nc.tensor.matmul(PS[1][:, 384:385], t_ws2[:], t_web[:], start=True, stop=True).then_inc(sem("products"), 1)
                pe.wait_ge(sem("factors"), 2)
                nc.tensor.transpose(PS[2][0:D, 0:64], t_w3p[:, 128:192], i64).then_inc(sem("products"), 1)
                pe.wait_ge(sem("factors"), 3)
                nc.tensor.matmul(PS[3][0:D, 0:192], t_ut, t_wih[:], start=True, stop=True).then_inc(sem("products"), 1)
                for n in range(3):
                    nc.tensor.matmul(PS[4][0:D, 0:1], t_std[:, n * D:(n + 1) * D], t_sc[:, n:n + 1],
                                     start=(n == 0), stop=(n == 2))
                nc.tensor.matmul(PS[5][:, 0:1], ident[:], t_bias[:, 0:1], start=True, stop=True).then_inc(sem("products"), 1)
                pe.wait_ge(sem("factors"), 4)
                for n, g in enumerate((1, 0, 2)):
                    for h in range(2):
                        nc.tensor.matmul(PS[6][h * D:(h + 1) * D, n:n + 1], t_wih[:, g * D:(g + 1) * D], t_co[:],
                                         start=True, stop=True).then_inc(sem("empty gates"), 1)

            @block.vector
            def _(dve):
                f = sem("factors")
                b = sem("stationaries")
                nc.vector.memset(col(C_EPS), EPS).then_inc(sem("constants"), 1)
                nc.vector.memset(col(C_NLIM), -LIMIT).then_inc(sem("constants"), 1)
                nc.vector.memset(col(C_ONE), 1.0).then_inc(sem("constants"), 1)
                nc.vector.memset(col(C_TWO), 2.0).then_inc(sem("constants"), 1)
                nc.vector.memset(col(C_EMPTY), EPS ** 0.5).then_inc(sem("constants"), 1)
                nc.vector.memset(col(C_SGN, 0, D), 1.0).then_inc(sem("constants"), 1)
                nc.vector.memset(col(C_SGN, D, P), -1.0).then_inc(sem("constants"), 1)
                for h in range(2):
                    for k in range(4):
                        nc.vector.memset(col(C_G0 + k, h * D, (h + 1) * D), float(2 * k + h)).then_inc(sem("constants"), 1)
                    for m in range(2):
                        nc.vector.memset(col(C_L0 + m, h * D, (h + 1) * D), float(2 * m + h)).then_inc(sem("constants"), 1)
                dve.wait_ge(sem("constants"), 19)
                dve.wait_ge(sem("products"), 1)
                nc.vector.tensor_copy(t_big[4][0:D, 0:128], PS[0][0:D, 0:128]).then_inc(b, 1)
                nc.vector.tensor_copy(t_e3t, PS[0][0:D, 192:196]).then_inc(f, 1)
                nc.vector.tensor_copy(t_sc[:, 0:1], col(C_EMPTY, 0, D)).then_inc(b, 1)
                dve.wait_ge(b, 2)
                import math
                ln2 = math.log(2.0)
                nc.vector.scalar_tensor_tensor(out=t_sc[:, 1:2], in0=col(C_RAVG, 0, D), scalar=ln2, in1=t_sc[:, 0:1],
                                               op0=ALU.mult, op1=ALU.mult).then_inc(b, 1)
                dve.wait_ge(b, 3)
                nc.vector.scalar_tensor_tensor(out=t_sc[:, 2:3], in0=col(C_AVG, 0, D), scalar=1.0 / ln2, in1=t_sc[:, 1:2],
                                               op0=ALU.mult, op1=ALU.mult).then_inc(b, 1)
                dve.wait_ge(sem("products"), 2)
                nc.vector.tensor_copy(t_w3p, PS[1][0:D, 64:256]).then_inc(f, 1)
                dve.wait_ge(sem("products cleared"), 13)
                for h in range(2):
                    q = slice(h * D, (h + 1) * D)
                    i64 = ident[q, q]
                    nc.vector.tensor_copy(bd["wews"][q, q], PS[1][0:D, 0:64]).then_inc(b, 1)
                    for n in range(2):
                        c = slice(n * D, (n + 1) * D)
                        nc.vector.tensor_copy(bd["ends"][q, c], PS[1][0:D, (128, 64)[h]:(192, 128)[h]]).then_inc(b, 1)
                    nc.vector.tensor_copy(bd["u0"][q, q], PS[1][0:D, 192:256]).then_inc(b, 1)
                    nc.vector.tensor_copy(bd["sumA"][q, 0:D], i64).then_inc(b, 1)
                    nc.vector.tensor_copy(bd["sumB"][q, D:P], i64).then_inc(b, 1)
                    nc.vector.tensor_copy(sel[h * D:h * D + 1, h:h + 1], ones[h * D:h * D + 1, 0:1]).then_inc(b, 1)
                    nc.vector.tensor_copy(bd["wa"][q, q], t_wa[q, 0:1].broadcast_to([D, D])).then_inc(b, 1)
                nc.vector.tensor_copy(attw[:], PS[1][0:4, 256:384]).then_inc(b, 1)
                nc.vector.tensor_copy(bd["mmA"][:, 0:D], o_mm).then_inc(b, 1)
                nc.vector.tensor_copy(bd["mmB"][:, D:P], o_mm).then_inc(b, 1)
                nc.vector.tensor_copy(bd["mq"][:], q_mm).then_inc(b, 1)
                nc.vector.tensor_scalar(bd["xxA"][:, 0:D], o_xx, col(C_SGN), None, ALU.mult).then_inc(b, 1)
                nc.vector.tensor_scalar(bd["xxB"][:, D:P], o_xx, col(C_SGN), None, ALU.mult).then_inc(b, 1)
                nc.vector.tensor_scalar(bd["xq"][:], q_xx, col(C_SGN), None, ALU.mult).then_inc(b, 1)
                nc.vector.tensor_tensor(col(C_ATT), PS[1][:, 384:385], t_bias[:, 0:1], ALU.add).then_inc(b, 1)
                dve.wait_ge(b, 4 + 16 + 8)
                nc.vector.tensor_tensor(col(C_ATT), col(C_ATT), t_bias[:, 1:2], ALU.add).then_inc(b, 1)
                nc.vector.tensor_copy(col(C_WEB), t_bias[:, 2:3]).then_inc(b, 1)
                nc.vector.tensor_copy(col(C_PRE), t_bias[:, 3:4]).then_inc(b, 1)
                nc.vector.tensor_scalar(col(C_SPRE), t_bias[:, 3:4], col(C_SGN), None, ALU.mult).then_inc(b, 1)
                nc.vector.tensor_copy(col(C_POST), t_bias[:, 4:5]).then_inc(b, 1)
                nc.vector.tensor_tensor(col(C_Z), t_bias[:, 5:6], t_bias[:, 6:7], ALU.add).then_inc(b, 1)
                nc.vector.tensor_tensor(col(C_R), t_bias[:, 7:8], t_bias[:, 8:9], ALU.add).then_inc(b, 1)
                nc.vector.tensor_copy(col(C_IN), t_bias[:, 9:10]).then_inc(b, 1)
                nc.vector.tensor_copy(col(C_HN), t_bias[:, 10:11]).then_inc(b, 1)
                dve.wait_ge(sem("products"), 3)
                nc.vector.tensor_copy(t_ut, PS[2][0:D, 0:64]).then_inc(f, 1)
                dve.wait_ge(sem("products"), 4)
                nc.vector.tensor_copy(t_gin, PS[3][0:D, 0:192]).then_inc(b, 1)
                dve.wait_ge(sem("products"), 5)
                nc.vector.tensor_tensor(t_co[:], PS[4][0:D, 0:1], t_post_col[:], ALU.add).then_inc(f, 1)
                dve.wait_ge(b, 4 + 16 + 8 + 10)
                for h in range(2):
                    q = slice(h * D, (h + 1) * D)
                    nc.vector.tensor_tensor(t_big[7][0:D, 64 + 192 * h:128 + 192 * h], t_gin[:, 64:128], t_whh[:, 64:128], ALU.add).then_inc(b, 1)
                    nc.vector.tensor_tensor(t_big[7][0:D, 128 + 192 * h:192 + 192 * h], t_gin[:, 0:64], t_whh[:, 0:64], ALU.add).then_inc(b, 1)
                    dve.wait_ge(b, 38 + 5 * h + 2)
                    nc.vector.tensor_copy(bd["dz"][q, q], t_big[7][0:D, 64 + 192 * h:128 + 192 * h]).then_inc(b, 1)
                    nc.vector.tensor_copy(bd["dr"][q, q], t_big[7][0:D, 128 + 192 * h:192 + 192 * h]).then_inc(b, 1)
                    nc.vector.tensor_copy(bd["din"][q, q], t_gin[:, 128:192]).then_inc(b, 1)
                dve.wait_ge(sem("empty gates"), 6)
                for n, (o, i) in enumerate(((C_DZ, C_Z), (C_DR, C_R), (C_DIN, C_IN))):
                    nc.vector.tensor_tensor(col(o), PS[6][:, n:n + 1], col(i), ALU.add)

        stage_over()

        TY = [sb(f"TY{k}", [P, 2, 1024], BF16) for k in range(2)]
        FL = [sb(f"FL{k}", [P, 512], BF16) for k in range(2)]
        S = sb("S", [P, 512])
        CR = sb("CR", [P, 2])
        MASKED = [[big[2 * h + k // 2][:, (k % 2) * 512:(k % 2 + 1) * 512] for k in range(4)] for h in range(2)]
        CHOSEN = [[big[4 + h][:, m * 512:(m + 1) * 512] for m in range(2)] for h in range(2)]

        def load_flags(sp, t, flags, i, name):
            for h in range(2):
                sp.dma_start(t[h * D:(h + 1) * D, :],
                             flags[bass.ds(i * PAIR + h * HALF, HALF)].rearrange("(o c) -> o c", o=1)
                             .broadcast_to([D, HALF])).then_inc(sem(name), 16)

        def ln_sum(dve, t, k, name, i, bias=False):
            v = t
            if bias:
                nc.vector.tensor_tensor(Y[k][:], t, bcd(CB[:]), ALU.add).then_inc(sem(name + " y"), 1)
                dve.wait_ge(sem(name + " y"), i + 1)
                v = Y[k][:]
            nc.vector.tensor_reduce(SM[k][:, 0, :], v, AX.X, ALU.add).then_inc(sem(name + " sum"), 1)
            dve.wait_ge(sem(name + " sum"), i + 1)
            nc.vector.scalar_tensor_tensor(out=XC[k][:], in0=bc8(SM[k][:, 0, :]), scalar=-1.0 / D, in1=v,
                                           op0=ALU.mult, op1=ALU.add).then_inc(sem(name + " centred"), 1)

        def ln_square(act, k, name, i):
            act.wait_ge(sem(name + " centred"), i + 1)
            nc.scalar.activation(SQ[k][:], XC[k][:], ACT.Square).then_inc(sem(name + " squares"), 1)

        def ln_var(dve, k, name, i):
            dve.wait_ge(sem(name + " squares"), i + 1)
            nc.vector.tensor_reduce(SM[k][:, 1, :], SQ[k][:], AX.X, ALU.add).then_inc(sem(name + " var"), 1)

        def ln_rstd(act, k, name, i):
            act.wait_ge(sem(name + " var"), i + 1)
            nc.scalar.activation(SM[k][:, 2, :], SM[k][:, 1, :], ACT.Ln, scale=1.0 / D, bias=col(C_EPS)).then_inc(sem(name + " log"), 1)
            act.wait_ge(sem(name + " log"), i + 1)
            nc.scalar.activation(SM[k][:, 3, :], SM[k][:, 2, :], ACT.Exp, scale=-0.5).then_inc(sem(name + " rstd"), 1)

        def ln_out(dve, k, name, i, twice=False):
            dve.wait_ge(sem(name + " rstd"), i + 1)
            for c in range(2 if twice else 1):
                nc.vector.scalar_tensor_tensor(out=H[k][:, :, c, :] if twice else H[k][:].rearrange("p a b d -> p (a b d)")[:, 0:512].rearrange("p (c d) -> p c d", d=D),
                                               in0=XC[k][:], scalar=0.0, in1=bc8(SM[k][:, 3, :]),
                                               op0=ALU.max, op1=ALU.mult).then_inc(sem(name + " h"), 1)

        def hrow(k, j):
            return H[k][:].rearrange("p a b d -> p (a b d)")[:, j * P:(j + 1) * P]

        def scan_pair(dve, out, flags, data, carry, name, n):
            for h in range(2):
                q = slice(h * D, (h + 1) * D)
                o = slice((1 - h) * D, (2 - h) * D)
                nc.vector.tensor_tensor_scan(out[q, :], flags[q, :], data[q, :], carry[q, 0:1], ALU.mult, ALU.add).then_inc(sem(name), 1)
                dve.wait_ge(sem(name), n + 2 * h + 1)
                nc.vector.tensor_copy(carry[o, 0:1], out[q, 511:512]).then_inc(sem(name), 1)
                dve.wait_ge(sem(name), n + 2 * h + 2)

        with nc.Block() as block:
            @block.scalar
            def _(act):
                load_log_exp(act)
                def stage(i, k):
                    nc.scalar.activation(ST[k][:], LI[:, bass.ds(i, 1), :, :].rearrange("p a b c -> p (a b) c"), ACT.Copy).then_inc(sem("l0 staged"), 1)
                stage(0, 0)
                stage(1, 1)
                ln_square(act, 0, "l0", 0)
                ln_rstd(act, 0, "l0", 0)

                def body(i, r, k, mapped=True):
                    if exists(i + 1):
                        ln_square(act, 1 - k, "l0", i + 1)
                        ln_rstd(act, 1 - k, "l0", i + 1)
                    if exists(i + 2):
                        act.wait_ge(sem("l0 x1"), i + 1)
                        if mapped:
                            act.wait_ge(sem(f"l0 where written {k}"), 128 * (r - EARLY // 2) + 128)
                        stage(i + 2, k)
                with act.Fori(0, EARLY // 2) as r:
                    body(2 * r, r, 0, mapped=False)
                    body(2 * r + 1, r, 1, mapped=False)
                rounds(act, body, first=EARLY)

            @block.gpsimd
            def _(pool):
                def body(i, r, k, mapped=True):
                    pool.wait_ge(sem("l0 staged"), i + 1)
                    pool.sem_inc(sem("l0 turn"), 1)
                    for c in range(8):
                        nc.gpsimd.indirect_dma_start(G[k][:, c, :], None, x, bass.IndirectOffsetOnAxis(ap=ST[k][:, 0, c:c + 1], axis=0)).then_inc(sem(f"l0 src landed {k}"), 16)
                    for c in range(8):
                        nc.gpsimd.indirect_dma_start(XG[k][:, c, :], None, x, bass.IndirectOffsetOnAxis(ap=ST[k][:, 1, c:c + 1], axis=0)).then_inc(sem(f"l0 dst landed {k}"), 16)
                    if mapped:
                        map_nodes(k, sem(f"l0 where written {k}"))
                with pool.Fori(0, EARLY // 2) as r:
                    body(2 * r, r, 0, mapped=False)
                    body(2 * r + 1, r, 1, mapped=False)
                rounds(pool, body, first=EARLY)
                for k in range(2):
                    pool.wait_ge(sem(f"l0 where written {k}"), 128 * ((NPAIR + 1 - k) // 2 - EARLY // 2))

            @block.sync
            def _(sp):
                def load(i, k):
                    for n, t in enumerate((thi_d, tlo_d)):
                        sp.dma_start(TY[k][:, n, :], t[bass.ds(i * PAIR, PAIR)].rearrange("(o c) -> o c", o=1).broadcast_to([P, PAIR])).then_inc(sem(f"l0 types landed {k}"), 16)
                    load_flags(sp, FL[k], same_prev_d, i, f"l0 flags landed {k}")
                load(0, 0)
                load(1, 1)

                def body(i, r, k):
                    for t in (ta, tb):
                        sp.dma_start(node_rows(t, i), node_rows(x, i)).then_inc(sem("tables filled"), 16)
                    sp.wait_ge(sem("l0 x1"), i + 1)
                    sp.dma_start(edge_rows(ta, i), XD[:, bass.ds(i * 512, 512)]).then_inc(sem("l0 rows written"), 16)
                    if exists(i + 2):
                        load(i + 2, k)
                rounds(sp, body)
                sp.wait_ge(sem("l0 rows written"), 16 * NPAIR)
                sp.wait_ge(sem("tables filled"), 32 * NPAIR)

            @block.tensor
            def _(pe):
                def body(i, r, k):
                    pe.wait_ge(sem("l0 h"), 2 * i + 2)
                    for h in range(2):
                        for j in range(4):
                            ins = nc.tensor.transpose(PS[h][:, j * P:(j + 1) * P],
                                                      H[k][:, 2 * j + h, :, :].rearrange("p b d -> p (b d)"), ident[:])
                        ins.then_inc(sem("l0 turned"), 1)
                    for h in range(2):
                        pe.wait_ge(sem("l0 masked"), 8 * i + 4 * h + 4)
                        for m in range(2):
                            for g in range(4):
                                ins = nc.tensor.matmul(PS[2 + 2 * h + m][:], W0S[:, g, 2 * m:2 * m + 2, :].rearrange("p l o -> p (l o)"),
                                                       MASKED[h][g], start=(g == 0), stop=(g == 3))
                        ins.then_inc(sem("l0 products"), 1)
                    for h in range(2):
                        pe.wait_ge(sem("l0 chosen"), 4 * i + 2 * h + 2)
                        for m in range(2):
                            ins = nc.tensor.matmul(PS[6][:], bd[("sumA", "sumB")[h]][:], CHOSEN[h][m],
                                                   start=(h + m == 0), stop=(h + m == 2))
                    ins.then_inc(sem("l0 messages"), 1)
                    pe.wait_ge(sem("l0 scanned"), 4 * i + 4)
                    for j in range(4):
                        ins = nc.tensor.transpose(PS[7][:, j * P:(j + 1) * P], S[:, j * P:(j + 1) * P], ident[:])
                    ins.then_inc(sem("l0 sums back"), 1)
                rounds(pe, body)

            @block.vector
            def _(dve):
                nc.vector.memset(CR[:], 0.0).then_inc(sem("l0 carry clear"), 1)
                dve.wait_ge(sem("l0 src landed 0"), 128)
                ln_sum(dve, G[0][:], 0, "l0", 0)
                ln_var(dve, 0, "l0", 0)
                ln_out(dve, 0, "l0", 0, twice=True)

                def body(i, r, k):
                    nk, nr = 1 - k, r + k
                    dve.wait_ge(sem(f"l0 types landed {k}"), 32 * r + 32)
                    for h in range(2):
                        dve.wait_ge(sem("l0 turned"), 2 * i + h + 1)
                        for g in range(4):
                            nc.vector.scalar_tensor_tensor(out=MASKED[h][g], in0=TY[k][:, 0, h * 512:(h + 1) * 512],
                                                           scalar=col(C_G0 + g), in1=PS[h][:],
                                                           op0=ALU.is_equal, op1=ALU.mult).then_inc(sem("l0 masked"), 1)
                    if exists(i + 1):
                        dve.wait_ge(sem(f"l0 src landed {nk}"), 128 * nr + 128)
                        ln_sum(dve, G[nk][:], nk, "l0", i + 1)
                    for h in range(2):
                        dve.wait_ge(sem("l0 products"), 2 * i + h + 1)
                        for m in range(2):
                            nc.vector.scalar_tensor_tensor(out=CHOSEN[h][m], in0=TY[k][:, 1, h * 512:(h + 1) * 512],
                                                           scalar=col(C_L0 + m), in1=PS[2 + 2 * h + m][:],
                                                           op0=ALU.is_equal, op1=ALU.mult).then_inc(sem("l0 chosen"), 1)
                        if h == 0 and exists(i + 1):
                            ln_var(dve, nk, "l0", i + 1)
                    if exists(i + 1):
                        ln_out(dve, nk, "l0", i + 1, twice=True)
                    dve.wait_ge(sem("l0 messages"), i + 1)
                    dve.wait_ge(sem(f"l0 flags landed {k}"), 32 * r + 32)
                    scan_pair(dve, S, FL[k], PS[6], CR, "l0 scanned", 4 * i)
                    dve.wait_ge(sem("l0 sums back"), i + 1)
                    dve.wait_ge(sem(f"l0 dst landed {k}"), 128 * r + 128)
                    nc.vector.tensor_tensor(rows(XD[:, bass.ds(i * 512, 512)]), rows(PS[7][:]), XG[k][:], ALU.add).then_inc(sem("l0 x1"), 1)
                rounds(dve, body)

        stage_over()

        U = [XG[k][:] for k in range(2)]
        EX = [big[k][:, 0:512] for k in range(2)]
        RU = [big[k][:, 512:1024] for k in range(2)]
        H2 = [big[2 + k][:, 0:512] for k in range(2)]

        def gather_stage(act, i, k, name):
            nc.scalar.activation(ST[k][:, 0, :], IX[:, bass.ds(i * 8, 8)], ACT.Copy).then_inc(sem(name + " staged"), 1)

        def gather(pool, i, k, name, table):
            pool.wait_ge(sem(name + " staged"), i + 1)
            pool.sem_inc(sem(name + " turn"), 1)
            for c in range(8):
                nc.gpsimd.indirect_dma_start(G[k][:, c, :], None, table, bass.IndirectOffsetOnAxis(ap=ST[k][:, 0, c:c + 1], axis=0)).then_inc(sem(f"{name} landed {k}"), 16)

        def turn_rows(pe, k, i, name, out):
            for j in range(4):
                ins = nc.tensor.transpose(out[:, j * P:(j + 1) * P], hrow(k, j), ident[:])
            ins.then_inc(sem(name + " turned"), 1)

        with nc.Block() as block:
            @block.gpsimd
            def _(pool):
                def find(i, k):
                    pool.wait_ge(sem("l1 sources"), i + 1)
                    pool.sem_inc(sem("l1 find turn"), 1)
                    for c in range(8):
                        nc.gpsimd.indirect_dma_start(MG[k][:, c:c + 1], None, where_d, bass.IndirectOffsetOnAxis(ap=ST[k][:, 1, c:c + 1], axis=0)).then_inc(sem(f"l1 found {k}"), 16)
                find(0, 0)
                find(1, 1)

                def body(i, r, k):
                    gather(pool, i, k, "l1", ta)
                    if exists(i + 2):
                        find(i + 2, k)
                rounds(pool, body)

            @block.sync
            def _(sp):
                load_flags(sp, FL[0], same_prev_d, 0, "l1 flags landed 0")
                load_flags(sp, FL[1], same_prev_d, 1, "l1 flags landed 1")

                def body(i, r, k):
                    if exists(i + 2):
                        sp.wait_ge(sem("l1 scanned"), 4 * i + 4)
                        load_flags(sp, FL[k], same_prev_d, i + 2, f"l1 flags landed {k}")
                rounds(sp, body)

            @block.scalar
            def _(act):
                load_log_exp(act)
                def sources(i, k):
                    nc.scalar.activation(ST[k][:, 1, :], LI[:, bass.ds(i, 1), 0, :].rearrange("p a c -> p (a c)"), ACT.Copy).then_inc(sem("l1 sources"), 1)

                def found(i, n, k):
                    act.wait_ge(sem(f"l1 found {k}"), 128 * n + 128)
                    nc.scalar.activation(IX[:, bass.ds(i * 8, 8)], MG[k][:], ACT.Copy).then_inc(sem("l1 found kept"), 1)
                    nc.scalar.activation(ST[k][:, 0, :], MG[k][:], ACT.Copy).then_inc(sem("l1 staged"), 1)
                sources(0, 0)
                sources(1, 1)
                found(0, 0, 0)
                sources(2, 0)
                found(1, 0, 1)
                ln_square(act, 0, "l1", 0)
                ln_rstd(act, 0, "l1", 0)

                def body(i, r, k):
                    if exists(i + 3):
                        sources(i + 3, 1 - k)
                    if exists(i + 2):
                        found(i + 2, r + 1, k)
                    if exists(i + 1):
                        ln_square(act, 1 - k, "l1", i + 1)
                        ln_rstd(act, 1 - k, "l1", i + 1)
                    act.wait_ge(sem("l1 u"), i + 1)
                    nc.scalar.activation(rows(EX[k]), U[k], ACT.Exp).then_inc(sem("l1 exp"), 1)
                    act.wait_ge(sem("l1 elu"), i + 1)
                    nc.scalar.activation(H2[k], HH[:, bass.ds(i * 512, 512)], ACT.Square).then_inc(sem("l1 squared"), 1)
                rounds(act, body)

            @block.tensor
            def _(pe):
                def total(ps, rhs, first, last):
                    return nc.tensor.matmul(ps[:], ones[:], rhs, start=first, stop=last, skip_group_check=True)
                pe.wait_ge(sem("l1 zeros"), 1)
                total(PS[4], H2[0], True, False)
                total(PS[5], H2[0], True, False).then_inc(sem("l1 sums open"), 1)

                def body(i, r, k):
                    pe.wait_ge(sem("l1 h"), i + 1)
                    turn_rows(pe, k, i, "l1", PS[0])
                    pe.wait_ge(sem("l1 scanned"), 4 * i + 4)
                    for j in range(4):
                        ins = nc.tensor.matmul(PS[1][:, j * P:(j + 1) * P], S[:, j * P:(j + 1) * P], bd["w1"][:], start=True, stop=True)
                    ins.then_inc(sem("l1 products"), 1)
                    last = isinstance(i, int) and i == NPAIR - 1
                    pe.wait_ge(sem("l1 elu"), i + 1)
                    total(PS[4], HH[:, bass.ds(i * 512, 512)], False, last)
                    pe.wait_ge(sem("l1 squared"), i + 1)
                    total(PS[5], H2[k], False, last).then_inc(sem("l1 summed"), 1)
                rounds(pe, body)

            @block.vector
            def _(dve):
                nc.vector.memset(CR[:], 0.0).then_inc(sem("l1 carry clear"), 1)
                nc.vector.memset(H2[0], 0.0).then_inc(sem("l1 zeros"), 1)
                dve.wait_ge(sem("l1 landed 0"), 128)
                ln_sum(dve, G[0][:], 0, "l1", 0)
                ln_var(dve, 0, "l1", 0)
                ln_out(dve, 0, "l1", 0)
                dve.wait_ge(sem("l1 sums open"), 1)

                def body(i, r, k):
                    nk, nr = 1 - k, r + k
                    more = exists(i + 1)
                    if more:
                        dve.wait_ge(sem(f"l1 landed {nk}"), 128 * nr + 128)
                        ln_sum(dve, G[nk][:], nk, "l1", i + 1)
                    dve.wait_ge(sem("l1 turned"), i + 1)
                    dve.wait_ge(sem(f"l1 flags landed {k}"), 32 * r + 32)
                    scan_pair(dve, S, FL[k], PS[0], CR, "l1 scanned", 4 * i)
                    if more:
                        ln_var(dve, nk, "l1", i + 1)
                    dve.wait_ge(sem("l1 products"), i + 1)
                    nc.vector.tensor_tensor(U[k], rows(PS[1][:]), bc8(RCL[:, bass.ds(i * 8, 8)]), ALU.mult).then_inc(sem("l1 u"), 1)
                    if more:
                        ln_out(dve, nk, "l1", i + 1)
                    dve.wait_ge(sem("l1 u"), i + 1)
                    nc.vector.tensor_scalar(rows(RU[k]), U[k], 0.0, -1.0, ALU.max, ALU.add).then_inc(sem("l1 relu"), 1)
                    dve.wait_ge(sem("l1 exp"), i + 1)
                    dve.wait_ge(sem("l1 relu"), i + 1)
                    nc.vector.scalar_tensor_tensor(out=HH[:, bass.ds(i * 512, 512)], in0=EX[k], scalar=1.0, in1=RU[k],
                                                   op0=ALU.min, op1=ALU.add).then_inc(sem("l1 elu"), 1)
                rounds(dve, body)

        gb = big[0][:, 0:128]
        bn = big[1][:, 0:64 * 8]
        with nc.Block() as block:
            @block.sync
            def _(sp):
                sp.dma_start(gb[:, 0:D], gamma.rearrange("(o d) -> o d", o=1).broadcast_to([P, D])).then_inc(sem("bn loaded"), 16)
                sp.dma_start(gb[:, D:2 * D], beta.rearrange("(o d) -> o d", o=1).broadcast_to([P, D])).then_inc(sem("bn loaded"), 16)

            @block.scalar
            def _(act):
                load_log_exp(act)
                act.wait_ge(sem("bn steps"), 6)
                nc.scalar.activation(bn[:, 320:384], bn[:, 256:320], ACT.Ln, bias=col(C_EPS)).then_inc(sem("bn rstd"), 1)
                act.wait_ge(sem("bn rstd"), 1)
                nc.scalar.activation(bn[:, 384:448], bn[:, 320:384], ACT.Exp, scale=-0.5).then_inc(sem("bn rstd"), 1)

            @block.tensor
            def _(pe):
                pe.wait_ge(sem("bn steps"), 9)
                for h in range(2):
                    nc.tensor.matmul(PS[0][h * D:(h + 1) * D, 0:1], CB[0:1, :], ones[0:1, 0:1], start=True, stop=True).then_inc(sem("c turned"), 1)

            @block.vector
            def _(dve):
                q = sem("bn steps")
                m, m2, sq, v = (bn[:, n * D:(n + 1) * D] for n in range(4))
                nc.vector.tensor_reduce(m, PS[4][:].rearrange("p (c d) -> p d c", d=D), AX.X, ALU.add).then_inc(q, 1)
                nc.vector.tensor_reduce(m2, PS[5][:].rearrange("p (c d) -> p d c", d=D), AX.X, ALU.add).then_inc(q, 1)
                dve.wait_ge(q, 2)
                nc.vector.tensor_scalar(m, m, 1.0 / N, None, ALU.mult).then_inc(q, 1)
                dve.wait_ge(q, 3)
                nc.vector.tensor_tensor(sq, m, m, ALU.mult).then_inc(q, 1)
                dve.wait_ge(q, 4)
                nc.vector.scalar_tensor_tensor(out=v, in0=m2, scalar=1.0 / N, in1=sq, op0=ALU.mult, op1=ALU.subtract).then_inc(q, 1)
                dve.wait_ge(q, 5)
                nc.vector.tensor_scalar(bn[:, 256:320], v, 0.0, None, ALU.max).then_inc(q, 1)
                dve.wait_ge(sem("bn rstd"), 2)
                y, yy, half_v = bn[:, 384:448], bn[:, 448:512], bn[:, 256:320]
                n = sem("bn newton")
                nc.vector.tensor_scalar(half_v, half_v, EPS, -0.5, ALU.add, ALU.mult).then_inc(n, 1)
                nc.vector.tensor_tensor(yy, y, y, ALU.mult).then_inc(n, 1)
                dve.wait_ge(n, 2)
                nc.vector.tensor_tensor(yy, yy, half_v, ALU.mult).then_inc(n, 1)
                dve.wait_ge(n, 3)
                nc.vector.scalar_tensor_tensor(out=y, in0=yy, scalar=1.5, in1=y, op0=ALU.add, op1=ALU.mult).then_inc(n, 1)
                dve.wait_ge(n, 4)
                dve.wait_ge(sem("bn loaded"), 32)
                nc.vector.tensor_tensor(AB[:], y, gb[:, 0:D], ALU.mult).then_inc(q, 1)
                dve.wait_ge(q, 7)
                nc.vector.tensor_tensor(sq, m, AB[:], ALU.mult).then_inc(q, 1)
                dve.wait_ge(q, 8)
                nc.vector.tensor_tensor(CB[:], gb[:, D:2 * D], sq, ALU.subtract).then_inc(q, 1)
                dve.wait_ge(sem("c turned"), 2)
                nc.vector.tensor_copy(col(C_C), PS[0][:, 0:1])

                dve.wait_ge(q, 9)

        def spread(name, make_z=False):
            stage_over()
            with nc.Block() as block:
                @block.gpsimd
                def _(pool):
                    def body(i, r, k):
                        down = i * -1 + (NPAIR - 1)
                        xd = rows(XD[:, bass.ds(down * 512, 512)])
                        if make_z:
                            nc.gpsimd.tensor_tensor(ZT[:], rows(HH[:, bass.ds(down * 512, 512)]), bcd(AB[:]), ALU.mult).then_inc(sem(name + " ah"), 1)
                            pool.wait_ge(sem(name + " ah"), i + 1)
                            pool.sem_inc(sem(name + " pool turn"), 1)
                            nc.gpsimd.tensor_tensor(xd, xd, ZT[:], ALU.add).then_inc(sem(name + " z"), 1)
                            pool.wait_ge(sem(name + " z"), i + 1)
                        else:
                            pool.wait_ge(sem(name + " y free"), i + 1)
                            pool.sem_inc(sem(name + " pool turn"), 1)
                            nc.gpsimd.tensor_tensor(Y[k][:], xd, bcd(CB[:]), ALU.add).then_inc(sem(name + " y"), 1)
                    if not make_z:
                        pool.sem_inc(sem(name + " y free"), 2)
                    rounds(pool, body)

                @block.sync
                def _(sp):
                    def store(i):
                        down = i * -1 + (NPAIR - 1)
                        sp.wait_ge(sem(name + " z"), i + 1)
                        sp.dma_start(edge_rows(ta, down), XD[:, bass.ds(down * 512, 512)]).then_inc(sem(name + " z written"), 16)
                    load_flags(sp, FL[0], same_next_d, NPAIR - 1, name + " flags landed 0")
                    load_flags(sp, FL[1], same_next_d, NPAIR - 2, name + " flags landed 1")

                    def body(i, r, k):
                        if make_z:
                            store(i)
                        if exists(i + 2):
                            down = i * -1 + (NPAIR - 3)
                            sp.wait_ge(sem(name + " spread"), 4 * i + 4)
                            load_flags(sp, FL[k], same_next_d, down, f"{name} flags landed {k}")
                    rounds(sp, body)
                    if make_z:
                        sp.wait_ge(sem(name + " z written"), 16 * NPAIR)

                @block.scalar
                def _(act):
                    load_log_exp(act)
                    act.sem_inc(sem(name + " kept"), 2)
                    ln_square(act, 0, name, 0)
                    ln_rstd(act, 0, name, 0)

                    def body(i, r, k):
                        down = i * -1 + (NPAIR - 1)
                        if exists(i + 1):
                            ln_square(act, 1 - k, name, i + 1)
                            ln_rstd(act, 1 - k, name, i + 1)
                        act.wait_ge(sem(name + " spread"), 4 * i + 4)
                        nc.scalar.activation(HH[:, bass.ds(down * 512, 512)], big[k][:, 0:512], ACT.Copy).then_inc(sem(name + " kept"), 1)
                    rounds(act, body)

                @block.tensor
                def _(pe):
                    def body(i, r, k):
                        pe.wait_ge(sem(name + " h"), i + 1)
                        turn_rows(pe, k, i, name, PS[k])
                    rounds(pe, body)

                @block.vector
                def _(dve):
                    def centre(i, k, at):
                        if make_z:
                            dve.wait_ge(sem(name + " z"), i + 1)
                            ln_sum(dve, rows(XD[:, bass.ds(at, 512)]), k, name, i, bias=True)
                        else:
                            dve.wait_ge(sem(name + " y"), i + 1)
                            ln_sum(dve, Y[k][:], k, name, i)
                            dve.wait_ge(sem(name + " centred"), i + 1)
                            dve.sem_inc(sem(name + " y free"), 1)

                    def normed(i, k, last):
                        dve.wait_ge(sem(name + " rstd"), i + 1)
                        nc.vector.tensor_tensor(SM[k][:, 3, :], SM[k][:, 3, :], LASTF[:, bass.ds(last, 8)], ALU.mult).then_inc(sem(name + " last"), 1)
                        dve.wait_ge(sem(name + " last"), i + 1)
                        ln_out(dve, k, name, i)
                    nc.vector.memset(CR[:], 0.0).then_inc(sem(name + " carry clear"), 1)
                    centre(0, 0, (NPAIR - 1) * 512)
                    ln_var(dve, 0, name, 0)
                    normed(0, 0, (NPAIR - 1) * 8)
                    dve.wait_ge(sem(name + " carry clear"), 1)

                    def body(i, r, k):
                        nk = 1 - k
                        more = exists(i + 1)
                        down = i * -1 + (NPAIR - 1)
                        if more:
                            centre(i + 1, nk, (down - 1) * 512)
                        dve.wait_ge(sem(name + " turned"), i + 1)
                        dve.wait_ge(sem(f"{name} flags landed {k}"), 32 * r + 32)
                        dve.wait_ge(sem(name + " kept"), i + 1)
                        for n, h in enumerate((1, 0)):
                            q = slice(h * D, (h + 1) * D)
                            o = slice((1 - h) * D, (2 - h) * D)
                            out = big[k][q, 0:512]
                            nc.vector.tensor_tensor_scan(out[:, ::-1], FL[k][q, ::-1], PS[k][q, ::-1], CR[q, 0:1], ALU.mult, ALU.add).then_inc(sem(name + " spread"), 1)
                            dve.wait_ge(sem(name + " spread"), 4 * i + 2 * n + 1)
                            nc.vector.tensor_copy(CR[o, 0:1], out[:, 0:1]).then_inc(sem(name + " spread"), 1)
                            dve.wait_ge(sem(name + " spread"), 4 * i + 2 * n + 2)
                            if n == 0 and more:
                                ln_var(dve, nk, name, i + 1)
                        if more:
                            normed(i + 1, nk, (down - 1) * 8)
                    rounds(dve, body)
        ZT = XG[0]
        spread("s2", make_z=True)

        stage_over()

        HS = sb("HS", [P, 512])
        XA, XB = big[0][:, 0:512], big[0][:, 512:1024]
        EE = [big[1][:, 0:512], big[6][:, 512:1024]]
        QU, WW = big[1][:, 512:1024], big[2][:, 0:512]
        LQ = big[2][:, 512:1024]
        LG = big[3][:, 0:512]
        LIM = [big[3][:, 512 + 256 * k:768 + 256 * k].bitcast(BF16) for k in range(2)]
        DIF = big[4]
        AW = big[5]
        VV = big[6][:, 0:512]
        MX = sb("MX", [P, 513])
        RDEN = sb("RDEN", [P, 8])
        SS = big[7][:].rearrange("p (n c) -> p n c", n=2)
        MSG = XG
        with nc.Block() as block:
            @block.gpsimd
            def _(pool):
                for i in range(3):
                    gather(pool, i, i % 2, "l2", ta)

                def body(i, r, k):
                    if exists(i + 3):
                        gather(pool, i + 3, 1 - k, "l2", ta)
                rounds(pool, body)

            @block.sync
            def _(sp):
                load_flags(sp, LIM[0], lim_d, 0, "l2 limits landed 0")
                load_flags(sp, LIM[1], lim_d, 1, "l2 limits landed 1")

                def body(i, r, k):
                    if exists(i + 2):
                        sp.wait_ge(sem("l2 before"), i + 1)
                        load_flags(sp, LIM[k], lim_d, i + 2, f"l2 limits landed {k}")
                    sp.wait_ge(sem("l2 z"), i + 1)
                    sp.dma_start(edge_rows(tb, i), XD[:, bass.ds(i * 512, 512)]).then_inc(sem("l2 rows written"), 16)
                rounds(sp, body)
                sp.wait_ge(sem("l2 rows written"), 16 * NPAIR)

            @block.scalar
            def _(act):
                def source(i):
                    act.wait_ge(sem("l2 turned"), i + 1)
                    nc.scalar.activation(HS[:], PS[0][:], ACT.Copy).then_inc(sem("l2 hs"), 1)

                def mish_parts(i, k):
                    act.wait_ge(sem("l2 products"), i + 1)
                    nc.scalar.activation(XA, PS[1][:], ACT.Identity, bias=col(C_ATT)).then_inc(sem("l2 pre"), 1)
                    nc.scalar.activation(EE[k], PS[2][:], ACT.Identity, bias=col(C_WEB)).then_inc(sem("l2 edges"), 1)
                    act.wait_ge(sem("l2 cut"), i + 1)
                    nc.scalar.activation(XB, XB, ACT.Exp).then_inc(sem("l2 u"), 1)
                    act.wait_ge(sem("l2 q"), i + 1)
                    nc.scalar.activation(LQ, QU, ACT.Ln, bias=col(C_TWO)).then_inc(sem("l2 log q"), 1)
                    act.wait_ge(sem("l2 log q"), i + 1)
                    nc.scalar.activation(LQ, LQ, ACT.Exp, scale=-1.0).then_inc(sem("l2 inverse"), 1)

                def logits(i):
                    act.wait_ge(sem("l2 logits"), i + 1)
                    nc.scalar.activation(LG, PS[3][:], ACT.Identity, bias=col(C_WAB)).then_inc(sem("l2 lg"), 1)
                load_log_exp(act)
                gather_stage(act, 0, 0, "l2")
                gather_stage(act, 1, 1, "l2")
                ln_square(act, 0, "l2", 0)
                gather_stage(act, 2, 0, "l2")
                ln_rstd(act, 0, "l2", 0)
                ln_square(act, 1, "l2", 1)
                ln_rstd(act, 1, "l2", 1)
                source(0)
                mish_parts(0, 0)
                logits(0)

                def body(i, r, k):
                    if exists(i + 3):
                        gather_stage(act, i + 3, 1 - k, "l2")
                    if exists(i + 1):
                        source(i + 1)
                    act.wait_ge(sem("l2 dif"), 2 * i + 2)
                    nc.scalar.activation(AW[:], DIF[:], ACT.Exp).then_inc(sem("l2 weights"), 1)
                    if exists(i + 1):
                        mish_parts(i + 1, 1 - k)
                    if exists(i + 2):
                        ln_square(act, k, "l2", i + 2)
                        ln_rstd(act, k, "l2", i + 2)
                    if exists(i + 1):
                        logits(i + 1)
                rounds(act, body)

            @block.tensor
            def _(pe):
                def products(i, k):
                    pe.wait_ge(sem("l2 h"), i + 1)
                    turn_rows(pe, k, i, "l2", PS[0])
                    hd = HH[:, bass.ds(i * 512, 512)]
                    nc.tensor.matmul(PS[1][:], bd["wr"][:], hd, start=True, stop=False)
                    pe.wait_ge(sem("l2 hs"), i + 1)
                    nc.tensor.matmul(PS[1][:], bd["wews"][:], HS[:], start=False, stop=True)
                    nc.tensor.matmul(PS[2][:], bd["we"][:], HS[:], start=True, stop=True).then_inc(sem("l2 products"), 1)

                def logits(i):
                    pe.wait_ge(sem("l2 mish"), i + 1)
                    nc.tensor.matmul(PS[3][:], bd["wa"][:], XB, start=True, stop=True).then_inc(sem("l2 logits"), 1)
                products(0, 0)
                logits(0)

                def body(i, r, k):
                    if exists(i + 1):
                        products(i + 1, 1 - k)
                    pe.wait_ge(sem("l2 summed"), 4 * i + 4)
                    for j in range(4):
                        nc.tensor.transpose(PS[4][:, j * P:(j + 1) * P], SS[:, 0, j * P:(j + 1) * P], ident[:])
                    for j in range(4):
                        ins = nc.tensor.matmul(PS[5][:, 2 * j:2 * j + 2], SS[:, 1, j * P:(j + 1) * P], sel[:], start=True, stop=True)
                    ins.then_inc(sem("l2 back"), 1)
                    if exists(i + 1):
                        logits(i + 1)
                rounds(pe, body)

            @block.vector
            def _(dve):
                def centre(i, n, k):
                    dve.wait_ge(sem(f"l2 landed {k}"), 128 * n + 128)
                    ln_sum(dve, G[k][:], k, "l2", i, bias=True)

                def cut(i):
                    dve.wait_ge(sem("l2 pre"), i + 1)
                    nc.vector.tensor_scalar(XB, XA, 20.0, None, ALU.min).then_inc(sem("l2 cut"), 1)

                def q(i):
                    dve.wait_ge(sem("l2 u"), i + 1)
                    nc.vector.scalar_tensor_tensor(out=QU, in0=XB, scalar=2.0, in1=XB, op0=ALU.add, op1=ALU.mult).then_inc(sem("l2 q"), 1)
                    dve.wait_ge(sem("l2 q"), i + 1)
                    nc.vector.tensor_tensor(WW, QU, XA, ALU.mult).then_inc(sem("l2 qx"), 1)

                def mish(i):
                    dve.wait_ge(sem("l2 inverse"), i + 1)
                    dve.wait_ge(sem("l2 qx"), i + 1)
                    nc.vector.tensor_tensor(XB, WW, LQ, ALU.mult).then_inc(sem("l2 mish"), 1)
                nc.vector.memset(CR[:], 0.0).then_inc(sem("l2 clear"), 1)
                nc.vector.memset(MX[:, 512:513], -LIMIT).then_inc(sem("l2 clear"), 1)
                for k in range(2):
                    centre(k, 0, k)
                    ln_var(dve, k, "l2", k)
                    ln_out(dve, k, "l2", k)
                cut(0)
                q(0)
                mish(0)
                dve.wait_ge(sem("l2 clear"), 2)

                def body(i, r, k):
                    dve.wait_ge(sem("l2 lg"), i + 1)
                    dve.wait_ge(sem(f"l2 limits landed {k}"), 32 * r + 32)
                    mx = sem("l2 max")
                    for h in range(2):
                        here = slice(h * D, (h + 1) * D)
                        there = slice((1 - h) * D, (2 - h) * D)
                        nc.vector.tensor_copy(MX[here, 0:1], MX[there, 512:513]).then_inc(mx, 1)
                        dve.wait_ge(mx, 4 * i + 2 * h + 1)
                        nc.vector.tensor_tensor_scan(MX[here, 1:513], LIM[k][here, :], LG[here, :], MX[here, 0:1], ALU.min, ALU.max).then_inc(mx, 1)
                        dve.wait_ge(mx, 4 * i + 2 * h + 2)
                    nc.vector.tensor_tensor(VV, MX[:, 0:512], LIM[k], ALU.min).then_inc(sem("l2 before"), 1)
                    nc.vector.tensor_tensor(DIF[:, 512:1024], LG, MX[:, 1:513], ALU.subtract).then_inc(sem("l2 dif"), 1)
                    dve.wait_ge(sem("l2 before"), i + 1)
                    nc.vector.tensor_tensor(DIF[:, 0:512], VV, MX[:, 1:513], ALU.subtract).then_inc(sem("l2 dif"), 1)
                    if exists(i + 2):
                        centre(i + 2, r + 1, k)
                    if exists(i + 1):
                        cut(i + 1)
                    dve.wait_ge(sem("l2 weights"), i + 1)
                    nc.vector.tensor_tensor(VV, AW[:, 512:1024], EE[k], ALU.mult).then_inc(sem("l2 weighted"), 1)
                    dve.wait_ge(sem("l2 weighted"), i + 1)
                    for h in range(2):
                        here = slice(h * D, (h + 1) * D)
                        there = slice((1 - h) * D, (2 - h) * D)
                        for n, v in enumerate((VV, AW[:, 512:1024])):
                            nc.vector.tensor_tensor_scan(SS[here, n, :], AW[here, 0:512], v[here, :], CR[here, n:n + 1], ALU.mult, ALU.add).then_inc(sem("l2 summed"), 1)
                        dve.wait_ge(sem("l2 summed"), 4 * i + 2 * h + 2)
                        nc.vector.tensor_copy(CR[there, :], SS[here, :, 511]).then_inc(sem("l2 carried"), 1)
                        if h == 0:
                            if exists(i + 1):
                                q(i + 1)
                        dve.wait_ge(sem("l2 carried"), 2 * i + h + 1)
                    if exists(i + 2):
                        ln_var(dve, k, "l2", i + 2)
                    if exists(i + 1):
                        mish(i + 1)
                    dve.wait_ge(sem("l2 back"), i + 1)
                    nc.vector.reciprocal(RDEN[:], PS[5][:, 0:8]).then_inc(sem("l2 rden"), 1)
                    if exists(i + 2):
                        ln_out(dve, k, "l2", i + 2)
                    dve.wait_ge(sem("l2 rden"), i + 1)
                    nc.vector.tensor_tensor(MSG[k][:], rows(PS[4][:]), bc8(RDEN[:]), ALU.mult).then_inc(sem("l2 msg"), 1)
                    dve.wait_ge(sem("l2 msg"), i + 1)
                    xd = rows(XD[:, bass.ds(i * 512, 512)])
                    nc.vector.tensor_tensor(xd, xd, MSG[k][:], ALU.add).then_inc(sem("l2 z"), 1)
                rounds(dve, body)

        spread("s3")

        ZR, RH, NT = big[7], S, MX[:, 0:512]
        FF = TY[0][:, 1, :].bitcast(F32)

        DP = 125
        DW = 4 * DP
        CYCLE = 4
        DROUNDS = (UNITS - 6) // CYCLE
        assert UNITS == CYCLE * DROUNDS + 6
        OD = [XG[k][0:DP] for k in range(2)]
        W0F = W0S[:].rearrange("p a b d -> p (a b d)")
        YD = [Y[0][:], Y[1][:], rows(W0F[:, 0:512]), rows(W0F[:, 512:1024])]
        x_u = x.rearrange("(u p c) d -> p u (c d)", p=DP, c=8)
        out_u = out.rearrange("(u p c) d -> p u (c d)", p=DP, c=8)
        HTD = [big[0][:, k * 512:k * 512 + DW] for k in range(2)]
        ZD = [big[7][:, k * 512:k * 512 + DW] for k in range(2)]
        RD = [big[6][:, k * 512:k * 512 + DW] for k in range(2)]
        ND, RHD, FD0 = NT[:, 0:DW], RH[:, 0:DW], FF[:, 0:DW]
        NEWTON = [big[5][:, k * 64:(k + 1) * 64].rearrange("p (n c) -> p n c", c=8) for k in range(2)]
        GUESS = float(0x5f3759df)
        with nc.Block() as block:
            def units(eng, body):
                with eng.Fori(0, DROUNDS) as r:
                    for j in range(CYCLE):
                        body(CYCLE * r + j, 2 * r + j // 2, j)
                for i in range(CYCLE * DROUNDS, UNITS):
                    body(i, i // 2, i % CYCLE)

            def unit_exists(i):
                return not isinstance(i, int) or i < UNITS

            @block.sync
            def _(sp):
                def load(i, k):
                    sp.dma_start(G[k][0:DP].rearrange("p c d -> p (c d)"), x_u[:, bass.ds(i, 1), :].rearrange("p a c -> p (a c)")).then_inc(sem(f"d landed {k}"), 16)
                load(0, 0)
                load(1, 1)
                for k in range(2):
                    sp.wait_ge(sem("d y"), k + 1)
                    load(2 + k, k)

                def body(i, n, j):
                    k = j % 2
                    if unit_exists(i + 4):
                        sp.wait_ge(sem("d y"), i + 3)
                        load(i + 4, k)
                    sp.wait_ge(sem("d o"), i + 1)
                    sp.dma_start(out_u[:, bass.ds(i, 1), :].rearrange("p a c -> p (a c)"), OD[k].rearrange("p c d -> p (c d)")).then_inc(sem(f"d written {k}"), 16)
                units(sp, body)
                for k in range(2):
                    sp.wait_ge(sem(f"d written {k}"), 16 * (UNITS // 2 + 1))

            @block.gpsimd
            def _(pool):
                for k in range(2):
                    pool.sem_inc(sem(f"d written {k}"), 16)

                def biased(i, n, j):
                    pool.wait_ge(sem(f"d landed {j % 2}"), 16 * n + 16)
                    pool.sem_inc(sem("d pool turn"), 1)
                    nc.gpsimd.tensor_tensor(YD[j], G[j % 2][:], bcd(CB[:]), ALU.add).then_inc(sem("d y"), 1)
                def newton(i, j):
                    k = j % 2
                    v, y, a, b = (NEWTON[k][:, m, :] for m in range(4))
                    step = sem("d newton")
                    pool.wait_ge(sem("d var"), i + 1)
                    pool.sem_inc(sem("d pool turn"), 1)
                    nc.gpsimd.tensor_scalar(v, SM[k][:, 1, :], 1.0 / D, EPS, ALU.mult, ALU.add).then_inc(step, 1)
                    count = i * 14 + 1
                    pool.wait_ge(step, count)
                    pool.sem_inc(sem("d pool turn"), 1)
                    nc.gpsimd.tensor_scalar(y.bitcast(I32), v.bitcast(I32), -0.5, GUESS, ALU.mult, ALU.add).then_inc(step, 1)
                    pool.wait_ge(step, count + 1)
                    for m in range(3):
                        nc.gpsimd.tensor_tensor(a, y, y, ALU.mult).then_inc(step, 1)
                        pool.wait_ge(step, count + 4 * m + 2)
                        nc.gpsimd.tensor_tensor(b, a, v, ALU.mult).then_inc(step, 1)
                        pool.wait_ge(step, count + 4 * m + 3)
                        pool.sem_inc(sem("d pool turn"), 1)
                        nc.gpsimd.tensor_scalar(a, b, -0.5, 1.5, ALU.mult, ALU.add).then_inc(step, 1)
                        pool.wait_ge(step, count + 4 * m + 4)
                        nc.gpsimd.tensor_tensor(SM[k][:, 3, :] if m == 2 else y, a, y, ALU.mult).then_inc(sem("d rstd") if m == 2 else step, 1)
                        if m < 2:
                            pool.wait_ge(step, count + 4 * m + 5)
                    pool.sem_inc(step, 1)
                for i in range(3):
                    biased(i, i // 2, i)
                newton(0, 0)
                newton(1, 1)

                def body(i, n, j):
                    if unit_exists(i + 3):
                        pool.wait_ge(sem("d o turn"), i + 1)
                        biased(i + 3, n + (j % 2) + 1, (j + 3) % CYCLE)
                    if unit_exists(i + 2):
                        newton(i + 2, j)
                pool.sem_inc(sem("d o turn"), 1)
                units(pool, body)

            @block.scalar
            def _(act):
                def gates(i, k):
                    act.wait_ge(sem("d gates"), 2 * i + 1)
                    nc.scalar.activation(RD[k], PS[5][:, 0:DW], ACT.Sigmoid, bias=col(C_DR)).then_inc(sem("d r"), 1)
                    act.wait_ge(sem("d gates"), 2 * i + 2)
                    nc.scalar.activation(ZD[k], PS[4][:, 0:DW], ACT.Sigmoid, bias=col(C_DZ)).then_inc(sem("d z"), 1)

                def ht(i, k):
                    act.wait_ge(sem("d turned"), i + 1)
                    nc.scalar.activation(HTD[k], PS[1][:, 0:DW], ACT.Copy).then_inc(sem("d ht"), 1)
                ln_square(act, 0, "d", 0)
                ln_square(act, 1, "d", 1)
                ht(0, 0)
                gates(0, 0)

                def body(i, n, j):
                    k = j % 2
                    act.wait_ge(sem("d n sum"), i + 1)
                    nc.scalar.activation(ND, PS[7][:, 0:DW], ACT.Tanh, bias=col(C_DIN)).then_inc(sem("d n"), 1)
                    if unit_exists(i + 1):
                        ht(i + 1, 1 - k)
                    if unit_exists(i + 2):
                        ln_square(act, k, "d", i + 2)
                    if unit_exists(i + 1):
                        gates(i + 1, 1 - k)
                units(act, body)

            @block.tensor
            def _(pe):
                def start(i, k):
                    pe.wait_ge(sem("d h"), i + 1)
                    for j in range(4):
                        ins = nc.tensor.transpose(PS[1][:, j * DP:(j + 1) * DP], hrow(k, j)[0:DP, :], ident[0:DP, 0:DP])
                    ins.then_inc(sem("d turned"), 1)
                    pe.wait_ge(sem("d ht"), i + 1)
                    nc.tensor.matmul(PS[5][:, 0:DW], bd["dr"][:], HTD[k], start=True, stop=True).then_inc(sem("d gates"), 1)
                    nc.tensor.matmul(PS[6][:, 0:DW], bd["hn"][:], HTD[k], start=True, stop=True).then_inc(sem("d hn"), 1)
                    nc.tensor.matmul(PS[4][:, 0:DW], bd["dz"][:], HTD[k], start=True, stop=True).then_inc(sem("d gates"), 1)
                    if not (isinstance(i, int) and i == 0):
                        pe.wait_ge(sem("d n"), i)
                    nc.tensor.matmul(PS[7][:, 0:DW], bd["din"][:], HTD[k], start=True, stop=False)
                def finish(i):
                    pe.wait_ge(sem("d rh"), i + 1)
                    nc.tensor.matmul(PS[7][:, 0:DW], ident[:], RHD, start=False, stop=True).then_inc(sem("d n sum"), 1)
                start(0, 0)
                finish(0)

                def body(i, n, j):
                    more = unit_exists(i + 1)
                    if more:
                        start(i + 1, 1 - j % 2)
                    pe.wait_ge(sem("d z(h - n)"), i + 1)
                    for j in range(4):
                        for t in (ND, FD0):
                            ins = nc.tensor.matmul(PS[0][0:DP, j * P:(j + 1) * P], t[:, j * DP:(j + 1) * DP], ident[:],
                                                   start=(t is ND), stop=(t is FD0))
                    ins.then_inc(sem("d back"), 1)
                    if more:
                        finish(i + 1)
                units(pe, body)

            @block.vector
            def _(dve):
                def centre(i, n, j):
                    k = j % 2
                    dve.wait_ge(sem("d y"), i + 1)
                    nc.vector.tensor_reduce(SM[k][:, 0, :], YD[j], AX.X, ALU.add).then_inc(sem("d sum"), 1)
                    dve.wait_ge(sem("d sum"), i + 1)
                    nc.vector.scalar_tensor_tensor(out=XC[k][:], in0=bc8(SM[k][:, 0, :]), scalar=-1.0 / D, in1=YD[j],
                                                   op0=ALU.mult, op1=ALU.add).then_inc(sem("d centred"), 1)
                for i in range(2):
                    centre(i, 0, i)
                for i in range(2):
                    ln_var(dve, i, "d", i)
                for i in range(2):
                    ln_out(dve, i, "d", i)

                def reset(i, k):
                    dve.wait_ge(sem("d hn"), i + 1)
                    dve.wait_ge(sem("d r"), i + 1)
                    nc.vector.scalar_tensor_tensor(out=RHD, in0=PS[6][:, 0:DW], scalar=col(C_HN), in1=RD[k],
                                                   op0=ALU.add, op1=ALU.mult).then_inc(sem("d rh"), 1)
                reset(0, 0)

                def body(i, n, j):
                    k = j % 2
                    if unit_exists(i + 2):
                        centre(i + 2, n + 1, (j + 2) % CYCLE)
                    dve.wait_ge(sem("d n"), i + 1)
                    nc.vector.tensor_tensor(FD0, HTD[k], ND, ALU.subtract).then_inc(sem("d h - n"), 1)
                    if unit_exists(i + 2):
                        ln_var(dve, k, "d", i + 2)
                    dve.wait_ge(sem("d z"), i + 1)
                    dve.wait_ge(sem("d h - n"), i + 1)
                    nc.vector.tensor_tensor(FD0, FD0, ZD[k], ALU.mult).then_inc(sem("d z(h - n)"), 1)
                    if unit_exists(i + 1):
                        reset(i + 1, 1 - k)
                    dve.wait_ge(sem("d back"), i + 1)
                    dve.wait_ge(sem(f"d written {k}"), 16 * n + 16)
                    nc.vector.tensor_tensor(OD[k], rows(PS[0][:])[0:DP], YD[j][0:DP], ALU.add).then_inc(sem("d o"), 1)
                    if unit_exists(i + 2):
                        ln_out(dve, k, "d", i + 2)
                    dve.wait_ge(sem("d o"), i + 1)
                    dve.sem_inc(sem("d o turn"), 1)
                units(dve, body)

        stage_over()

        TT, V1, V2, S1, S2, MM = (big[n] for n in (0, 1, 2, 4, 5, 6))
        OT = big[3][:, 0:512]
        LIMD = big[3][:, 512:1024].bitcast(BF16)
        ZZ = BEFORE
        FD = TY[0][:, 0, :]
        EW = W0S[:].rearrange("p a b d -> p (a b d)")
        RC = TY[1][:].rearrange("p a b -> p (a b)").bitcast(F32)
        SC = sb("SC", [P, 1024])
        AT = [H[k][0:4].rearrange("p a b d -> p (a b d)")[:, 512:1024] for k in range(2)]
        SCT = sb("SCT", [P, 2, 8], I32)
        VAR = S1[D:P, :]
        ENDS = [HS, sb("ENDS1", [P, 512])]
        ROW = [XG[k] for k in range(2)]
        both = [slice(h * 512, (h + 1) * 512) for h in range(2)]
        with nc.Block() as block:
            @block.gpsimd
            def _(pool):
                pool.sem_inc(sem("l3 rows free"), 2)
                for i in range(3):
                    gather(pool, i, i % 2, "l3", tb)

                def body(i, r, k):
                    if exists(i + 3):
                        gather(pool, i + 3, 1 - k, "l3", tb)
                    nc.gpsimd.tensor_copy(SCT[:, k, :], LI[:, bass.ds(i, 1), 2, :].rearrange("p a c -> p (a c)")).then_inc(sem("l3 dst staged"), 1)
                    pool.wait_ge(sem("l3 dst staged"), i + 1)
                    pool.wait_ge(sem("l3 rows"), i + 1)
                    pool.sem_inc(sem("l3 out turn"), 1)
                    for c in range(8):
                        nc.gpsimd.indirect_dma_start(out, bass.IndirectOffsetOnAxis(ap=SCT[:, k, c:c + 1], axis=0), ROW[k][:, c, :], None,
                                                     bounds_check=N - 1, oob_is_err=False).then_inc(sem(f"l3 written {k}"), 16)
                    pool.wait_ge(sem(f"l3 written {k}"), 128 * r + 128)
                    pool.sem_inc(sem("l3 rows free"), 1)
                rounds(pool, body)

            @block.sync
            def _(sp):
                def spread_line(t, d, i, name):
                    sp.dma_start(t, d[bass.ds(i * PAIR, PAIR)].rearrange("(o c) -> o c", o=1).broadcast_to([t.shape[0], PAIR])).then_inc(sem(name), 16)

                def load_weight(i):
                    spread_line(EW, ew_d, i, "l3 ew landed")

                def load_attr(i):
                    for h in range(2):
                        sp.dma_start(AT[h], comp_d[:, bass.ds(i * PAIR + h * HALF, HALF)]).then_inc(sem("l3 attr landed"), 16)

                def load_b(i):
                    spread_line(RC, rcnt_d, i, "l3 rcnt landed")
                    spread_line(FD, same_prev_d, i, "l3 flags landed")
                    spread_line(LIMD, lim_d, i, "l3 limits landed")

                def load_c(i):
                    spread_line(SC[0:D, :], amp_d, i, "l3 scalers landed")
                    spread_line(SC[D:P, :], att_amp_d, i, "l3 scalers landed")
                load_attr(0)
                load_weight(0)
                load_b(0)
                load_c(0)
                sp.wait_ge(sem("l3 raw"), 2)
                load_attr(1)
                sp.wait_ge(sem("l3 t"), 2)
                load_weight(1)
                sp.wait_ge(sem("l3 carried"), 4)
                load_b(1)

                def body(i, r, k):
                    if exists(i + 2):
                        sp.wait_ge(sem("l3 raw"), 2 * i + 4)
                        load_attr(i + 2)
                    if exists(i + 1):
                        sp.wait_ge(sem("l3 scaled"), 2 * i + 2)
                        load_c(i + 1)
                    if exists(i + 2):
                        sp.wait_ge(sem("l3 t"), 2 * i + 4)
                        load_weight(i + 2)
                        sp.wait_ge(sem("l3 carried"), 2 * i + 6)
                        load_b(i + 2)
                rounds(sp, body)

            @block.scalar
            def _(act):
                def source(i):
                    act.wait_ge(sem("l3 turned"), i + 1)
                    for h in range(2):
                        nc.scalar.activation(ENDS[h][0:D, :], PS[0][h * D:(h + 1) * D, :], ACT.Copy).then_inc(sem("l3 hs"), 1)

                def operands(i):
                    act.wait_ge(sem("l3 t"), 2 * i + 2)
                    nc.scalar.activation(V1[0:D, :], TT[0:D, :], ACT.Identity, bias=col(C_PRE, 0, D)).then_inc(sem("l3 v1"), 1)
                    nc.scalar.activation(V1[D:P, :], TT[D:P, :], ACT.Square, bias=col(C_PRE, D, P)).then_inc(sem("l3 v1"), 1)
                    nc.scalar.activation(V2[:], TT[:], ACT.Identity, scale=col(C_SGN), bias=col(C_SPRE)).then_inc(sem("l3 v2"), 1)

                def mean_squared(i):
                    act.wait_ge(sem("l3 mean"), i + 1)
                    nc.scalar.activation(VAR, MM[0:D, :], ACT.Square).then_inc(sem("l3 mean squared"), 1)

                def std(i):
                    act.wait_ge(sem("l3 variance"), i + 1)
                    nc.scalar.activation(VAR, VAR, ACT.Ln).then_inc(sem("l3 var log"), 1)
                    act.wait_ge(sem("l3 var log"), i + 1)
                    nc.scalar.activation(MM[D:P, :], VAR, ACT.Exp, scale=0.5).then_inc(sem("l3 std"), 1)
                load_log_exp(act)
                gather_stage(act, 0, 0, "l3")
                gather_stage(act, 1, 1, "l3")
                ln_square(act, 0, "l3", 0)
                gather_stage(act, 2, 0, "l3")
                ln_rstd(act, 0, "l3", 0)
                ln_square(act, 1, "l3", 1)
                ln_rstd(act, 1, "l3", 1)
                source(0)
                operands(0)
                mean_squared(0)
                std(0)
                source(1)

                def body(i, r, k):
                    if exists(i + 3):
                        gather_stage(act, i + 3, 1 - k, "l3")
                    if exists(i + 1):
                        operands(i + 1)
                    if exists(i + 2):
                        ln_square(act, k, "l3", i + 2)
                    act.wait_ge(sem("l3 total"), i + 1)
                    nc.scalar.activation(OT, PS[3][:], ACT.Identity, bias=col(C_POST)).then_inc(sem("l3 out"), 1)
                    act.wait_ge(sem("l3 gate r"), i + 1)
                    nc.scalar.activation(ZR[:, 512:1024], PS[5][:], ACT.Sigmoid, bias=col(C_R)).then_inc(sem("l3 sr"), 1)
                    if exists(i + 1):
                        mean_squared(i + 1)
                    act.wait_ge(sem("l3 gate z"), i + 1)
                    nc.scalar.activation(ZR[:, 0:512], PS[4][:], ACT.Sigmoid, bias=col(C_Z)).then_inc(sem("l3 sz"), 1)
                    act.wait_ge(sem("l3 n sum"), i + 1)
                    nc.scalar.activation(NT, RH[:], ACT.Tanh, bias=col(C_IN)).then_inc(sem("l3 n"), 1)
                    if exists(i + 1):
                        load_log_exp(act)
                    if exists(i + 2):
                        ln_rstd(act, k, "l3", i + 2)
                    if exists(i + 1):
                        std(i + 1)
                    if exists(i + 2):
                        source(i + 2)
                rounds(act, body)

            @block.tensor
            def _(pe):
                def dst(i):
                    return HH[:, bass.ds(i * 512, 512)]

                def raw_attr(i):
                    pe.wait_ge(sem("l3 attr landed"), 32 * i + 32)
                    for h in range(2):
                        nc.tensor.matmul(PS[1 + h][:], attw[:], AT[h], start=True, stop=False)

                def raw_ends(i):
                    for h in range(2):
                        pe.wait_ge(sem("l3 hs"), 2 * i + h + 1)
                        pe.wait_ge(sem("l3 hd"), 2 * i + h + 1)
                        nc.tensor.matmul(PS[1 + h][:], bd["ends"][:], ENDS[h][:], start=False, stop=True).then_inc(sem("l3 raw"), 1)
                def turn(i, k):
                    pe.wait_ge(sem("l3 h"), i + 1)
                    turn_rows(pe, k, i, "l3", PS[0])
                def own_parts(i):
                    nc.tensor.matmul(PS[3][:], bd["u0"][:], dst(i), start=True, stop=False)
                    if not (isinstance(i, int) and i == 0):
                        pe.wait_ge(sem("l3 sr"), i)
                    nc.tensor.matmul(PS[5][:], bd["hr"][:], dst(i), start=True, stop=False)
                raw_attr(0)
                turn(0, 0)
                raw_ends(0)
                pe.wait_ge(sem("l3 t"), 2)
                raw_attr(1)
                turn(1, 1)
                own_parts(0)

                def body(i, r, k):
                    pe.wait_ge(sem("l3 std"), i + 1)
                    for h, c in enumerate(both):
                        nc.tensor.matmul(PS[6 + h][:], bd["mq"][:], MM[:, c], start=True, stop=False)
                        nc.tensor.matmul(PS[6 + h][:], bd["xq"][:], S2[:, c], start=False, stop=True).then_inc(sem("l3 q"), 1)
                    if exists(i + 1):
                        raw_ends(i + 1)
                    for h, c in enumerate(both):
                        nc.tensor.matmul(PS[3][:], bd[("mmA", "mmB")[h]][:], MM[:, c], start=False, stop=False)
                        ins = nc.tensor.matmul(PS[3][:], bd[("xxA", "xxB")[h]][:], S2[:, c], start=False, stop=False)
                    ins.then_inc(sem("l3 aggregates used"), 1)
                    for h, c in enumerate(both):
                        pe.wait_ge(sem("l3 scaled"), 2 * i + h + 1)
                        ins = nc.tensor.matmul(PS[3][:], bd[("sumA", "sumB")[h]][:], ZZ[:, c], start=False, stop=(h == 1))
                    ins.then_inc(sem("l3 total"), 1)
                    nc.tensor.matmul(PS[6][:], bd["hn"][:], dst(i), start=True, stop=True)
                    pe.wait_ge(sem("l3 out"), i + 1)
                    nc.tensor.matmul(PS[5][:], bd["r"][:], OT, start=False, stop=True).then_inc(sem("l3 gate r"), 1)
                    nc.tensor.matmul(PS[4][:], bd["hz"][:], dst(i), start=True, stop=False)
                    nc.tensor.matmul(PS[4][:], bd["z"][:], OT, start=False, stop=True).then_inc(sem("l3 gate z"), 1)
                    nc.tensor.matmul(PS[7][:], bd["in"][:], OT, start=True, stop=True).then_inc(sem("l3 in"), 1)
                    if exists(i + 2):
                        pe.wait_ge(sem("l3 t"), 2 * i + 4)
                        raw_attr(i + 2)
                    if exists(i + 1):
                        own_parts(i + 1)
                    if exists(i + 2):
                        turn(i + 2, k)
                    pe.wait_ge(sem("l3 f"), i + 1)
                    for j in range(4):
                        ins = nc.tensor.transpose(PS[4][:, j * P:(j + 1) * P], FF[:, j * P:(j + 1) * P], ident[:])
                    ins.then_inc(sem("l3 back"), 1)
                rounds(pe, body)

            @block.vector
            def _(dve):
                def centre(i, n, k):
                    dve.wait_ge(sem(f"l3 landed {k}"), 128 * n + 128)
                    ln_sum(dve, G[k][:], k, "l3", i, bias=True)

                def weighted(i):
                    dve.wait_ge(sem("l3 ew landed"), 16 * i + 16)
                    for h, c in enumerate(both):
                        dve.wait_ge(sem("l3 raw"), 2 * i + h + 1)
                        nc.vector.tensor_tensor(TT[:, c], PS[1 + h][:], EW[:, c], ALU.mult).then_inc(sem("l3 t"), 1)

                def own(i):
                    for h in range(2):
                        nc.vector.tensor_copy(ENDS[h][D:P, :], HH[h * D:(h + 1) * D, bass.ds(i * 512, 512)]).then_inc(sem("l3 hd"), 1)

                def scans(i):
                    if not (isinstance(i, int) and i == 0):
                        dve.wait_ge(sem("l3 aggregates used"), i)
                    dve.wait_ge(sem("l3 v1"), 2 * i + 2)
                    dve.wait_ge(sem("l3 flags landed"), 16 * i + 16)
                    dve.wait_ge(sem("l3 carried"), 2 * i + 2)
                    nc.vector.tensor_tensor_scan(S1[:], FD, V1[:], CR[:, 0:1], ALU.mult, ALU.add).then_inc(sem("l3 sums"), 1)
                    dve.wait_ge(sem("l3 v2"), i + 1)
                    dve.wait_ge(sem("l3 limits landed"), 16 * i + 16)
                    nc.vector.tensor_tensor_scan(S2[:], LIMD, V2[:], CR[:, 1:2], ALU.min, ALU.max).then_inc(sem("l3 maxima"), 1)
                    dve.wait_ge(sem("l3 rcnt landed"), 16 * i + 16)
                    dve.wait_ge(sem("l3 sums"), i + 1)
                    nc.vector.tensor_copy(CR[:, 0:1], S1[:, 1023:1024]).then_inc(sem("l3 carried"), 1)
                    nc.vector.tensor_tensor(MM[:], S1[:], RC, ALU.mult).then_inc(sem("l3 mean"), 1)
                    dve.wait_ge(sem("l3 maxima"), i + 1)
                    nc.vector.tensor_copy(CR[:, 1:2], S2[:, 1023:1024]).then_inc(sem("l3 carried"), 1)

                def variance(i):
                    dve.wait_ge(sem("l3 mean squared"), i + 1)
                    nc.vector.tensor_tensor(VAR, MM[D:P, :], VAR, ALU.subtract).then_inc(sem("l3 raw variance"), 1)
                    dve.wait_ge(sem("l3 raw variance"), i + 1)
                    nc.vector.tensor_scalar(VAR, VAR, 0.0, EPS, ALU.max, ALU.add).then_inc(sem("l3 variance"), 1)
                nc.vector.memset(CR[:, 0:1], 0.0).then_inc(sem("l3 carried"), 1)
                nc.vector.memset(CR[:, 1:2], -LIMIT).then_inc(sem("l3 carried"), 1)
                for k in range(2):
                    centre(k, 0, k)
                    ln_var(dve, k, "l3", k)
                    ln_out(dve, k, "l3", k)
                own(0)
                weighted(0)
                own(1)
                scans(0)
                variance(0)

                def body(i, r, k):
                    dve.wait_ge(sem("l3 scalers landed"), 32 * i + 32)
                    for h, c in enumerate(both):
                        dve.wait_ge(sem("l3 q"), 2 * i + h + 1)
                        nc.vector.tensor_tensor(ZZ[:, c], PS[6 + h][:], SC[:, c], ALU.mult).then_inc(sem("l3 scaled"), 1)
                    if exists(i + 1):
                        weighted(i + 1)
                    if exists(i + 2):
                        own(i + 2)
                        centre(i + 2, r + 1, k)
                    if exists(i + 1):
                        scans(i + 1)
                    if exists(i + 2):
                        ln_var(dve, k, "l3", i + 2)
                    dve.wait_ge(sem("l3 sr"), i + 1)
                    nc.vector.scalar_tensor_tensor(out=RH[:], in0=PS[6][:], scalar=col(C_HN), in1=ZR[:, 512:1024],
                                                   op0=ALU.add, op1=ALU.mult).then_inc(sem("l3 rh"), 1)
                    dve.wait_ge(sem("l3 rh"), i + 1)
                    dve.wait_ge(sem("l3 in"), i + 1)
                    nc.vector.tensor_tensor(RH[:], RH[:], PS[7][:], ALU.add).then_inc(sem("l3 n sum"), 1)
                    if exists(i + 1):
                        variance(i + 1)
                    dve.wait_ge(sem("l3 n"), i + 1)
                    nc.vector.tensor_tensor(FF, HH[:, bass.ds(i * 512, 512)], NT, ALU.subtract).then_inc(sem("l3 h - n"), 1)
                    if exists(i + 2):
                        ln_out(dve, k, "l3", i + 2)
                    dve.wait_ge(sem("l3 sz"), i + 1)
                    dve.wait_ge(sem("l3 h - n"), i + 1)
                    nc.vector.tensor_tensor(FF, FF, ZR[:, 0:512], ALU.mult).then_inc(sem("l3 z(h - n)"), 1)
                    dve.wait_ge(sem("l3 z(h - n)"), i + 1)
                    nc.vector.scalar_tensor_tensor(out=FF, in0=FF, scalar=col(C_C), in1=NT, op0=ALU.add, op1=ALU.add).then_inc(sem("l3 f"), 1)
                    dve.wait_ge(sem("l3 back"), i + 1)
                    dve.wait_ge(sem("l3 rows free"), i + 1)
                    nc.vector.tensor_tensor(ROW[k][:], rows(PS[4][:]), rows(XD[:, bass.ds(i * 512, 512)]), ALU.add).then_inc(sem("l3 rows"), 1)
                rounds(dve, body)
        stage_over()


_INS = ['x', 'src', 'dst', 'edge_attr_4', 'edge_type_32', 'node_vec', 'L0_gnn_weight', 'L1_gnn_W', 'L1_gnn_gamma',
        'L1_gnn_beta', 'L2_gnn_We_k', 'L2_gnn_We_b', 'L2_gnn_Ws_k', 'L2_gnn_Ws_b', 'L2_gnn_Wr_k', 'L2_gnn_Wr_b',
        'L2_gnn_Wa_k', 'L2_gnn_Wa_b', 'L3_gnn_W', 'L3_gnn_We', 'L3_gnn_be', 'L3_gnn_Wpre', 'L3_gnn_bpre',
        'L3_gnn_Wpost', 'L3_gnn_bpost', 'L3_gnn_Wih', 'L3_gnn_bih', 'L3_gnn_Whh', 'L3_gnn_bhh']
_OUTS = [((50000, 64), 'float32')]


def kernel(**inputs):
    import numpy as _np
    import concourse.bacc as _bacc
    from concourse import mybir as _mybir
    from concourse.bass_utils import run_bass_kernel_spmd as _run

    nc = _bacc.Bacc("TRN2", target_bir_lowering=False, num_devices=1)
    arrays, args = {}, []
    for name in _INS:
        a = _np.ascontiguousarray(inputs[name])
        arrays[f"in_{name}_dram"] = a
        args.append(nc.dram_tensor(f"in_{name}_dram", a.shape, _mybir.dt.from_np(a.dtype), kind="ExternalInput").ap())
    for i, (shape, dtype) in enumerate(_OUTS):
        dt = _mybir.dt.from_np(_np.dtype(dtype))
        args.append(nc.dram_tensor(f"out_{i}_dram", shape, dt, kind="ExternalOutput").ap())
    gnn_kernel(nc, *args)
    r = _run(nc, [arrays], core_ids=[0])
    got = tuple(r.results[0][f"out_{i}_dram"] for i in range(len(_OUTS)))
    return got[0]
```
